# Optimizing a Trainium2 kernel written in Bass

```python
import numpy as np
import jax
import jax.numpy as jnp

def _softmax(x, axis=-1):
    return jax.nn.softmax(x, axis=axis)

def _gelu(x):
    return jax.nn.gelu(x, approximate=True)

def _silu(x):
    return jax.nn.silu(x)

def _sigmoid(x):
    return jax.nn.sigmoid(x)

def _layernorm(x, axis=-1, eps=1e-05):
    m = jnp.mean(x, axis=axis, keepdims=True)
    v = jnp.var(x, axis=axis, keepdims=True)
    return (x - m) / jnp.sqrt(v + eps)

def _scatter_add(tgt, idx, src, axis=0):
    return tgt.at[idx].add(src)

def _segment_sum(src, seg, n):
    return jax.ops.segment_sum(src, seg, n)
kernel_name = 'mk_gnn_resnorm_d2_gnn_r8_35bc4d'

def setup_inputs(seed: int=0):
    np.random.seed(seed)
    _w = jnp.asarray

    def _rec_inputs():
        import jax
        import jax.numpy as jnp
        _gk = jax.random.key(seed)
        x = -0.0003713 + 1 * jax.random.normal(jax.random.fold_in(_gk, 1), (6250, 128), jnp.float32)
        _s = jax.random.randint(jax.random.fold_in(_gk, 2), (50000,), 0, 6250, jnp.int32)
        _d = jax.random.randint(jax.random.fold_in(_gk, 3), (50000,), 0, 6250, jnp.int32)
        _loop = jnp.arange(6250, dtype=jnp.int32)
        src = jnp.concatenate([_s, _d, _loop])
        dst = jnp.concatenate([_d, _s, _loop])
        _o = jnp.argsort(dst, stable=True)
        src = src[_o]
        dst = dst[_o]
        edge_attr_128 = -8.16379e-05 + 0.999858 * jax.random.normal(jax.random.fold_in(_gk, 11), (106250, 128), jnp.float32)
        return (x, src, dst, edge_attr_128)
    x, src, dst, edge_attr_128 = _rec_inputs()

    def _L0_gnn_setup():
        import jax, jax.numpy as jnp
        import numpy as np
        N_NODES = 12500
        N_EDGES = 400000
        D_FEAT = 128
        K = 10
        ALPHA = 0.1

        def _appnp(x, src, dst, norm, n_nodes):
            h = x

            def step(xk, _):
                msg = norm[:, None] * xk[src]
                agg = jax.ops.segment_sum(msg, dst, num_segments=n_nodes)
                return ((1.0 - ALPHA) * agg + ALPHA * h, None)
            xK, _ = jax.lax.scan(step, x, None, length=K)
            return xK
        key = jax.random.key(seed)
        k1, k2 = jax.random.split(key)
        x = jax.random.normal(k1, (N_NODES, D_FEAT), dtype=jnp.float32)
        edge_index = jax.random.randint(k2, (2, N_EDGES), 0, N_NODES, dtype=jnp.int64)
        return {'x': x, 'edge_index': edge_index}
    _L0_gnn_all = _L0_gnn_setup()
    _L0_gnn_in = {k: v for k, v in _L0_gnn_all.items() if k in ()}
    del _L0_gnn_all

    def _L1_gnn_setup():
        import jax, jax.numpy as jnp
        import numpy as np
        N_NODES = 6250
        N_EDGES = 100000
        DIM = 128
        key = jax.random.key(seed)
        k1, k2, k3, k4, k5, k6 = jax.random.split(key, 6)
        node_emb = jax.random.normal(k1, (N_NODES, DIM), dtype=jnp.float32)
        edge_emb = jax.random.normal(k2, (N_EDGES, DIM), dtype=jnp.float32)
        W_att_w = jax.random.normal(k3, (2 * DIM,), dtype=jnp.float32) * 0.05
        W_att_b = jax.random.normal(k4, (1,), dtype=jnp.float32) * 0.05
        src = jax.random.randint(k5, (N_EDGES,), 0, N_NODES, dtype=jnp.int32)
        off = jax.random.randint(k6, (N_EDGES,), 1, N_NODES, dtype=jnp.int32)
        dst = (src + off) % N_NODES
        edge_list = jnp.stack([src, dst], axis=1)
        return {'node_emb': node_emb, 'edge_emb': edge_emb, 'W_att_w': W_att_w, 'W_att_b': W_att_b, 'edge_list': edge_list}
    _L1_gnn_all = _L1_gnn_setup()
    _L1_gnn_in = {k: v for k, v in _L1_gnn_all.items() if k in ('W_att_w', 'W_att_b')}
    del _L1_gnn_all
    return {'x': x, 'src': src, 'dst': dst, 'edge_attr_128': edge_attr_128, 'L1_gnn_W_att_w': _L1_gnn_in['W_att_w'], 'L1_gnn_W_att_b': _L1_gnn_in['W_att_b']}

def reference(x, src, dst, edge_attr_128, L1_gnn_W_att_w, L1_gnn_W_att_b):
    import jax
    import jax.numpy as jnp

    def _L0_gnn_ref(x, edge_index):
        import jax, jax.numpy as jnp
        import numpy as np
        N_NODES = 12500
        N_EDGES = 400000
        D_FEAT = 128
        K = 10
        ALPHA = 0.1

        def _appnp(x, src, dst, norm, n_nodes):
            h = x

            def step(xk, _):
                msg = norm[:, None] * xk[src]
                agg = jax.ops.segment_sum(msg, dst, num_segments=n_nodes)
                return ((1.0 - ALPHA) * agg + ALPHA * h, None)
            xK, _ = jax.lax.scan(step, x, None, length=K)
            return xK
        n = x.shape[0]
        src = edge_index[0]
        dst = edge_index[1]
        loop = jnp.arange(n, dtype=src.dtype)
        src = jnp.concatenate([src, loop])
        dst = jnp.concatenate([dst, loop])
        ones = jnp.ones(src.shape[0], dtype=x.dtype)
        deg = jax.ops.segment_sum(ones, dst, num_segments=n)
        deg_inv_sqrt = jnp.where(deg > 0, jax.lax.rsqrt(deg), 0.0)
        norm = deg_inv_sqrt[src] * deg_inv_sqrt[dst]
        out = _appnp(x, src, dst, norm, n)
        return jax.nn.relu(out)

    def _L1_gnn_ref(node_emb, edge_emb, W_att_w, W_att_b, edge_list):
        import jax, jax.numpy as jnp
        import numpy as np
        N_NODES = 6250
        N_EDGES = 100000
        DIM = 128
        n_nodes, node_dim = node_emb.shape
        n_edges = edge_emb.shape[0]
        w_n = W_att_w[:node_dim]
        w_e = W_att_w[node_dim:]
        b = W_att_b[0]
        seg = jnp.concatenate([edge_list[:, 0], edge_list[:, 1]])
        s_node = node_emb @ w_n
        s_edge = edge_emb @ w_e
        raw = s_node[seg] + jnp.concatenate([s_edge, s_edge]) + b
        score = jax.nn.leaky_relu(raw, negative_slope=0.2)
        m = jax.ops.segment_max(score, seg, num_segments=n_nodes)
        m = jnp.where(jnp.isfinite(m), m, 0.0)
        ex = jnp.exp(score - m[seg])
        denom = jax.ops.segment_sum(ex, seg, num_segments=n_nodes)
        denom_safe = jnp.where(denom > 0, denom, 1.0)
        att = ex / denom_safe[seg]
        ee2 = jnp.concatenate([edge_emb, edge_emb], axis=0)
        agg = jax.ops.segment_sum(att[:, None] * ee2, seg, num_segments=n_nodes)
        out = jax.nn.gelu(agg, approximate=False)
        deg = jax.ops.segment_sum(jnp.ones_like(score), seg, num_segments=n_nodes)
        return jnp.where((deg > 0)[:, None], out, node_emb)
    edge_index = jnp.stack([src, dst])
    edge_index_t = jnp.stack([src, dst], axis=1)
    x = _layernorm(x + _L0_gnn_ref(x, edge_index), axis=-1)
    x = _layernorm(x + _L1_gnn_ref(x, edge_attr_128, L1_gnn_W_att_w, L1_gnn_W_att_b, edge_index_t), axis=-1)
    return x

_drawn_inputs = setup_inputs


def setup_inputs(seed=0):
    import zlib

    import numpy as np

    out = dict(_drawn_inputs(seed))
    spreads = {}
    factors = {}
    for name, (base, spread) in spreads.items():
        noise = np.random.default_rng([zlib.crc32(name.encode()), seed]).standard_normal(out[name].shape)
        drawn = base * np.exp(spread * noise) if base else spread * noise
        out[name] = jnp.asarray(drawn.astype(out[name].dtype))
    for name, factor in factors.items():
        out[name] = (out[name] * factor).astype(out[name].dtype)
    return out
```

```python
import concourse.bass as bass
from concourse import mybir
from contextlib import ExitStack, contextmanager

P = 128
FINE = 8
KEY_ROWS = 3
SRC_BITS = 13
MOST_EQUAL = 15.0
STEPS = 10
ALPHA = 0.1
SLOPE = 0.2
EPS = 1e-5
BIG = 1e30
ONE, SCORE, DST1, SRC1, SRC = 128, 129, 130, 131, 132
ROW = 133

FP32, FP16, BF16 = mybir.dt.float32, mybir.dt.float16, mybir.dt.bfloat16
FP8, I32, U32, U16, U8 = mybir.dt.float8e4, mybir.dt.int32, mybir.dt.uint32, mybir.dt.uint16, mybir.dt.uint8
ALU = mybir.AluOpType
ACT = mybir.ActivationFunctionType
X = mybir.AxisListType.X
XY = mybir.AxisListType.XY


class Shapes:

    def __init__(self, n_nodes, n_edges):
        self.nodes, self.edges = n_nodes, n_edges
        self.EP = max(p for p in range(1, P + 1) if n_edges % p == 0)
        self.ET = n_edges // self.EP
        self.CH = max(c for c in range(1, 26) if self.ET % (2 * c) == 0)
        self.W = -(-n_nodes // P)
        mean = n_edges * P / n_nodes
        self.CAP = int(-(-(mean + 5 * mean ** 0.5) // P))
        self.WS = self.CAP * P
        assert self.W * self.WS >= n_edges and n_nodes < 1 << SRC_BITS
        self.FW = self.W * P // FINE
        self.FG = -(-self.FW // P)
        self.W8 = 8 * self.FG
        self.KR = n_edges // P + KEY_ROWS
        self.FC = FINE * self.W
        self.PAD = self.W * P


class Chain:

    def __init__(self, eng, sem):
        self.eng, self.sem, self.n = eng, sem, 0

    def add(self, ins):
        ins.then_inc(self.sem, 1)
        self.n = self.n + 1

    def wait(self):
        self.eng.wait_ge(self.sem, self.n)

    def link(self, ins):
        self.add(ins)
        self.wait()

    @contextmanager
    def loop(self, trips, per):
        start = self.n
        with self.eng.Fori(0, trips) as i:
            self.n = start + i * per
            counted = Counted(self, per)
            yield i
            counted.check()
        self.n = start + trips * per


class Counted:
    def __init__(self, chain, per):
        self.chain, self.per, self.calls = chain, per, 0
        self.add = chain.add
        chain.add = self.counting

    def counting(self, ins):
        self.calls += 1
        self.add(ins)

    def check(self):
        del self.chain.add
        assert self.calls == self.per, (self.calls, self.per)


def scratch(nc, name, shape, dtype):
    return nc.dram_tensor(name, shape, dtype)


def constants(nc, sb, s):
    c = {}
    c["row"] = sb("c_row", [P, P], FP32)
    c["row1"] = sb("c_row1", [P, P], FP32)
    c["col"] = sb("c_col", [P, 1], FP32)
    c["ident"] = sb("c_ident", [P, P], FP32)
    c["ident16"] = sb("c_ident16", [P, P], FP16)
    c["ones"] = sb("c_ones", [P, P], FP32)
    c["before"] = sb("c_before", [P, P], FP32)
    c["we"] = sb("c_we", [P, P], FP32)
    c["wn"] = sb("c_wn", [P, P], FP32)
    c["b"] = sb("c_b", [P, 1], FP32)
    return c


def slots_phase(nc, s, c, k, src, dst, att_w, att_b):
    ctx = ExitStack()
    with ctx:
        def sb(name, shape, dt):
            return ctx.enter_context(nc.sbuf_tensor(name, shape, dt))

        def sem(name):
            return ctx.enter_context(nc.semaphore(name))

        EP, ET, W = s.EP, s.ET, s.W
        ends = [sb("end_dst", [EP, ET + 1], I32), sb("end_src", [EP, ET + 1], I32)]
        window = [sb("win_dst", [EP, ET], FP16), sb("win_src", [EP, ET], FP16)]
        low = sb("low_dst", [EP, ET], FP16)
        tmp_i = sb("tmp_i", [EP, ET], I32)
        same = sb("same", [EP, ET], BF16)
        ones_e = sb("ones_e", [EP, ET], BF16)
        count = sb("count", [EP, ET], FP32)
        slot = [sb("slot_d", [EP, ET], FP32), sb("slot_s", [EP, ET], FP32)]
        own = sb("own_order", [EP, ET], FP32)
        tail = sb("tail_keys", [1, s.KR * P - s.edges], I32)
        key = sb("keys", [EP, ET], I32)
        total = [sb("tot_d", [P, W], FP32), sb("tot_s", [P, W], FP32)]
        accum = sb("accum", [P, 1], FP32)
        first = [sb("first_d", [P, W], FP32), sb("first_s", [P, W], FP32)]
        wins = [sb("wins_d", [P, W], FP32), sb("wins_s", [P, W], FP32)]
        winbase = sb("winbase", [P, W], FP32)
        onesw = sb("onesw", [P, s.W8], FP32)
        wstart = sb("wstart", [P, W + 1], FP32)
        most = sb("most", [P, 8], FP32)
        hot_lo = sb("hot_lo", [EP, 2, s.CH, P], FP16)
        hot_hi = sb("hot_hi", [EP, 2, s.CH, W], FP16)
        r8 = sb("row8", [P, P], FP32)
        below = sb("below", [P, P], FP32)
        group = sb("group", [P, P], FP32)
        wrow = sb("wrow", [P, s.W8], FP32)
        q16i = sb("q16i", [P, 1], I32)
        q16 = sb("q16", [P, 1], FP32)
        mask8 = sb("mask8", [P, s.W8], FP32)
        at8 = sb("at8", [P, s.W8], FP32)
        start8 = sb("start8", [P, s.FG], FP32)
        start8i = sb("start8i", [P, s.FG], I32)
        row8i = sb("row8i", [P, s.FG], I32)
        rowf = sb("rowf", [P, s.FG], FP32)
        c8 = sb("c8", [P, W], FP32)
        row16 = sb("row16", [P, P], FP16)
        wrow16 = sb("wrow16", [P, W], FP16)
        ps_deg = ctx.enter_context(nc.psum_tensor("ps_deg", [P, 512], FP32))
        ps = [ctx.enter_context(nc.psum_tensor(f"ps_tot{i}", [P, 512], FP32)) for i in range(4)]

        loaded, consts, own_dve, hots, hist, summed, totals = (
            sem("sl_loaded"), sem("sl_consts"), sem("sl_dve"), sem("sl_hots"), sem("sl_hist"),
            sem("sl_summed"), sem("sl_totals"))
        stored, keyed, degs = sem("sl_stored"), sem("sl_keyed"), sem("sl_degs")
        memd = sem("sl_memd")
        block = ctx.enter_context(nc.Block())
        n_loads = 8

        @block.sync
        def _(eng):
            eng.wait_ge(memd, 1)
            d = dst.rearrange("(p t) -> p t", t=ET)
            eng.dma_start(ends[0][:, 0:ET], d).then_inc(loaded, 16)
            eng.dma_start(ends[0][0:EP - 1, ET:ET + 1], d[1:EP, 0:1], allow_slow_non_contiguous=True).then_inc(loaded, 16)
            eng.dma_start(ends[1][:, 0:ET], src.rearrange("(p t) -> p t", t=ET)).then_inc(loaded, 16)
            w2 = att_w.rearrange("(a n) -> a n", a=2)
            eng.dma_start(c["wn"][:, :], w2[0:1, :].broadcast_to([P, P])).then_inc(loaded, 16)
            eng.dma_start(c["we"][:, :], w2[1:2, :].broadcast_to([P, P])).then_inc(loaded, 16)
            eng.dma_start(c["b"][:, :], att_b.rearrange("(a n) -> a n", a=1).broadcast_to([P, 1])).then_inc(loaded, 16)
            eng.wait_ge(keyed, 1)
            flat = k["keys"].rearrange("r c -> (r c)")
            eng.dma_start(flat[0:s.edges].rearrange("(p t) -> p t", t=ET), key[:, :]).then_inc(stored, 16)
            eng.dma_start(flat[s.edges:s.KR * P].rearrange("(a n) -> a n", a=1), tail[:, :]).then_inc(stored, 16)
            eng.wait_ge(stored, 32)

        @block.gpsimd
        def _(eng):
            def iota(out, pattern, base, mult):
                eng.iota(out, pattern, base=base, channel_multiplier=mult,
                         allow_small_or_imprecise_dtypes=True).then_inc(consts, 1)
            iota(c["row"][:, :], [[1, P]], 0, 0)
            iota(c["row1"][:, :], [[1, P]], 1, 0)
            iota(c["col"][:, :], [[0, 1]], 0, 1)
            iota(own[:, :], [[1, ET]], 0, ET)
            iota(winbase[:, :], [[s.WS, W]], -1, 0)
            iota(r8[:, :], [[0, P // 16], [FINE, 16]], 0, 0)
            iota(wrow[:, :], [[0, s.FG], [1, 8]], 0, 0)
            iota(q16i[:, :], [[0, 1]], 0, 1)
            iota(row16[:, :], [[1, P]], 0, 0)
            iota(wrow16[:, :], [[1, W]], 0, 0)
            iota(k["base8"][:, :], [[FINE * P, s.FG]], 0, FINE)
            iota(k["first_node"][:, :], [[P, W]], 0, 0)
            iota(k["wcol"][:, :], [[1, W]], 0, 0)

        N_CONSTS = 13

        @block.vector
        def _(eng):
            ch = Chain(eng, own_dve)
            eng.memset(ends[0][:, ET:ET + 1], 1 << SRC_BITS).then_inc(memd, 1)
            ch.add(eng.memset(c["ones"][:, :], 1.0))
            ch.add(eng.memset(ones_e[:, :], 1.0))
            ch.add(eng.memset(k["flags"][:, :], 0.0))
            for n in range(2):
                ch.add(eng.memset(slot[n][:, :], 0.0))
            ch.add(eng.memset(onesw[:, :], 1.0))
            ch.add(eng.memset(tail[:, :], (1 << SRC_BITS) - 1 << SRC_BITS))
            for t in total:
                ch.add(eng.memset(t[:, :], 0.0))
            ch.add(eng.memset(most[:, :], 0.0))
            ch.add(eng.memset(c8[:, :], 0.0))
            ch.add(eng.memset(at8[:, :], 0.0))
            eng.wait_ge(consts, N_CONSTS)
            ch.add(eng.tensor_scalar(c["ident"][:, :], c["row"][:, :], c["col"][:, 0:1], None, ALU.is_equal))
            ch.add(eng.tensor_scalar(c["ident16"][:, :], c["row"][:, :], c["col"][:, 0:1], None, ALU.is_equal))
            ch.add(eng.tensor_scalar(c["before"][:, :], c["row"][:, :], c["col"][:, 0:1], None, ALU.is_gt))
            ch.add(eng.tensor_scalar(below[:, :], r8[:, :], c["col"][:, 0:1], None, ALU.is_gt))
            ch.add(eng.tensor_scalar(group[:, :], r8[:, :], float(FINE), c["col"][:, 0:1], ALU.add, ALU.is_gt))
            ch.link(eng.tensor_scalar(q16i[:, :], q16i[:, :], 4, None, ALU.logical_shift_right))
            ch.add(eng.tensor_tensor(group[:, :], group[:, :], below[:, :], ALU.subtract))
            ch.link(eng.tensor_copy(q16[:, :], q16i[:, :]))
            ch.add(eng.tensor_scalar(mask8[:, :], wrow[:, :], q16[:, 0:1], None, ALU.is_equal))
            eng.wait_ge(loaded, 16 * 6)
            for n in range(2):
                ch.link(eng.tensor_scalar(tmp_i[:, :], ends[n][:, 0:ET], 7, None, ALU.logical_shift_right))
                ch.link(eng.tensor_copy(window[n][:, :], tmp_i[:, :]))
                ch.add(eng.tensor_scalar(k["end1"][n][:, :], ends[n][:, 0:ET], 1.0, None, ALU.add))
            ch.link(eng.tensor_scalar(tmp_i[:, :], ends[0][:, 0:ET], P - 1, None, ALU.bitwise_and))
            ch.add(eng.tensor_copy(low[:, :], tmp_i[:, :]))
            ch.add(eng.tensor_copy(k["src_i"][:, :], ends[1][:, 0:ET]))
            ch.link(eng.tensor_scalar(key[:, :], ends[0][:, 0:ET], SRC_BITS, None, ALU.logical_shift_left))
            eng.tensor_tensor(key[:, :], key[:, :], ends[1][:, 0:ET], ALU.bitwise_or).then_inc(keyed, 1)
            ch.link(eng.tensor_tensor(count[:, :], ends[0][:, 0:ET], ends[0][:, 1:ET + 1], ALU.is_gt))
            ch.link(eng.tensor_reduce(most[0:EP, 0:1], count[:, :], X, ALU.add))

            for n in range(2):
                with ch.loop(W, 2) as h:
                    ch.link(eng.tensor_scalar(same[:, :], window[n][:, :], k["wcol"][0:EP, bass.ds(h, 1)], 0.0,
                                              ALU.is_equal, ALU.add, accum_out=accum[0:EP, :]))
                    ch.link(eng.tensor_copy(total[n][0:EP, bass.ds(h, 1)], accum[0:EP, :]))
            eng.drain().then_inc(totals, 1)

            n_ch = ET // (2 * s.CH)
            with ch.loop(n_ch, 0) as i:
                for b in range(2):
                    eng.wait_ge(hist, i * 2 + b + 1)
                    cols = slice(None), bass.ds((i * 2 + b) * s.CH, s.CH)
                    eng.tensor_tensor(hot_lo[:, b, :, :], row16[0:EP, :].unsqueeze(1).broadcast_to([EP, s.CH, P]),
                                      low[cols].unsqueeze(2).broadcast_to([EP, s.CH, P]),
                                      ALU.is_equal).then_inc(hots, 1)
                    eng.tensor_tensor(hot_hi[:, b, :, :], wrow16[0:EP, :].unsqueeze(1).broadcast_to([EP, s.CH, W]),
                                      window[0][cols].unsqueeze(2).broadcast_to([EP, s.CH, W]),
                                      ALU.is_equal).then_inc(hots, 1)

            eng.wait_ge(summed, 2)
            for n in range(2):
                ch.add(eng.tensor_tensor(first[n][:, :], ps[0][:, n * W:(n + 1) * W], winbase[:, :], ALU.add))
                ch.add(eng.tensor_copy(wins[n][:, :], ps[1][:, n * W:(n + 1) * W]))
            ch.link(eng.memset(wstart[:, 0:1], 0.0))
            ch.add(eng.tensor_scalar(k["flags"][:, 2:3], ps[2][:, 0:1], 0.0, None, ALU.is_equal))
            for n in range(2):
                ch.add(eng.tensor_reduce(most[:, 2 + n:3 + n], wins[n][:, :], X, ALU.max))
            ch.link(eng.tensor_tensor_scan(wstart[:, 1:W + 1], onesw[:, 0:W], wins[0][:, :], 0.0, ALU.mult, ALU.add))
            ch.link(eng.tensor_tensor(most[:, 4:5], most[:, 2:3], most[:, 3:4], ALU.max))
            ch.link(eng.tensor_scalar(k["flags"][:, 0:1], most[:, 4:5], float(s.WS), None, ALU.is_le))

            for n in range(2):
                with ch.loop(W, 4) as h:
                    ch.link(eng.tensor_scalar(same[:, :], window[n][:, :], k["wcol"][0:EP, bass.ds(h, 1)], None,
                                              ALU.is_equal))
                    ch.link(eng.tensor_tensor_scan(count[:, :], ones_e[:, :], same[:, :],
                                                   first[n][0:EP, bass.ds(h, 1)], ALU.mult, ALU.add))
                    ch.link(eng.tensor_tensor(count[:, :], count[:, :], same[:, :], ALU.mult))
                    ch.link(eng.tensor_tensor(slot[n][:, :], slot[n][:, :], count[:, :], ALU.add))
                ch.link(eng.tensor_tensor(slot[n][:, :], slot[n][:, :], own[:, :], ALU.subtract))
                ch.link(eng.scalar_tensor_tensor(k["slot"][n][:, :], slot[n][:, :], k["flags"][0:EP, 0:1],
                                                 own[:, :], ALU.mult, ALU.add))

            eng.wait_ge(hist, 2 * n_ch + 2)
            ch.add(eng.tensor_scalar(k["deg"][:, :], ps_deg[:, 0:W], 1.0, None, ALU.add))
            eng.tensor_copy(k["deg0"][:, :], ps_deg[:, 0:W]).then_inc(degs, 1)
            eng.wait_ge(summed, 3)
            ch.link(eng.tensor_tensor(at8[:, 0:W], ps[3][:, 0:W], wstart[:, 0:W], ALU.add))
            ch.link(eng.tensor_tensor(at8[:, :], at8[:, :], mask8[:, :], ALU.mult))
            ch.link(eng.tensor_reduce(start8[:, :], at8[:, :].rearrange("p (g w) -> p g w", w=8), X, ALU.add))
            ch.link(eng.tensor_copy(start8i[:, :], start8[:, :]))
            ch.link(eng.tensor_scalar(row8i[:, :], start8i[:, :], 7, None, ALU.logical_shift_right))
            ch.link(eng.tensor_copy(rowf[:, :], row8i[:, :]))
            for r in range(KEY_ROWS):
                ch.add(eng.tensor_scalar(k["keyrow"][:, r, :], rowf[:, :], float(r), None, ALU.add))
            ch.link(eng.tensor_copy(c8[:, :], ps[3][:, W:2 * W]))
            ch.link(eng.tensor_reduce(k["most8"][:, :], c8[:, :], X, ALU.max))

        @block.tensor
        def _(eng):
            eng.sem_inc(hist, 2)
            eng.wait_ge(totals, 1)
            for n in range(2):
                eng.matmul(ps[0][:, n * W:(n + 1) * W], c["before"][:, :], total[n][:, :], start=True, stop=True)
                eng.matmul(ps[1][:, n * W:(n + 1) * W], c["ones"][:, :], total[n][:, :], start=True, stop=True)
            eng.matmul(ps[2][:, 0:1], c["ones"][:, :], most[:, 0:1], start=True, stop=True).then_inc(summed, 2)
            n_ch = ET // (2 * s.CH)

            def chunk(b, n, first, last):
                eng.wait_ge(hots, 2 * n + 2)
                for t in range(s.CH):
                    m = eng.matmul(ps_deg[:, 0:W], hot_lo[:, b, t, :], hot_hi[:, b, t, :],
                                   start=first and t == 0, stop=last and t == s.CH - 1)
                m.then_inc(hist, 1)
            chunk(0, 0, True, False)
            chunk(1, 1, False, n_ch == 1)
            if n_ch > 1:
                if n_ch > 2:
                    with eng.Fori(1, n_ch - 1) as i:
                        chunk(0, i * 2, False, False)
                        chunk(1, i * 2 + 1, False, False)
                chunk(0, 2 * n_ch - 2, False, False)
                chunk(1, 2 * n_ch - 1, False, True)
            eng.wait_ge(degs, 1)
            eng.matmul(ps[3][:, 0:W], below[:, :], k["deg0"][:, :], start=True, stop=True)
            eng.matmul(ps[3][:, W:2 * W], group[:, :], k["deg0"][:, :], start=True, stop=True).then_inc(summed, 1)


def kept(nc, sb, s):
    k = {}
    k["slot"] = [sb("k_slot_d", [s.EP, s.ET], I32), sb("k_slot_s", [s.EP, s.ET], I32)]
    k["end1"] = [sb("k_dst1", [s.EP, s.ET], FP32), sb("k_src1", [s.EP, s.ET], FP32)]
    k["src_i"] = sb("k_src_i", [s.EP, s.ET], I32)
    k["wcol"] = sb("k_wcol", [P, s.W], FP32)
    k["base8"] = sb("k_base8", [P, s.FG], FP32)
    k["deg"] = sb("k_deg", [P, s.W], FP32)
    k["deg0"] = sb("k_deg0", [P, s.W], FP32)
    k["keyrow"] = sb("k_keyrow", [P, KEY_ROWS, s.FG], I32)
    k["most8"] = sb("k_most8", [P, 1], FP32)
    k["flags"] = sb("k_flags", [P, 4], FP32)
    k["list"] = [scratch(nc, f"edge_list_{n}", [s.W * s.WS, ROW], FP32).ap() for n in ("dst", "src")]
    k["root"] = sb("k_root", [P, s.W], FP32)
    k["keep"] = sb("k_keep", [P, s.W], FP32)
    k["unscale"] = sb("k_unscale", [P, 1], FP32)
    k["first_node"] = sb("k_first_node", [P, s.W], FP32)
    k["node_rows"] = scratch(nc, "node_rows", [s.W, 2, P], FP32).ap()
    k["z_rows"] = scratch(nc, "z_rows", [s.PAD, P], FP32).ap()
    k["adj"] = scratch(nc, "adjacency", [s.W, P, s.W * P // 4], U32).ap()
    k["dense"] = sb("k_dense", [P, 1], I32)
    k["by_window"] = sb("k_by_window", [P, 1], I32)
    k["keys"] = scratch(nc, "edge_keys", [s.KR, P], I32).ap()
    return k


def scatter_phase(nc, s, c, k, edge_rows):
    ctx = ExitStack()
    with ctx:
        def sb(name, shape, dt):
            return ctx.enter_context(nc.sbuf_tensor(name, shape, dt))

        def sem(name):
            return ctx.enter_context(nc.semaphore(name))

        EP, CH = s.EP, s.CH
        pairs = s.ET // (2 * CH)
        per_stage = 16 * 2 * CH
        zeros = sb("zeros", [P, s.CAP * ROW], FP32)
        stage = [sb(f"stage{b}", [EP, CH, ROW], FP32) for b in range(2)]
        place = [sb(f"place{b}", [EP, 2, CH], I32) for b in range(2)]
        product = sb("product", [EP, CH, P], FP32)
        zeroed, blank, own_dve, begun = sem("sc_zeroed"), sem("sc_blank"), sem("sc_dve"), sem("sc_begun")
        loaded = [sem(f"sc_loaded{b}") for b in range(2)]
        filled = [sem(f"sc_filled{b}") for b in range(2)]
        scattered = [sem(f"sc_scattered{b}") for b in range(2)]
        rows = edge_rows.rearrange("(p t) f -> p t f", t=s.ET)
        flat = [k["list"][n].rearrange("(w p q) f -> w p (q f)", p=P, q=s.CAP) for n in range(2)]
        block = ctx.enter_context(nc.Block())

        @block.sync
        def _(eng):
            eng.wait_ge(blank, 1)
            with eng.Fori(0, s.W) as w:
                for n in range(2):
                    eng.dma_start(flat[n][bass.ds(w, 1), :, :].squeeze(0), zeros[:, :]).then_inc(zeroed, 16)
            with eng.Fori(0, pairs) as i:
                for b in range(2):
                    eng.wait_ge(scattered[b], per_stage * i)
                    eng.dma_start(stage[b][:, :, 0:P], rows[:, bass.ds((2 * i + b) * CH, CH), :]).then_inc(loaded[b], 16)

        @block.vector
        def _(eng):
            ch = Chain(eng, own_dve)
            eng.memset(zeros[:, :], 0.0).then_inc(blank, 1)
            for b in range(2):
                ch.add(eng.memset(stage[b][:, :, ONE:ONE + 1], 1.0))
            with ch.loop(pairs, 2) as i:
                for b in range(2):
                    cols = slice(None), bass.ds((2 * i + b) * CH, CH)
                    eng.wait_ge(scattered[b], per_stage * i)
                    for n in range(2):
                        eng.tensor_copy(place[b][:, n, :], k["slot"][n][cols])
                        eng.tensor_copy(stage[b][:, :, DST1 + n], k["end1"][n][cols])
                    eng.tensor_copy(stage[b][:, :, SRC].bitcast(I32), k["src_i"][cols])
                    eng.wait_ge(loaded[b], 16 * (i + 1))
                    ch.link(eng.tensor_tensor(product[:, :, :], stage[b][:, :, 0:P],
                                              c["we"][0:EP, :].unsqueeze(1).broadcast_to([EP, CH, P]), ALU.mult))
                    eng.tensor_reduce(stage[b][:, :, SCORE], product[:, :, :], X, ALU.add).then_inc(filled[b], 1)
                    eng.wait_ge(filled[b], i + 1)

        @block.gpsimd
        def _(eng):
            with eng.Fori(0, pairs) as i:
                for b in range(2):
                    eng.wait_ge(filled[b], i + 1)
                    eng.wait_ge(zeroed, 16 * 2 * s.W)
                    eng.sem_inc(begun, 1)
                    for t in range(CH):
                        for n in range(2):
                            eng.indirect_dma_start(
                                k["list"][n], bass.IndirectOffsetOnAxis(ap=place[b][:, n, t:t + 1], axis=0),
                                stage[b][:, t, :], None).then_inc(scattered[b], 16)
            for b in range(2):
                eng.wait_ge(scattered[b], per_stage * pairs)


def adjacency_phase(nc, s, c, k):
    ctx = ExitStack()
    with ctx:
        def sb(name, shape, dt):
            return ctx.enter_context(nc.sbuf_tensor(name, shape, dt))

        def sem(name):
            return ctx.enter_context(nc.semaphore(name))

        W, FG, FC, R = s.W, s.FG, s.FC, KEY_ROWS
        RING = 4
        G = P // FINE
        NK = FG * R * P
        key = sb("a_key", [P, FG, R, P], I32)
        tmp = sb("a_tmp", [P, FG, R, P], I32)
        lowf = sb("a_lowf", [P, FG, R, P], FP32)
        node = sb("a_node", [P, FG, R, P], FP32)
        column = sb("a_column", [P, FG, R, P], FP32)
        inside = sb("a_inside", [P, FG, R, P], FP32)
        turned = [sb(f"a_turned{n}", [P, R, FG * P], FP32) for n in range(2)]
        hot_low = sb("a_hot_low", [P, RING, R, P], FP16)
        hot_col = sb("a_hot_col", [P, RING, R, FC], FP16)
        cols = sb("a_cols", [P, FC], FP16)
        row16 = sb("a_row16", [P, P], FP16)
        out8 = [sb(f"a_out{b}", [P, W, P], FP8) for b in range(2)]
        part = [sb(f"a_part{b}", [P, G], FP32) for b in range(2)]
        sums = sb("a_sums", [P, W * G], FP32)
        most = sb("a_most", [P, 4], FP32)
        allmost = sb("a_allmost", [P, 4], FP32)
        flat = lambda t: t[:, :, :, :].rearrange("p g r e -> p (g r e)")
        psum = [ctx.enter_context(nc.psum_tensor(f"a_ps{i}", [P, 512], FP32)) for i in range(RING)]
        pst = [ctx.enter_context(nc.psum_tensor(f"a_pst{i}", [P, 512], FP32)) for i in range(2)]

        gathered, consts, own_dve, ready, turn, copied = (
            sem("ad_gathered"), sem("ad_consts"), sem("ad_dve"), sem("ad_ready"), sem("ad_turn"), sem("ad_copied"))
        begun = sem("ad_begun")
        hot, built, evicted, summed, most_ready, most_all = (
            sem("ad_hot"), sem("ad_built"), sem("ad_evicted"), sem("ad_summed"), sem("ad_most"), sem("ad_most_all"))
        stored = [sem(f"ad_stored{b}") for b in range(2)]
        turns = [(g, r, n) for g in range(FG) for r in range(R) for n in range(2)]
        block = ctx.enter_context(nc.Block())

        def windows(eng, body):
            if W > 1:
                with eng.Fori(0, W // 2) as i:
                    for b in range(2):
                        body(2 * i + b, b, i)
            if W % 2:
                body(W - 1, 0, W // 2)

        @block.gpsimd
        def _(eng):
            eng.iota(cols[:, :], [[1, FC]], base=0, channel_multiplier=0,
                     allow_small_or_imprecise_dtypes=True).then_inc(consts, 1)
            eng.iota(row16[:, :], [[1, P]], base=0, channel_multiplier=0,
                     allow_small_or_imprecise_dtypes=True).then_inc(consts, 1)
            for g in range(FG):
                for r in range(R):
                    eng.indirect_dma_start(
                        key[:, g, r, :], None, k["keys"],
                        bass.IndirectOffsetOnAxis(ap=k["keyrow"][:, r, g:g + 1], axis=0)).then_inc(gathered, 16)
            eng.wait_ge(most_ready, 1)
            eng.partition_all_reduce(allmost[:, :], most[:, :], P, bass.bass_isa.ReduceOp.max).then_inc(most_all, 1)

        @block.vector
        def _(eng):
            ch = Chain(eng, own_dve)
            ch.add(eng.memset(most[:, :], 0.0))
            eng.wait_ge(gathered, 16 * FG * R)
            ch.link(eng.tensor_scalar(flat(tmp), flat(key), SRC_BITS, None, ALU.logical_shift_right))
            ch.add(eng.tensor_copy(flat(node), flat(tmp)))
            ch.link(eng.tensor_scalar(flat(key), flat(key), (1 << SRC_BITS) - 1, None, ALU.bitwise_and))
            ch.link(eng.tensor_scalar(flat(tmp), flat(key), P - 1, None, ALU.bitwise_and))
            eng.tensor_copy(flat(lowf), flat(tmp)).then_inc(ready, 1)
            ch.link(eng.tensor_scalar(flat(key), flat(key), 7, None, ALU.logical_shift_right))
            eng.wait_ge(ready, 1)
            ch.add(eng.tensor_copy(flat(column), flat(key)))
            for g in range(FG):
                ch.add(eng.tensor_scalar(node[:, g, :, :], node[:, g, :, :], k["base8"][:, g:g + 1], None,
                                         ALU.subtract))
            ch.wait()
            ch.add(eng.tensor_scalar(flat(inside), flat(node), 0.0, None, ALU.is_ge))
            ch.link(eng.scalar_tensor_tensor(flat(column), flat(column), float(FINE), flat(node), ALU.mult, ALU.add))
            ch.link(eng.scalar_tensor_tensor(flat(inside), flat(node), float(FINE - 1), flat(inside),
                                             ALU.is_le, ALU.mult))
            ch.link(eng.tensor_scalar(flat(inside), flat(inside), -1024.0, 1024.0, ALU.mult, ALU.add))
            eng.tensor_tensor(flat(column), flat(column), flat(inside), ALU.add).then_inc(ready, 1)
            eng.wait_ge(consts, 2)
            eng.wait_ge(copied, 2 + len(turns))

            def body(j, b, visit):
                for g in range(G):
                    n = j * G + g
                    r0 = g % RING
                    eng.wait_ge(built, n + 1)
                    for r in range(R):
                        eng.tensor_scalar(hot_low[:, r0, r, :], row16[:, :], turned[0][:, r, bass.ds(n, 1)], None,
                                          ALU.is_equal)
                        ins = eng.tensor_scalar(hot_col[:, r0, r, :], cols[:, :], turned[1][:, r, bass.ds(n, 1)],
                                                None, ALU.is_equal)
                    ins.then_inc(hot, 1)
            windows(eng, body)
            eng.wait_ge(summed, W)
            ch.add(eng.tensor_reduce(most[:, 0:1], sums[:, :], X, ALU.max))
            eng.tensor_copy(most[:, 1:2], k["most8"][:, :]).then_inc(most_ready, 1)
            eng.wait_ge(most_all, 1)
            ch.link(eng.tensor_scalar(most[:, 2:3], allmost[:, 0:1], MOST_EQUAL, None, ALU.is_le))
            ch.link(eng.tensor_scalar(most[:, 3:4], allmost[:, 1:2], float((R - 1) * P), None, ALU.is_le))
            ch.link(eng.tensor_tensor(most[:, 2:3], most[:, 2:3], most[:, 3:4], ALU.mult))
            ch.link(eng.tensor_tensor(most[:, 2:3], most[:, 2:3], k["flags"][:, 2:3], ALU.mult))
            ch.link(eng.tensor_copy(k["dense"][:, :], most[:, 2:3]))
            ch.link(eng.tensor_copy(k["by_window"][:, :], k["flags"][:, 0:1]))

        @block.tensor
        def _(eng):
            eng.sem_inc(built, RING)
            eng.wait_ge(ready, 2)
            for i, (g, r, n) in enumerate(turns):
                eng.wait_ge(copied, i + 1)
                eng.transpose(pst[i % 2][:, 0:P], (lowf, column)[n][:, g, r, :], c["ident"][:, :]).then_inc(turn, 1)

            def body(j, b, visit):
                for g in range(G):
                    n = j * G + g
                    eng.wait_ge(hot, n + 1)
                    eng.wait_ge(evicted, n + 1)
                    for r in range(R):
                        m = eng.matmul(psum[g % RING][:, 0:FC], hot_low[:, g % RING, r, :], hot_col[:, g % RING, r, :],
                                       start=r == 0, stop=r == R - 1)
                    m.then_inc(built, 1)
            windows(eng, body)

        @block.scalar
        def _(eng):
            eng.sem_inc(copied, 2)
            for i, (g, r, n) in enumerate(turns):
                eng.wait_ge(turn, i + 1)
                eng.copy(turned[n][:, r, g * P:(g + 1) * P], pst[i % 2][:, 0:P]).then_inc(copied, 1)
            eng.sem_inc(evicted, RING)

            def body(j, b, visit):
                eng.wait_ge(stored[b], 16 * visit)
                eng.wait_ge(summed, j)
                for g in range(G):
                    n = j * G + g
                    eng.wait_ge(built, RING + n + 1)
                    eng.sem_inc(begun, 1)
                    eng.activation(out8[b][:, :, FINE * g:FINE * (g + 1)],
                                   psum[g % RING][:, 0:FC].rearrange("p (w f) -> p w f", f=FINE), ACT.Copy,
                                   accum_out=part[b][:, g:g + 1], saturate=False).then_inc(evicted, 1)
                eng.wait_ge(evicted, RING + (j + 1) * G)
                eng.copy(sums[:, bass.ds(j * G, G)], part[b][:, :]).then_inc(summed, 1)
            windows(eng, body)

        @block.sync
        def _(eng):
            def body(j, b, visit):
                eng.wait_ge(evicted, RING + (j + 1) * G)
                eng.dma_start(k["adj"][bass.ds(j, 1), :, :].squeeze(0),
                              out8[b][:, :, :].rearrange("p w n -> p (w n)").bitcast(U32)).then_inc(stored[b], 16)
            windows(eng, body)
            for b in range(2):
                eng.wait_ge(stored[b], 16 * ((W + 1 - b) // 2))




def load_nodes(eng, s, tile, x, done):
    full, rest = s.nodes // P, s.nodes % P
    eng.dma_start(tile[:, 0:full, :], x[0:full * P, :].rearrange("(w p) f -> p w f", p=P)).then_inc(done, 16)
    if rest:
        eng.dma_start(tile[0:rest, full, :], x[full * P:s.nodes, :]).then_inc(done, 16)
    return 32 if rest else 16


def prepare_phase(nc, s, c, k, v, x):
    ctx = ExitStack()
    with ctx:
        def sb(name, shape, dt):
            return ctx.enter_context(nc.sbuf_tensor(name, shape, dt))

        def sem(name):
            return ctx.enter_context(nc.semaphore(name))

        W = s.W
        inv_root = sb("p_inv_root", [P, W], FP32)
        most = sb("p_most", [P, 1], FP32)
        power = sb("p_power", [P, 1], FP32)
        scale = sb("p_scale", [P, 1], FP32)
        blank, loaded, rooted, own_dve, part, whole = (
            sem("pr_blank"), sem("pr_loaded"), sem("pr_rooted"), sem("pr_dve"), sem("pr_part"), sem("pr_whole"))
        z, z01, pieces = v["z"], v["z01"], v["pieces"][0]
        wide = lambda t: t[:, :].unsqueeze(2).broadcast_to([P, W, P])
        counts = [0]
        block = ctx.enter_context(nc.Block())

        @block.sync
        def _(eng):
            eng.wait_ge(blank, 1)
            counts[0] = load_nodes(eng, s, z, x, loaded)

        @block.scalar
        def _(eng):
            eng.activation(k["root"][:, :], k["deg"][:, :], ACT.Sqrt).then_inc(rooted, 1)

        @block.gpsimd
        def _(eng):
            eng.wait_ge(part, 1)
            eng.partition_all_reduce(power[:, :], most[:, :], P, bass.bass_isa.ReduceOp.max).then_inc(whole, 1)

        @block.vector
        def _(eng):
            ch = Chain(eng, own_dve)
            eng.memset(z[:, W - 1, :], 0.0).then_inc(blank, 1)
            ch.link(eng.reciprocal(k["keep"][:, :], k["deg"][:, :]))
            ch.add(eng.tensor_scalar(k["keep"][:, :], k["keep"][:, :], 1.0 - ALPHA, None, ALU.mult))
            eng.wait_ge(rooted, 1)
            ch.link(eng.reciprocal(inv_root[:, :], k["root"][:, :]))
            eng.wait_ge(loaded, counts[0])
            ch.link(eng.tensor_tensor(z[:, :, :], z[:, :, :], wide(inv_root), ALU.mult))
            eng.tensor_reduce(most[:, :], z[:, :, :], XY, ALU.max, apply_absolute_value=True).then_inc(part, 1)
            eng.wait_ge(whole, 1)
            bits, sbits = power[:, :].bitcast(I32), scale[:, :].bitcast(I32)
            ch.link(eng.tensor_scalar(bits, bits, 0x7F800000, None, ALU.bitwise_and))
            ch.link(eng.tensor_scalar(bits, bits, float(16 << 23), None, ALU.max))
            ch.link(eng.tensor_scalar(sbits, bits, -1.0, float((127 + 127 + 14) << 23), ALU.mult, ALU.add))
            ch.add(eng.tensor_scalar(k["unscale"][:, :].bitcast(I32), sbits, -1.0, float((127 + 127) << 23),
                                     ALU.mult, ALU.add))
            ch.link(eng.tensor_scalar(z[:, :, :], z[:, :, :], scale[:, 0:1], None, ALU.mult))
            ch.add(eng.tensor_scalar(z01[:, :, :], z[:, :, :], ALPHA, None, ALU.mult))
            ch.link(eng.tensor_copy(pieces[:, :, 0:P], z[:, :, :]))
            ch.link(eng.tensor_tensor(pieces[:, :, P:2 * P], z[:, :, :], pieces[:, :, 0:P], ALU.subtract))


def appnp_phase(nc, s, c, k, v):
    ctx = ExitStack()
    with ctx:
        def sb(name, shape, dt):
            return ctx.enter_context(nc.sbuf_tensor(name, shape, dt))

        def sem(name):
            return ctx.enter_context(nc.semaphore(name))

        W, CAP = s.W, s.CAP
        NB = max([b for b in range(3, 8) if W % b == 0] or [4])
        visits = [W // NB + (b < W % NB) for b in range(NB)]
        z, z01, pieces = v["z"], v["z01"], v["pieces"]
        matrix = [sb(f"matrix{b}", [P, W, P], FP8) for b in range(NB)]
        part = [sb(f"z_part{b}", [P, P], FP32) for b in range(NB)]
        psum = [ctx.enter_context(nc.psum_tensor(f"z_ps{b}", [P, 512], FP32)) for b in range(NB)]
        loaded = [sem(f"ap_loaded{b}") for b in range(NB)]
        summed = [sem(f"ap_summed{b}") for b in range(NB)]
        added = [sem(f"ap_added{b}") for b in range(NB)]
        scaled, own_dve, updated = sem("ap_scaled"), sem("ap_dve"), sem("ap_updated")
        meta = sb("g_meta", [P, CAP, 3], FP32)
        gathered = sb("g_gathered", [P, CAP, P], FP32)
        hot = sb("g_hot", [P, CAP, P], FP32)
        names = sb("g_names", [P, P], FP32)
        acc = sb("g_acc", [P, P], FP32)
        psg = ctx.enter_context(nc.psum_tensor("g_ps", [P, 512], FP32))
        g_saved, g_meta, g_rows, g_hot, g_sum, g_used, g_done, g_own, g_begun = (
            sem("ge_saved"), sem("ge_meta"), sem("ge_rows"), sem("ge_hot"), sem("ge_sum"), sem("ge_used"),
            sem("ge_done"), sem("ge_own"), sem("ge_begun"))
        block = ctx.enter_context(nc.Block())

        def is_dense(eng):
            return eng.value_load(k["dense"][0:1, 0:1], min_val=0, max_val=1) == 1

        def steps(eng, body):
            with eng.Fori(0, STEPS // 2) as pair:
                for par in range(2):
                    step = pair * 2 + par
                    if W >= NB:
                        with eng.Fori(0, W // NB) as i:
                            for b in range(NB):
                                body(step, par, i * NB + b, b, step * visits[b] + i)
                    for b in range(W % NB):
                        body(step, par, W - W % NB + b, b, step * visits[b] + W // NB)

        def chunks(eng, body, step_start=lambda step: None):
            with eng.Fori(0, STEPS) as step:
                step_start(step)
                with eng.Fori(0, W) as w:
                    with eng.Fori(0, W) as ck:
                        body(step, ck, (step * W + w) * W + ck)

        @block.sync
        def _(eng):
            with eng.If(is_dense(eng)):
                def body(step, par, j, b, visit):
                    eng.wait_ge(summed[b], visit)
                    eng.dma_start(matrix[b][:, :, :].rearrange("p w n -> p (w n)").bitcast(U32),
                                  k["adj"][bass.ds(j, 1), :, :].squeeze(0)).then_inc(loaded[b], 16)
                steps(eng, body)
            with eng.Else():
                listed = k["list"][0].rearrange("(w p q) f -> w p q f", p=P, q=CAP)

                def step_start(step):
                    eng.wait_ge(g_done, step * W)
                    eng.dma_start(k["z_rows"].rearrange("(w p) f -> p w f", p=P), z[:, :, :]).then_inc(g_saved, 16)

                def body(step, ck, q):
                    eng.wait_ge(g_saved, 16 * (step + 1))
                    eng.wait_ge(g_used, q)
                    eng.dma_start(meta[:, :, :], listed[bass.ds(ck, 1), :, :, DST1:SRC + 1].squeeze(0))\
                       .then_inc(g_meta, 16)
                chunks(eng, body, step_start)

        @block.gpsimd
        def _(eng):
            with eng.If(is_dense(eng)):
                eng.engine_nop()
            with eng.Else():
                def body(step, ck, q):
                    eng.wait_ge(g_meta, 16 * (q + 1))
                    eng.sem_inc(g_begun, 1)
                    for t in range(CAP):
                        eng.indirect_dma_start(gathered[:, t, :], None, k["z_rows"], bass.IndirectOffsetOnAxis(
                            ap=meta[:, t, 2:3].bitcast(I32), axis=0)).then_inc(g_rows, 16)
                chunks(eng, body)
                eng.wait_ge(g_rows, 16 * CAP * STEPS * W * W)

        @block.tensor
        def _(eng):
            with eng.If(is_dense(eng)):
                def body(step, par, j, b, visit):
                    eng.wait_ge(updated, step * W)
                    eng.wait_ge(loaded[b], 16 * (visit + 1))
                    eng.wait_ge(added[b], visit)
                    out = psum[b][:, 0:2 * P]
                    eng.matmul(out, c["ident16"][:, :], pieces[par][:, bass.ds(j, 1), :].squeeze(1),
                               start=True, stop=False)
                    for w in range(W):
                        m = eng.matmul(out, matrix[b][:, w, :], pieces[par][:, w, :], start=False, stop=w == W - 1)
                    m.then_inc(summed[b], 1)
                steps(eng, body)
            with eng.Else():
                def body(step, ck, q):
                    eng.wait_ge(g_hot, q + 1)
                    eng.wait_ge(g_rows, 16 * CAP * (q + 1))
                    for t in range(CAP):
                        m = eng.matmul(psg[:, 0:P], hot[:, t, :], gathered[:, t, :], start=t == 0, stop=t == CAP - 1)
                    m.then_inc(g_sum, 1)
                chunks(eng, body)

        @block.scalar
        def _(eng):
            with eng.If(is_dense(eng)):
                def body(step, par, j, b, visit):
                    eng.wait_ge(summed[b], visit + 1)
                    eng.wait_ge(added[b], visit)
                    eng.activation(part[b][:, :], psum[b][:, P:2 * P], ACT.Copy,
                                   scale=k["keep"][:, bass.ds(j, 1)]).then_inc(scaled, 1)
                steps(eng, body)
            with eng.Else():
                eng.drain()

        @block.vector
        def _(eng):
            with eng.If(is_dense(eng)):
                def body(step, par, j, b, visit):
                    n = step * W + j
                    now = z[:, bass.ds(j, 1), :].squeeze(1)
                    new = pieces[1 - par][:, bass.ds(j, 1), :].squeeze(1)
                    eng.wait_ge(scaled, n + 1)
                    eng.scalar_tensor_tensor(now, psum[b][:, 0:P], k["keep"][:, bass.ds(j, 1)], part[b][:, :],
                                             ALU.mult, ALU.add).then_inc(added[b], 1)
                    eng.wait_ge(added[b], visit + 1)
                    eng.tensor_tensor(now, now, z01[:, bass.ds(j, 1), :].squeeze(1), ALU.add).then_inc(own_dve, 1)
                    eng.wait_ge(own_dve, 2 * n + 1)
                    eng.tensor_copy(new[:, 0:P], now).then_inc(own_dve, 1)
                    eng.wait_ge(own_dve, 2 * n + 2)
                    eng.tensor_tensor(new[:, P:2 * P], now, new[:, 0:P], ALU.subtract).then_inc(updated, 1)
                steps(eng, body)
            with eng.Else():
                per = 1 + 4 * W
                with eng.Fori(0, STEPS) as step:
                    eng.wait_ge(g_saved, 16 * (step + 1))
                    eng.wait_ge(g_own, step * per)
                    eng.tensor_copy(names[:, :], c["row1"][:, :]).then_inc(g_own, 1)
                    with eng.Fori(0, W) as w:
                        own = step * per + 1 + 4 * w
                        eng.wait_ge(g_own, own)
                        eng.wait_ge(g_done, step * W + w)
                        eng.memset(acc[:, :], 0.0).then_inc(g_own, 1)
                        with eng.Fori(0, W) as ck:
                            q = (step * W + w) * W + ck
                            eng.wait_ge(g_own, own + 1)
                            eng.wait_ge(g_meta, 16 * (q + 1))
                            eng.tensor_tensor(hot[:, :, :], names[:, :].unsqueeze(1).broadcast_to([P, CAP, P]),
                                              meta[:, :, 0:1].broadcast_to([P, CAP, P]),
                                              ALU.is_equal).then_inc(g_hot, 1)
                            eng.wait_ge(g_sum, q + 1)
                            eng.wait_ge(g_used, q)
                            eng.tensor_tensor(acc[:, :], acc[:, :], psg[:, 0:P], ALU.add).then_inc(g_used, 1)
                        now = z[:, bass.ds(w, 1), :].squeeze(1)
                        eng.wait_ge(g_used, (step * W + w + 1) * W)
                        eng.tensor_tensor(acc[:, :], acc[:, :], now, ALU.add).then_inc(g_own, 1)
                        eng.wait_ge(g_own, own + 2)
                        eng.tensor_scalar(acc[:, :], acc[:, :], k["keep"][:, bass.ds(w, 1)], None,
                                          ALU.mult).then_inc(g_own, 1)
                        eng.tensor_scalar(names[:, :], names[:, :], float(P), None, ALU.add).then_inc(g_own, 1)
                        eng.wait_ge(g_own, own + 4)
                        eng.tensor_tensor(now, acc[:, :], z01[:, bass.ds(w, 1), :].squeeze(1),
                                          ALU.add).then_inc(g_done, 1)
                    eng.wait_ge(g_done, (step + 1) * W)


def ring(eng, trips, body):
    if trips > 1:
        with eng.Fori(0, trips // 2) as i:
            for b in range(2):
                body(2 * i + b, b, i)
    if trips % 2:
        body(trips - 1, 0, trips // 2)


def window_chunks(eng, s, k, body):
    with eng.If(eng.value_load(k["by_window"][0:1, 0:1], min_val=0, max_val=1) == 1):
        ring(eng, s.W, lambda w, b, i: body(w, w, w, b, i))
    with eng.Else():
        with eng.Fori(0, s.W) as w:
            ring(eng, s.W, lambda ck, b, i: body(w, ck, w * s.W + ck, b, w * ((s.W + 1 - b) // 2) + i))


def maxima_phase(nc, s, c, k):
    ctx = ExitStack()
    with ctx:
        def sb(name, shape, dt):
            return ctx.enter_context(nc.sbuf_tensor(name, shape, dt))

        def sem(name):
            return ctx.enter_context(nc.semaphore(name))

        W, CAP = s.W, s.CAP
        banks = -(-CAP // 4)
        meta = [sb(f"m_meta{b}", [P, 2, CAP, 3], FP32) for b in range(2)]
        masked = [sb(f"m_masked{b}", [P, 2, CAP, P], FP32) for b in range(2)]
        names = sb("m_names", [P, P], FP32)
        best = sb("m_best", [P, W], FP32)
        new_best = sb("m_new_best", [P, 1], FP32)
        cand = sb("m_cand", [P, 2 * banks], FP32)
        turned = sb("m_turned", [P, P], FP32)
        psum = [ctx.enter_context(nc.psum_tensor(f"m_ps{i}", [P, 512], FP32)) for i in range(banks)]
        pst = ctx.enter_context(nc.psum_tensor("m_pst", [P, 512], FP32))
        loaded = [sem(f"mx_loaded{b}") for b in range(2)]
        turns = [sem(f"mx_turns{b}") for b in range(2)]
        masks, reads, own_dve, final, turn, flat, stored = (
            sem("mx_masks"), sem("mx_reads"), sem("mx_dve"), sem("mx_final"), sem("mx_turn"), sem("mx_flat"),
            sem("mx_stored"))
        listed = [k["list"][n].rearrange("(w p q) f -> w p q f", p=P, q=CAP) for n in range(2)]
        PER = 5
        block = ctx.enter_context(nc.Block())

        @block.sync
        def _(eng):
            def body(w, ck, q, b, visit):
                eng.wait_ge(turns[b], 2 * visit)
                for n in range(2):
                    eng.dma_start(meta[b][:, n, :, :], listed[n][bass.ds(ck, 1), :, :, SCORE:SRC].squeeze(0))\
                       .then_inc(loaded[b], 16)
            window_chunks(eng, s, k, body)
            eng.wait_ge(flat, 1)
            eng.dma_start(k["node_rows"][:, 1, :], turned[0:W, :]).then_inc(stored, 16)
            eng.wait_ge(stored, 16)

        @block.vector
        def _(eng):
            ch = Chain(eng, own_dve)
            ch.link(eng.memset(best[:, :], -BIG))

            def body(w, ck, q, b, visit):
                ch.n = 1 + q * PER
                ch.link(eng.tensor_scalar(names[:, :], c["row1"][:, :], k["first_node"][:, bass.ds(w, 1)], None,
                                          ALU.add))
                eng.wait_ge(loaded[b], 32 * (visit + 1))
                eng.wait_ge(turns[b], 2 * visit)
                for n in range(2):
                    tiles = masked[b][:, n, :, :]
                    ch.link(eng.tensor_tensor(tiles, names[:, :].unsqueeze(1).broadcast_to([P, CAP, P]),
                                              meta[b][:, n, :, 1 + n:2 + n].broadcast_to([P, CAP, P]),
                                              ALU.not_equal))
                    eng.scalar_tensor_tensor(tiles, tiles, -BIG, meta[b][:, n, :, 0:1].broadcast_to([P, CAP, P]),
                                             ALU.mult, ALU.add).then_inc(masks, 1)
                for n in range(2):
                    eng.wait_ge(turns[b], 2 * visit + n + 1)
                    for g in range(banks):
                        t = min(4, CAP - 4 * g)
                        eng.tensor_reduce(cand[:, n * banks + g:n * banks + g + 1], psum[g][:, 0:t * P], X,
                                          ALU.max).then_inc(reads, 1)
                eng.wait_ge(reads, banks + 2 * banks * (q + 1))
                ch.link(eng.tensor_reduce(new_best[:, :], cand[:, :], X, ALU.max))
                now = best[:, bass.ds(w, 1)]
                ch.link(eng.tensor_tensor(now, now, new_best[:, :], ALU.max))
            window_chunks(eng, s, k, body)
            eng.drain().then_inc(final, 1)
            eng.wait_ge(turn, 1)
            eng.tensor_copy(turned[0:W, :], pst[0:W, 0:P]).then_inc(flat, 1)

        @block.tensor
        def _(eng):
            eng.sem_inc(reads, banks)

            def body(w, ck, q, b, visit):
                for n in range(2):
                    eng.wait_ge(masks, 2 * q + n + 1)
                    for t in range(CAP):
                        if t % 4 == 0:
                            eng.wait_ge(reads, (2 * q + n) * banks + t // 4 + 1)
                        m = eng.transpose(psum[t // 4][:, (t % 4) * P:(t % 4 + 1) * P], masked[b][:, n, t, :],
                                          c["ident"][:, :])
                    m.then_inc(turns[b], 1)
            window_chunks(eng, s, k, body)
            eng.wait_ge(final, 1)
            eng.transpose(pst[0:W, 0:P], best[:, :], c["ident"][:, :]).then_inc(turn, 1)


def layer_norm(eng, ch, s, t, sq, mean, var, root_sem, ready_sem):
    wide = lambda a: a[:, :].unsqueeze(2).broadcast_to([P, s.W, P])
    ch.link(eng.tensor_reduce(mean[:, :], t[:, :, :], X, ALU.add))
    ch.link(eng.tensor_scalar(mean[:, :], mean[:, :], 1.0 / P, None, ALU.mult))
    ch.link(eng.tensor_tensor(t[:, :, :], t[:, :, :], wide(mean), ALU.subtract))
    ch.link(eng.tensor_tensor(sq[:, :, :], t[:, :, :], t[:, :, :], ALU.mult))
    ch.link(eng.tensor_reduce(var[:, :], sq[:, :, :], X, ALU.add))
    eng.tensor_scalar(var[:, :], var[:, :], 1.0 / P, EPS, ALU.mult, ALU.add).then_inc(ready_sem, 1)
    eng.wait_ge(root_sem, 1)
    ch.link(eng.reciprocal(var[:, :], var[:, :]))
    ch.link(eng.tensor_tensor(t[:, :, :], t[:, :, :], wide(var), ALU.mult))


def nodes_phase(nc, s, c, k, v, x):
    ctx = ExitStack()
    with ctx:
        def sb(name, shape, dt):
            return ctx.enter_context(nc.sbuf_tensor(name, shape, dt))

        def sem(name):
            return ctx.enter_context(nc.semaphore(name))

        W = s.W
        z, other = v["z"], v["z01"]
        mean, var, score = sb("n_mean", [P, W], FP32), sb("n_var", [P, W], FP32), sb("n_score", [P, W], FP32)
        turned = sb("n_turned", [P, P], FP32)
        pst = ctx.enter_context(nc.psum_tensor("n_pst", [P, 512], FP32))
        loaded, own_dve, varied, rooted, scored, turn, flat, stored = (
            sem("no_loaded"), sem("no_dve"), sem("no_varied"), sem("no_rooted"), sem("no_scored"), sem("no_turn"),
            sem("no_flat"), sem("no_stored"))
        wide = lambda a: a[:, :].unsqueeze(2).broadcast_to([P, W, P])
        counts = [0]
        block = ctx.enter_context(nc.Block())

        @block.sync
        def _(eng):
            counts[0] = load_nodes(eng, s, other, x, loaded)
            eng.wait_ge(flat, 1)
            eng.dma_start(k["node_rows"][:, 0, :], turned[0:W, :]).then_inc(stored, 16)
            eng.wait_ge(stored, 16)

        @block.scalar
        def _(eng):
            eng.wait_ge(varied, 1)
            eng.activation(var[:, :], var[:, :], ACT.Sqrt).then_inc(rooted, 1)

        @block.tensor
        def _(eng):
            eng.wait_ge(scored, 1)
            eng.transpose(pst[0:W, 0:P], score[:, :], c["ident"][:, :]).then_inc(turn, 1)

        @block.vector
        def _(eng):
            ch = Chain(eng, own_dve)
            ch.link(eng.tensor_tensor(z[:, :, :], z[:, :, :], wide(k["root"]), ALU.mult))
            ch.link(eng.tensor_scalar(z[:, :, :], z[:, :, :], k["unscale"][:, 0:1], 0.0, ALU.mult, ALU.max))
            eng.wait_ge(loaded, counts[0])
            ch.link(eng.tensor_tensor(z[:, :, :], z[:, :, :], other[:, :, :], ALU.add))
            layer_norm(eng, ch, s, z, other, mean, var, rooted, varied)
            ch.link(eng.tensor_tensor(other[:, :, :], z[:, :, :],
                                      c["wn"][:, :].unsqueeze(1).broadcast_to([P, W, P]), ALU.mult))
            ch.link(eng.tensor_reduce(score[:, :], other[:, :, :], X, ALU.add))
            eng.tensor_scalar(score[:, :], score[:, :], c["b"][:, 0:1], None, ALU.add).then_inc(scored, 1)
            eng.wait_ge(turn, 1)
            eng.tensor_copy(turned[0:W, :], pst[0:W, 0:P]).then_inc(flat, 1)


def attention_phase(nc, s, c, k, v):
    ctx = ExitStack()
    with ctx:
        def sb(name, shape, dt):
            return ctx.enter_context(nc.sbuf_tensor(name, shape, dt))

        def sem(name):
            return ctx.enter_context(nc.semaphore(name))

        W, CAP = s.W, s.CAP
        T = 2 * CAP
        acc = v["acc"]
        rows = [sb(f"t_rows{b}", [P, 2, CAP, ROW], FP32) for b in range(2)]
        tables = [sb(f"t_tables{b}", [P, 2, P], FP32) for b in range(2)]
        weights = sb("t_weights", [P, 2, CAP, P], FP32)
        waste = sb("t_waste", [P, 2, P], FP32)
        names = sb("t_names", [P, P], FP32)
        names_p = sb("t_names_p", [P, P], FP32)
        own = [sb(f"t_own{b}", [P, 2, CAP], FP32) for b in range(2)]
        top = [sb(f"t_top{b}", [P, 2, CAP], FP32) for b in range(2)]
        score = [sb(f"t_score{b}", [P, 2, CAP], FP32) for b in range(2)]
        weight = [sb(f"t_weight{b}", [P, 2, CAP], FP32) for b in range(2)]
        sums = [sb(f"t_sums{b}", [P, P + 1], FP32) for b in range(2)]
        psum = [ctx.enter_context(nc.psum_tensor(f"t_ps{b}", [P, 512], FP32)) for b in range(2)]
        loaded = [sem(f"at_loaded{b}") for b in range(2)]
        summed = [sem(f"at_summed{b}") for b in range(2)]
        own_dve, gathered, scored, weighed, hot, read, added, begun, named, blank = (
            sem("at_dve"), sem("at_gathered"), sem("at_scored"), sem("at_weighed"), sem("at_hot"), sem("at_read"),
            sem("at_added"), sem("at_begun"), sem("at_named"), sem("at_blank"))
        listed = [k["list"][n].rearrange("(w p q) f -> w p (q f)", p=P, q=CAP) for n in range(2)]
        PER = 6
        block = ctx.enter_context(nc.Block())

        @block.sync
        def _(eng):
            def body(w, ck, q, b, visit):
                eng.wait_ge(summed[b], visit)
                for n in range(2):
                    eng.dma_start(rows[b][:, n, :, :].rearrange("p q f -> p (q f)"),
                                  listed[n][bass.ds(ck, 1), :, :].squeeze(0)).then_inc(loaded[b], 16)
                eng.dma_start(tables[b][:, :, :],
                              k["node_rows"][bass.ds(w, 1), :, :].broadcast_to([P, 2, P])).then_inc(loaded[b], 16)
            window_chunks(eng, s, k, body)

        @block.vector
        def _(eng):
            eng.memset(acc[:, :, :], 0.0).then_inc(blank, 1)
            ch = Chain(eng, own_dve)

            def body(w, ck, q, b, visit):
                ch.n = q * PER
                ch.wait()
                eng.wait_ge(gathered, 2 * T * q)
                ch.link(eng.tensor_scalar(names[:, :], c["row1"][:, :], k["first_node"][:, bass.ds(w, 1)], None,
                                          ALU.add))
                eng.wait_ge(loaded[b], 48 * (visit + 1))
                for t in range(T):
                    n, i = t // CAP, t % CAP
                    for m, into in enumerate((own, top)):
                        if t:
                            eng.wait_ge(gathered, 2 * (T * q + t - 1) + m + 1)
                        eng.scalar_tensor_tensor(waste[:, m, :], names[:, :], rows[b][:, n, i, DST1 + n:DST1 + n + 1],
                                                 tables[b][:, m, :], ALU.is_equal, ALU.mult,
                                                 accum_out=into[b][:, n, i:i + 1]).then_inc(gathered, 1)
                eng.wait_ge(gathered, 2 * T * (q + 1))
                edge = rows[b][:, :, :, SCORE]
                ch.add(eng.tensor_tensor(score[b][:, :, :], own[b][:, :, :], edge, ALU.add))
                ch.link(eng.tensor_tensor(top[b][:, :, :], own[b][:, :, :], top[b][:, :, :], ALU.add))
                ch.add(eng.scalar_tensor_tensor(score[b][:, :, :], score[b][:, :, :], SLOPE, score[b][:, :, :],
                                                ALU.mult, ALU.max))
                ch.link(eng.scalar_tensor_tensor(top[b][:, :, :], top[b][:, :, :], SLOPE, top[b][:, :, :],
                                                 ALU.mult, ALU.max))
                ch.link(eng.tensor_tensor(score[b][:, :, :], score[b][:, :, :], top[b][:, :, :], ALU.subtract))
                eng.tensor_scalar(score[b][:, :, :], score[b][:, :, :], 0.0, None, ALU.min).then_inc(scored, 1)
                eng.wait_ge(scored, q + 1)
            window_chunks(eng, s, k, body)

        @block.scalar
        def _(eng):
            def body(w, ck, q, b, visit):
                eng.wait_ge(scored, q + 1)
                eng.activation(weight[b][:, :, :], score[b][:, :, :], ACT.Exp).then_inc(weighed, 1)
                eng.wait_ge(summed[b], visit + 1)
                eng.copy(sums[b][:, :], psum[b][:, 0:P + 1]).then_inc(read, 1)
            window_chunks(eng, s, k, body)

        @block.gpsimd
        def _(eng):
            eng.wait_ge(blank, 1)

            def body(w, ck, q, b, visit):
                eng.wait_ge(hot, T * q)
                eng.sem_inc(begun, 1)
                eng.tensor_tensor(names_p[:, :], c["row1"][:, :],
                                  k["first_node"][:, bass.ds(w, 1)].broadcast_to([P, P]), ALU.add).then_inc(named, 1)
                eng.wait_ge(named, q + 1)
                eng.wait_ge(weighed, q + 1)
                eng.sem_inc(begun, 1)
                for t in range(T):
                    n, i = t // CAP, t % CAP
                    eng.tensor_scalar(weights[:, n, i, :], names_p[:, :], rows[b][:, n, i, DST1 + n:DST1 + n + 1],
                                      weight[b][:, n, i:i + 1], ALU.is_equal, ALU.mult).then_inc(hot, 1)
                eng.wait_ge(read, q + 1)
                eng.wait_ge(added, q)
                eng.sem_inc(begun, 1)
                now = acc[:, bass.ds(w, 1), :].squeeze(1)
                eng.tensor_tensor(now, now, sums[b][:, :], ALU.add).then_inc(added, 1)
            window_chunks(eng, s, k, body)

        @block.tensor
        def _(eng):
            def body(w, ck, q, b, visit):
                for t in range(T):
                    n, i = t // CAP, t % CAP
                    eng.wait_ge(hot, T * q + t + 1)
                    m = eng.matmul(psum[b][:, 0:P + 1], weights[:, n, i, :], rows[b][:, n, i, 0:P + 1],
                                   start=t == 0, stop=t == T - 1)
                m.then_inc(summed[b], 1)
            window_chunks(eng, s, k, body)


def output_phase(nc, s, c, k, v, out):
    ctx = ExitStack()
    with ctx:
        def sb(name, shape, dt):
            return ctx.enter_context(nc.sbuf_tensor(name, shape, dt))

        def sem(name):
            return ctx.enter_context(nc.semaphore(name))

        W = s.W
        x1, acc, t = v["z"], v["acc"], v["z01"]
        mean, var = sb("o_mean", [P, W], FP32), sb("o_var", [P, W], FP32)
        none, some, inv = sb("o_none", [P, W], FP32), sb("o_some", [P, W], FP32), sb("o_inv", [P, W], FP32)
        own_dve, ready, gelu, varied, rooted, normed, stored = (
            sem("ou_dve"), sem("ou_ready"), sem("ou_gelu"), sem("ou_varied"), sem("ou_rooted"), sem("ou_normed"),
            sem("ou_stored"))
        wide = lambda a: a[:, :].unsqueeze(2).broadcast_to([P, W, P])
        block = ctx.enter_context(nc.Block())

        @block.vector
        def _(eng):
            ch = Chain(eng, own_dve)
            total = acc[:, :, P]
            ch.link(eng.tensor_scalar(some[:, :], total, 0.0, None, ALU.is_gt))
            ch.link(eng.tensor_scalar(none[:, :], some[:, :], -1.0, 1.0, ALU.mult, ALU.add))
            ch.link(eng.tensor_tensor(inv[:, :], total, none[:, :], ALU.add))
            ch.link(eng.reciprocal(inv[:, :], inv[:, :]))
            eng.tensor_tensor(t[:, :, :], acc[:, :, 0:P], wide(inv), ALU.mult).then_inc(ready, 1)
            eng.wait_ge(gelu, 1)
            ch.link(eng.tensor_scalar(none[:, :], none[:, :], 1.0, None, ALU.add))
            ch.link(eng.tensor_tensor(x1[:, :, :], x1[:, :, :], wide(none), ALU.mult))
            ch.link(eng.tensor_tensor(t[:, :, :], t[:, :, :], x1[:, :, :], ALU.add))
            layer_norm(eng, ch, s, t, x1, mean, var, rooted, varied)
            eng.drain().then_inc(normed, 1)

        @block.scalar
        def _(eng):
            eng.wait_ge(ready, 1)
            eng.activation(t[:, :, :], t[:, :, :], ACT.Gelu).then_inc(gelu, 1)
            eng.wait_ge(varied, 1)
            eng.activation(var[:, :], var[:, :], ACT.Sqrt).then_inc(rooted, 1)

        @block.sync
        def _(eng):
            eng.wait_ge(normed, 1)
            full, rest = s.nodes // P, s.nodes % P
            eng.dma_start(out[0:full * P, :].rearrange("(w p) f -> p w f", p=P), t[:, 0:full, :]).then_inc(stored, 16)
            if rest:
                eng.dma_start(out[full * P:s.nodes, :], t[0:rest, full, :]).then_inc(stored, 16)
            eng.wait_ge(stored, 32 if rest else 16)


def gnn_kernel(nc, x, src, dst, edge_rows, att_w, att_b, out):
    s = Shapes(x.shape[0], src.shape[0])
    ctx = ExitStack()
    with ctx:
        def sb(name, shape, dt):
            return ctx.enter_context(nc.sbuf_tensor(name, shape, dt))

        c, k = constants(nc, sb, s), kept(nc, sb, s)
        slots_phase(nc, s, c, k, src, dst, att_w, att_b)
        scatter_phase(nc, s, c, k, edge_rows)
        adjacency_phase(nc, s, c, k)
        maxima_phase(nc, s, c, k)
        v = {"z": sb("v_z", [P, s.W, P], FP32), "z01": sb("v_z01", [P, s.W, P], FP32)}
        with ExitStack() as dense:
            v["pieces"] = [dense.enter_context(nc.sbuf_tensor(f"v_pieces{n}", [P, s.W, 2 * P], FP16))
                           for n in range(2)]
            prepare_phase(nc, s, c, k, v, x)
            appnp_phase(nc, s, c, k, v)
        nodes_phase(nc, s, c, k, v, x)
        v["acc"] = sb("v_acc", [P, s.W, P + 1], FP32)
        attention_phase(nc, s, c, k, v)
        output_phase(nc, s, c, k, v, out)


_INS = ["x", "src", "dst", "edge_attr_128", "L1_gnn_W_att_w", "L1_gnn_W_att_b"]


def kernel(**inputs):
    import numpy as _np
    import concourse.bacc as _bacc
    from concourse import mybir as _mybir
    from concourse.bass_utils import run_bass_kernel_spmd as _run

    nc = _bacc.Bacc("TRN2", target_bir_lowering=False, num_devices=1)
    arrays, args = {}, []
    for name in _INS:
        a = _np.ascontiguousarray(inputs[name])
        arrays[f"in_{name}_dram"] = a
        args.append(nc.dram_tensor(f"in_{name}_dram", a.shape, _mybir.dt.from_np(a.dtype), kind="ExternalInput").ap())
    shape = inputs["x"].shape
    args.append(nc.dram_tensor("out_dram", shape, _mybir.dt.float32, kind="ExternalOutput").ap())
    gnn_kernel(nc, *args)
    r = _run(nc, [arrays], core_ids=[0])
    return r.results[0]["out_dram"]
```

```python
import concourse.bass as bass
from concourse import mybir
from contextlib import ExitStack, contextmanager

P = 128
FINE = 8
KEY_ROWS = 3
SRC_BITS = 13
MOST_EQUAL = 15.0
STEPS = 10
ALPHA = 0.1
SLOPE = 0.2
EPS = 1e-5
BIG = 1e30
ONE, SCORE, DST1, SRC1, SRC = 128, 129, 130, 131, 132
ROW = 133

FP32, FP16, BF16 = mybir.dt.float32, mybir.dt.float16, mybir.dt.bfloat16
FP8, I32, U32, U16, U8 = mybir.dt.float8e4, mybir.dt.int32, mybir.dt.uint32, mybir.dt.uint16, mybir.dt.uint8
ALU = mybir.AluOpType
ACT = mybir.ActivationFunctionType
X = mybir.AxisListType.X
XY = mybir.AxisListType.XY


class Shapes:

    def __init__(self, n_nodes, n_edges):
        self.nodes, self.edges = n_nodes, n_edges
        self.EP = max(p for p in range(1, P + 1) if n_edges % p == 0)
        self.ET = n_edges // self.EP
        self.CH = max(c for c in range(1, 26) if self.ET % (2 * c) == 0)
        self.W = -(-n_nodes // P)
        mean = n_edges * P / n_nodes
        self.CAP = int(-(-(mean + 5 * mean ** 0.5) // P))
        self.WS = self.CAP * P
        assert self.W * self.WS >= n_edges and n_nodes < 1 << SRC_BITS
        self.FW = self.W * P // FINE
        self.FG = -(-self.FW // P)
        self.W8 = 8 * self.FG
        self.KR = n_edges // P + KEY_ROWS
        self.FC = FINE * self.W
        self.PAD = self.W * P


class Chain:

    def __init__(self, eng, sem):
        self.eng, self.sem, self.n = eng, sem, 0

    def add(self, ins):
        ins.then_inc(self.sem, 1)
        self.n = self.n + 1

    def wait(self):
        self.eng.wait_ge(self.sem, self.n)

    def link(self, ins):
        self.add(ins)
        self.wait()

    @contextmanager
    def loop(self, trips, per):
        start = self.n
        with self.eng.Fori(0, trips) as i:
            self.n = start + i * per
            counted = Counted(self, per)
            yield i
            counted.check()
        self.n = start + trips * per


class Counted:
    def __init__(self, chain, per):
        self.chain, self.per, self.calls = chain, per, 0
        self.add = chain.add
        chain.add = self.counting

    def counting(self, ins):
        self.calls += 1
        self.add(ins)

    def check(self):
        del self.chain.add
        assert self.calls == self.per, (self.calls, self.per)


def scratch(nc, name, shape, dtype):
    return nc.dram_tensor(name, shape, dtype)


def constants(nc, sb, s):
    c = {}
    c["row"] = sb("c_row", [P, P], FP32)
    c["row1"] = sb("c_row1", [P, P], FP32)
    c["col"] = sb("c_col", [P, 1], FP32)
    c["ident"] = sb("c_ident", [P, P], FP32)
    c["ident16"] = sb("c_ident16", [P, P], FP16)
    c["ones"] = sb("c_ones", [P, P], FP32)
    c["before"] = sb("c_before", [P, P], FP32)
    c["we"] = sb("c_we", [P, P], FP32)
    c["wn"] = sb("c_wn", [P, P], FP32)
    c["b"] = sb("c_b", [P, 1], FP32)
    return c


def slots_phase(nc, s, c, k, src, dst, att_w, att_b):
    ctx = ExitStack()
    with ctx:
        def sb(name, shape, dt):
            return ctx.enter_context(nc.sbuf_tensor(name, shape, dt))

        def sem(name):
            return ctx.enter_context(nc.semaphore(name))

        EP, ET, W = s.EP, s.ET, s.W
        ends = [sb("end_dst", [EP, ET + 1], I32), sb("end_src", [EP, ET + 1], I32)]
        window = [sb("win_dst", [EP, ET], FP16), sb("win_src", [EP, ET], FP16)]
        low = sb("low_dst", [EP, ET], FP16)
        tmp_i = sb("tmp_i", [EP, ET], I32)
        same = sb("same", [EP, ET], BF16)
        ones_e = sb("ones_e", [EP, ET], BF16)
        count = sb("count", [EP, ET], FP32)
        slot = [sb("slot_d", [EP, ET], FP32), sb("slot_s", [EP, ET], FP32)]
        own = sb("own_order", [EP, ET], FP32)
        tail = sb("tail_keys", [1, s.KR * P - s.edges], I32)
        key = sb("keys", [EP, ET], I32)
        total = [sb("tot_d", [P, W], FP32), sb("tot_s", [P, W], FP32)]
        accum = sb("accum", [P, 1], FP32)
        first = [sb("first_d", [P, W], FP32), sb("first_s", [P, W], FP32)]
        wins = [sb("wins_d", [P, W], FP32), sb("wins_s", [P, W], FP32)]
        winbase = sb("winbase", [P, W], FP32)
        onesw = sb("onesw", [P, s.W8], FP32)
        wstart = sb("wstart", [P, W + 1], FP32)
        most = sb("most", [P, 8], FP32)
        hot_lo = sb("hot_lo", [EP, 2, s.CH, P], FP16)
        hot_hi = sb("hot_hi", [EP, 2, s.CH, W], FP16)
        r8 = sb("row8", [P, P], FP32)
        below = sb("below", [P, P], FP32)
        group = sb("group", [P, P], FP32)
        wrow = sb("wrow", [P, s.W8], FP32)
        q16i = sb("q16i", [P, 1], I32)
        q16 = sb("q16", [P, 1], FP32)
        mask8 = sb("mask8", [P, s.W8], FP32)
        at8 = sb("at8", [P, s.W8], FP32)
        start8 = sb("start8", [P, s.FG], FP32)
        start8i = sb("start8i", [P, s.FG], I32)
        row8i = sb("row8i", [P, s.FG], I32)
        rowf = sb("rowf", [P, s.FG], FP32)
        c8 = sb("c8", [P, W], FP32)
        row16 = sb("row16", [P, P], FP16)
        wrow16 = sb("wrow16", [P, W], FP16)
        ps_deg = ctx.enter_context(nc.psum_tensor("ps_deg", [P, 512], FP32))
        ps = [ctx.enter_context(nc.psum_tensor(f"ps_tot{i}", [P, 512], FP32)) for i in range(4)]

        loaded, consts, own_dve, hots, hist, summed, totals = (
            sem("sl_loaded"), sem("sl_consts"), sem("sl_dve"), sem("sl_hots"), sem("sl_hist"),
            sem("sl_summed"), sem("sl_totals"))
        stored, keyed, degs = sem("sl_stored"), sem("sl_keyed"), sem("sl_degs")
        memd = sem("sl_memd")
        zeros = sb("zeros", [P, s.CAP * ROW], FP32)
        blank, zeroed = sem("sl_blank"), sem("sl_zeroed")
        lists = [k["list"][n].rearrange("(w p q) f -> w p (q f)", p=P, q=s.CAP) for n in range(2)]
        block = ctx.enter_context(nc.Block())

        @block.scalar
        def _(eng):
            eng.wait_ge(blank, 1)
            with eng.Fori(0, W) as w:
                for n in range(2):
                    eng.dma_start(lists[n][bass.ds(w, 1), :, :].squeeze(0), zeros[:, :]).then_inc(zeroed, 16)
            eng.wait_ge(zeroed, 16 * 2 * W)

        @block.sync
        def _(eng):
            eng.wait_ge(memd, 1)
            d = dst.rearrange("(p t) -> p t", t=ET)
            eng.dma_start(ends[0][:, 0:ET], d).then_inc(loaded, 16)
            eng.dma_start(ends[0][0:EP - 1, ET:ET + 1], d[1:EP, 0:1], allow_slow_non_contiguous=True).then_inc(loaded, 16)
            eng.dma_start(ends[1][:, 0:ET], src.rearrange("(p t) -> p t", t=ET)).then_inc(loaded, 16)
            w2 = att_w.rearrange("(a n) -> a n", a=2)
            eng.dma_start(c["wn"][:, :], w2[0:1, :].broadcast_to([P, P])).then_inc(loaded, 16)
            eng.dma_start(c["we"][:, :], w2[1:2, :].broadcast_to([P, P])).then_inc(loaded, 16)
            eng.dma_start(c["b"][:, :], att_b.rearrange("(a n) -> a n", a=1).broadcast_to([P, 1])).then_inc(loaded, 16)
            eng.wait_ge(keyed, 1)
            flat = k["keys"].rearrange("r c -> (r c)")
            eng.dma_start(flat[0:s.edges].rearrange("(p t) -> p t", t=ET), key[:, :]).then_inc(stored, 16)
            eng.dma_start(flat[s.edges:s.KR * P].rearrange("(a n) -> a n", a=1), tail[:, :]).then_inc(stored, 16)
            eng.wait_ge(stored, 32)

        @block.gpsimd
        def _(eng):
            def iota(out, pattern, base, mult):
                eng.iota(out, pattern, base=base, channel_multiplier=mult,
                         allow_small_or_imprecise_dtypes=True).then_inc(consts, 1)
            iota(c["row"][:, :], [[1, P]], 0, 0)
            iota(c["row1"][:, :], [[1, P]], 1, 0)
            iota(c["col"][:, :], [[0, 1]], 0, 1)
            iota(own[:, :], [[1, ET]], 0, ET)
            iota(winbase[:, :], [[s.WS, W]], -1, 0)
            iota(r8[:, :], [[0, P // 16], [FINE, 16]], 0, 0)
            iota(wrow[:, :], [[0, s.FG], [1, 8]], 0, 0)
            iota(q16i[:, :], [[0, 1]], 0, 1)
            iota(row16[:, :], [[1, P]], 0, 0)
            iota(wrow16[:, :], [[1, W]], 0, 0)
            iota(k["base8"][:, :], [[FINE * P, s.FG]], 0, FINE)
            iota(k["first_node"][:, :], [[P, W]], 0, 0)
            iota(k["wcol"][:, :], [[1, W]], 0, 0)

        N_CONSTS = 13

        @block.vector
        def _(eng):
            ch = Chain(eng, own_dve)
            eng.memset(ends[0][:, ET:ET + 1], 1 << SRC_BITS).then_inc(memd, 1)
            eng.memset(k["spare_row"][:, :], 0)
            eng.memset(zeros[:, :], 0.0).then_inc(blank, 1)
            ch.add(eng.memset(c["ones"][:, :], 1.0))
            ch.add(eng.memset(ones_e[:, :], 1.0))
            ch.add(eng.memset(k["flags"][:, :], 0.0))
            for n in range(2):
                ch.add(eng.memset(slot[n][:, :], 0.0))
            ch.add(eng.memset(onesw[:, :], 1.0))
            ch.add(eng.memset(tail[:, :], (1 << SRC_BITS) - 1 << SRC_BITS))
            for t in total:
                ch.add(eng.memset(t[:, :], 0.0))
            ch.add(eng.memset(most[:, :], 0.0))
            ch.add(eng.memset(c8[:, :], 0.0))
            ch.add(eng.memset(at8[:, :], 0.0))
            eng.wait_ge(consts, N_CONSTS)
            ch.add(eng.tensor_scalar(c["ident"][:, :], c["row"][:, :], c["col"][:, 0:1], None, ALU.is_equal))
            ch.add(eng.tensor_scalar(c["ident16"][:, :], c["row"][:, :], c["col"][:, 0:1], None, ALU.is_equal))
            ch.add(eng.tensor_scalar(c["before"][:, :], c["row"][:, :], c["col"][:, 0:1], None, ALU.is_gt))
            ch.add(eng.tensor_scalar(below[:, :], r8[:, :], c["col"][:, 0:1], None, ALU.is_gt))
            ch.add(eng.tensor_scalar(group[:, :], r8[:, :], float(FINE), c["col"][:, 0:1], ALU.add, ALU.is_gt))
            ch.link(eng.tensor_scalar(q16i[:, :], q16i[:, :], 4, None, ALU.logical_shift_right))
            ch.add(eng.tensor_tensor(group[:, :], group[:, :], below[:, :], ALU.subtract))
            ch.link(eng.tensor_copy(q16[:, :], q16i[:, :]))
            ch.add(eng.tensor_scalar(mask8[:, :], wrow[:, :], q16[:, 0:1], None, ALU.is_equal))
            eng.wait_ge(loaded, 16 * 6)
            for n in range(2):
                ch.link(eng.tensor_scalar(tmp_i[:, :], ends[n][:, 0:ET], 7, None, ALU.logical_shift_right))
                ch.link(eng.tensor_copy(window[n][:, :], tmp_i[:, :]))
                ch.add(eng.tensor_scalar(k["end1"][n][:, :], ends[n][:, 0:ET], 1.0, None, ALU.add))
            ch.link(eng.tensor_scalar(tmp_i[:, :], ends[0][:, 0:ET], P - 1, None, ALU.bitwise_and))
            ch.add(eng.tensor_copy(low[:, :], tmp_i[:, :]))
            ch.add(eng.tensor_copy(k["src_i"][:, :], ends[1][:, 0:ET]))
            ch.link(eng.tensor_scalar(key[:, :], ends[0][:, 0:ET], SRC_BITS, None, ALU.logical_shift_left))
            eng.tensor_tensor(key[:, :], key[:, :], ends[1][:, 0:ET], ALU.bitwise_or).then_inc(keyed, 1)
            ch.link(eng.tensor_tensor(count[:, :], ends[0][:, 0:ET], ends[0][:, 1:ET + 1], ALU.is_gt))
            ch.link(eng.tensor_reduce(most[0:EP, 0:1], count[:, :], X, ALU.add))

            for n in range(2):
                with ch.loop(W, 2) as h:
                    ch.link(eng.tensor_scalar(same[:, :], window[n][:, :], k["wcol"][0:EP, bass.ds(h, 1)], 0.0,
                                              ALU.is_equal, ALU.add, accum_out=accum[0:EP, :]))
                    ch.link(eng.tensor_copy(total[n][0:EP, bass.ds(h, 1)], accum[0:EP, :]))
            eng.drain().then_inc(totals, 1)

            n_ch = ET // (2 * s.CH)
            with ch.loop(n_ch, 0) as i:
                for b in range(2):
                    eng.wait_ge(hist, i * 2 + b + 1)
                    cols = slice(None), bass.ds((i * 2 + b) * s.CH, s.CH)
                    eng.tensor_tensor(hot_lo[:, b, :, :], row16[0:EP, :].unsqueeze(1).broadcast_to([EP, s.CH, P]),
                                      low[cols].unsqueeze(2).broadcast_to([EP, s.CH, P]),
                                      ALU.is_equal).then_inc(hots, 1)
                    eng.tensor_tensor(hot_hi[:, b, :, :], wrow16[0:EP, :].unsqueeze(1).broadcast_to([EP, s.CH, W]),
                                      window[0][cols].unsqueeze(2).broadcast_to([EP, s.CH, W]),
                                      ALU.is_equal).then_inc(hots, 1)

            eng.wait_ge(summed, 2)
            for n in range(2):
                ch.add(eng.tensor_tensor(first[n][:, :], ps[0][:, n * W:(n + 1) * W], winbase[:, :], ALU.add))
                ch.add(eng.tensor_copy(wins[n][:, :], ps[1][:, n * W:(n + 1) * W]))
            ch.link(eng.memset(wstart[:, 0:1], 0.0))
            ch.add(eng.tensor_scalar(k["flags"][:, 2:3], ps[2][:, 0:1], 0.0, None, ALU.is_equal))
            for n in range(2):
                ch.add(eng.tensor_reduce(most[:, 2 + n:3 + n], wins[n][:, :], X, ALU.max))
            ch.link(eng.tensor_tensor_scan(wstart[:, 1:W + 1], onesw[:, 0:W], wins[0][:, :], 0.0, ALU.mult, ALU.add))
            ch.link(eng.tensor_tensor(most[:, 4:5], most[:, 2:3], most[:, 3:4], ALU.max))
            ch.link(eng.tensor_scalar(k["flags"][:, 0:1], most[:, 4:5], float(s.WS), None, ALU.is_le))

            for n in range(2):
                with ch.loop(W, 4) as h:
                    ch.link(eng.tensor_scalar(same[:, :], window[n][:, :], k["wcol"][0:EP, bass.ds(h, 1)], None,
                                              ALU.is_equal))
                    ch.link(eng.tensor_tensor_scan(count[:, :], ones_e[:, :], same[:, :],
                                                   first[n][0:EP, bass.ds(h, 1)], ALU.mult, ALU.add))
                    ch.link(eng.tensor_tensor(count[:, :], count[:, :], same[:, :], ALU.mult))
                    ch.link(eng.tensor_tensor(slot[n][:, :], slot[n][:, :], count[:, :], ALU.add))
                ch.link(eng.tensor_tensor(slot[n][:, :], slot[n][:, :], own[:, :], ALU.subtract))
                ch.link(eng.scalar_tensor_tensor(k["slot"][n][:, :], slot[n][:, :], k["flags"][0:EP, 0:1],
                                                 own[:, :], ALU.mult, ALU.add))

            eng.wait_ge(hist, 2 * n_ch + 2)
            ch.add(eng.tensor_scalar(k["deg"][:, :], ps_deg[:, 0:W], 1.0, None, ALU.add))
            eng.tensor_copy(k["deg0"][:, :], ps_deg[:, 0:W]).then_inc(degs, 1)
            eng.wait_ge(summed, 3)
            ch.link(eng.tensor_tensor(at8[:, 0:W], ps[3][:, 0:W], wstart[:, 0:W], ALU.add))
            ch.link(eng.tensor_tensor(at8[:, :], at8[:, :], mask8[:, :], ALU.mult))
            ch.link(eng.tensor_reduce(start8[:, :], at8[:, :].rearrange("p (g w) -> p g w", w=8), X, ALU.add))
            ch.link(eng.tensor_copy(start8i[:, :], start8[:, :]))
            ch.link(eng.tensor_scalar(row8i[:, :], start8i[:, :], 7, None, ALU.logical_shift_right))
            ch.link(eng.tensor_copy(rowf[:, :], row8i[:, :]))
            for r in range(KEY_ROWS):
                ch.add(eng.tensor_scalar(k["keyrow"][:, r, :], rowf[:, :], float(r), None, ALU.add))
            ch.link(eng.tensor_copy(c8[:, :], ps[3][:, W:2 * W]))
            ch.link(eng.tensor_reduce(k["most8"][:, :], c8[:, :], X, ALU.max))

        @block.tensor
        def _(eng):
            eng.sem_inc(hist, 2)
            eng.wait_ge(totals, 1)
            for n in range(2):
                eng.matmul(ps[0][:, n * W:(n + 1) * W], c["before"][:, :], total[n][:, :], start=True, stop=True)
                eng.matmul(ps[1][:, n * W:(n + 1) * W], c["ones"][:, :], total[n][:, :], start=True, stop=True)
            eng.matmul(ps[2][:, 0:1], c["ones"][:, :], most[:, 0:1], start=True, stop=True).then_inc(summed, 2)
            n_ch = ET // (2 * s.CH)

            def chunk(b, n, first, last):
                eng.wait_ge(hots, 2 * n + 2)
                for t in range(s.CH):
                    m = eng.matmul(ps_deg[:, 0:W], hot_lo[:, b, t, :], hot_hi[:, b, t, :],
                                   start=first and t == 0, stop=last and t == s.CH - 1)
                m.then_inc(hist, 1)
            chunk(0, 0, True, False)
            chunk(1, 1, False, n_ch == 1)
            if n_ch > 1:
                if n_ch > 2:
                    with eng.Fori(1, n_ch - 1) as i:
                        chunk(0, i * 2, False, False)
                        chunk(1, i * 2 + 1, False, False)
                chunk(0, 2 * n_ch - 2, False, False)
                chunk(1, 2 * n_ch - 1, False, True)
            eng.wait_ge(degs, 1)
            eng.matmul(ps[3][:, 0:W], below[:, :], k["deg0"][:, :], start=True, stop=True)
            eng.matmul(ps[3][:, W:2 * W], group[:, :], k["deg0"][:, :], start=True, stop=True).then_inc(summed, 1)


def credit(eng, k, row, sem):
    eng.dma_start(k["spare"][row:row + 1, :], k["spare_row"][0:1, :]).then_inc(sem, 16)


def kept(nc, sb, s):
    k = {}
    k["wcol"] = sb("k_wcol", [P, s.W], FP32)
    k["base8"] = sb("k_base8", [P, s.FG], FP32)
    k["deg"] = sb("k_deg", [P, s.W], FP32)
    k["deg0"] = sb("k_deg0", [P, s.W], FP32)
    k["keyrow"] = sb("k_keyrow", [P, KEY_ROWS, s.FG], I32)
    k["most8"] = sb("k_most8", [P, 1], FP32)
    k["flags"] = sb("k_flags", [P, 4], FP32)
    k["list"] = [scratch(nc, f"edge_list_{n}", [s.W * s.WS, ROW], FP32).ap() for n in ("dst", "src")]
    k["root"] = sb("k_root", [P, s.W], FP32)
    k["keep"] = sb("k_keep", [P, s.W], FP32)
    k["unscale"] = sb("k_unscale", [P, 1], FP32)
    k["first_node"] = sb("k_first_node", [P, s.W], FP32)
    k["node_rows"] = scratch(nc, "node_rows", [s.W, 2, P], FP32).ap()
    k["z_rows"] = scratch(nc, "z_rows", [s.PAD, P], FP32).ap()
    k["adj"] = scratch(nc, "adjacency", [s.W, P, s.W * P // 4], U32).ap()
    k["lift"] = sb("k_lift", [P, 1], FP32)
    k["spare"] = scratch(nc, "spare", [4, 16], I32).ap()
    k["spare_row"] = sb("k_spare", [1, 16], I32)
    k["dense"] = sb("k_dense", [P, 1], I32)
    k["by_window"] = sb("k_by_window", [P, 1], I32)
    k["keys"] = scratch(nc, "edge_keys", [s.KR, P], I32).ap()
    return k


def of_edges(nc, sb, s, k):
    k["slot"] = [sb("k_slot_d", [s.EP, s.ET], I32), sb("k_slot_s", [s.EP, s.ET], I32)]
    k["end1"] = [sb("k_dst1", [s.EP, s.ET], FP32), sb("k_src1", [s.EP, s.ET], FP32)]
    k["src_i"] = sb("k_src_i", [s.EP, s.ET], I32)


def adjacency_phase(nc, s, c, k):
    ctx = ExitStack()
    with ctx:
        def sb(name, shape, dt):
            return ctx.enter_context(nc.sbuf_tensor(name, shape, dt))

        def sem(name):
            return ctx.enter_context(nc.semaphore(name))

        W, FG, FC, R = s.W, s.FG, s.FC, KEY_ROWS
        RING = 4
        G = P // FINE
        NK = FG * R * P
        key = sb("a_key", [P, FG, R, P], I32)
        tmp = sb("a_tmp", [P, FG, R, P], I32)
        lowf = sb("a_lowf", [P, FG, R, P], FP32)
        node = sb("a_node", [P, FG, R, P], FP32)
        column = sb("a_column", [P, FG, R, P], FP32)
        inside = sb("a_inside", [P, FG, R, P], FP32)
        turned = [sb(f"a_turned{n}", [P, R, FG * P], FP32) for n in range(2)]
        hot_low = sb("a_hot_low", [P, RING, R, P], FP16)
        hot_col = sb("a_hot_col", [P, RING, R, FC], FP16)
        cols = sb("a_cols", [P, FC], FP16)
        row16 = sb("a_row16", [P, P], FP16)
        out8 = [sb(f"a_out{b}", [P, W, P], FP8) for b in range(2)]
        part = [sb(f"a_part{b}", [P, G], FP32) for b in range(2)]
        sums = sb("a_sums", [P, W * G], FP32)
        most = sb("a_most", [P, 4], FP32)
        allmost = sb("a_allmost", [P, 4], FP32)
        flat = lambda t: t[:, :, :, :].rearrange("p g r e -> p (g r e)")
        psum = [ctx.enter_context(nc.psum_tensor(f"a_ps{i}", [P, 512], FP32)) for i in range(RING)]
        pst = [ctx.enter_context(nc.psum_tensor(f"a_pst{i}", [P, 512], FP32)) for i in range(2)]

        gathered, consts, own_dve, ready, turn, copied = (
            sem("ad_gathered"), sem("ad_consts"), sem("ad_dve"), sem("ad_ready"), sem("ad_turn"), sem("ad_copied"))
        begun = sem("ad_begun")
        hot, built, evicted, summed, most_ready, most_all = (
            sem("ad_hot"), sem("ad_built"), sem("ad_evicted"), sem("ad_summed"), sem("ad_most"), sem("ad_most_all"))
        stored = [sem(f"ad_stored{b}") for b in range(2)]
        turns = [(g, r, n) for g in range(FG) for r in range(R) for n in range(2)]
        block = ctx.enter_context(nc.Block())

        def windows(eng, body):
            if W > 1:
                with eng.Fori(0, W // 2) as i:
                    for b in range(2):
                        body(2 * i + b, b, i)
            if W % 2:
                body(W - 1, 0, W // 2)

        @block.gpsimd
        def _(eng):
            eng.iota(cols[:, :], [[1, FC]], base=0, channel_multiplier=0,
                     allow_small_or_imprecise_dtypes=True).then_inc(consts, 1)
            eng.iota(row16[:, :], [[1, P]], base=0, channel_multiplier=0,
                     allow_small_or_imprecise_dtypes=True).then_inc(consts, 1)
            for g in range(FG):
                for r in range(R):
                    eng.indirect_dma_start(
                        key[:, g, r, :], None, k["keys"],
                        bass.IndirectOffsetOnAxis(ap=k["keyrow"][:, r, g:g + 1], axis=0)).then_inc(gathered, 16)
            eng.wait_ge(most_ready, 1)
            eng.partition_all_reduce(allmost[:, :], most[:, :], P, bass.bass_isa.ReduceOp.max).then_inc(most_all, 1)

        @block.vector
        def _(eng):
            ch = Chain(eng, own_dve)
            ch.add(eng.memset(most[:, :], 0.0))
            eng.wait_ge(gathered, 16 * FG * R)
            ch.link(eng.tensor_scalar(flat(tmp), flat(key), SRC_BITS, None, ALU.logical_shift_right))
            ch.add(eng.tensor_copy(flat(node), flat(tmp)))
            ch.link(eng.tensor_scalar(flat(key), flat(key), (1 << SRC_BITS) - 1, None, ALU.bitwise_and))
            ch.link(eng.tensor_scalar(flat(tmp), flat(key), P - 1, None, ALU.bitwise_and))
            eng.tensor_copy(flat(lowf), flat(tmp)).then_inc(ready, 1)
            ch.link(eng.tensor_scalar(flat(key), flat(key), 7, None, ALU.logical_shift_right))
            eng.wait_ge(ready, 1)
            ch.add(eng.tensor_copy(flat(column), flat(key)))
            for g in range(FG):
                ch.add(eng.tensor_scalar(node[:, g, :, :], node[:, g, :, :], k["base8"][:, g:g + 1], None,
                                         ALU.subtract))
            ch.wait()
            ch.add(eng.tensor_scalar(flat(inside), flat(node), 0.0, None, ALU.is_ge))
            ch.link(eng.scalar_tensor_tensor(flat(column), flat(column), float(FINE), flat(node), ALU.mult, ALU.add))
            ch.link(eng.scalar_tensor_tensor(flat(inside), flat(node), float(FINE - 1), flat(inside),
                                             ALU.is_le, ALU.mult))
            ch.link(eng.tensor_scalar(flat(inside), flat(inside), -1024.0, 1024.0, ALU.mult, ALU.add))
            eng.tensor_tensor(flat(column), flat(column), flat(inside), ALU.add).then_inc(ready, 1)
            eng.wait_ge(consts, 2)
            eng.wait_ge(copied, 2 + len(turns))

            def body(j, b, visit):
                for g in range(G):
                    n = j * G + g
                    r0 = g % RING
                    eng.wait_ge(built, n + 1)
                    for r in range(R):
                        eng.tensor_scalar(hot_low[:, r0, r, :], row16[:, :], turned[0][:, r, bass.ds(n, 1)], None,
                                          ALU.is_equal)
                        ins = eng.tensor_scalar(hot_col[:, r0, r, :], cols[:, :], turned[1][:, r, bass.ds(n, 1)],
                                                None, ALU.is_equal)
                    ins.then_inc(hot, 1)
            windows(eng, body)
            eng.wait_ge(summed, W)
            ch.add(eng.tensor_reduce(most[:, 0:1], sums[:, :], X, ALU.max))
            eng.tensor_copy(most[:, 1:2], k["most8"][:, :]).then_inc(most_ready, 1)
            eng.wait_ge(most_all, 1)
            ch.link(eng.tensor_scalar(most[:, 2:3], allmost[:, 0:1], MOST_EQUAL, None, ALU.is_le))
            ch.link(eng.tensor_scalar(most[:, 3:4], allmost[:, 1:2], float((R - 1) * P), None, ALU.is_le))
            ch.link(eng.tensor_tensor(most[:, 2:3], most[:, 2:3], most[:, 3:4], ALU.mult))
            ch.link(eng.tensor_tensor(most[:, 2:3], most[:, 2:3], k["flags"][:, 2:3], ALU.mult))
            ch.link(eng.tensor_copy(k["dense"][:, :], most[:, 2:3]))
            ch.link(eng.tensor_copy(k["by_window"][:, :], k["flags"][:, 0:1]))

        @block.tensor
        def _(eng):
            eng.sem_inc(built, RING)
            eng.wait_ge(ready, 2)
            for i, (g, r, n) in enumerate(turns):
                eng.wait_ge(copied, i + 1)
                eng.transpose(pst[i % 2][:, 0:P], (lowf, column)[n][:, g, r, :], c["ident"][:, :]).then_inc(turn, 1)

            def body(j, b, visit):
                for g in range(G):
                    n = j * G + g
                    eng.wait_ge(hot, n + 1)
                    eng.wait_ge(evicted, n + 1)
                    for r in range(R):
                        m = eng.matmul(psum[g % RING][:, 0:FC], hot_low[:, g % RING, r, :], hot_col[:, g % RING, r, :],
                                       start=r == 0, stop=r == R - 1)
                    m.then_inc(built, 1)
            windows(eng, body)

        @block.scalar
        def _(eng):
            eng.sem_inc(copied, 2)
            for i, (g, r, n) in enumerate(turns):
                eng.wait_ge(turn, i + 1)
                eng.copy(turned[n][:, r, g * P:(g + 1) * P], pst[i % 2][:, 0:P]).then_inc(copied, 1)
            eng.sem_inc(evicted, RING)

            def body(j, b, visit):
                eng.wait_ge(stored[b], 16 * visit)
                eng.wait_ge(summed, j)
                for g in range(G):
                    n = j * G + g
                    eng.wait_ge(built, RING + n + 1)
                    eng.sem_inc(begun, 1)
                    eng.activation(out8[b][:, :, FINE * g:FINE * (g + 1)],
                                   psum[g % RING][:, 0:FC].rearrange("p (w f) -> p w f", f=FINE), ACT.Copy,
                                   accum_out=part[b][:, g:g + 1], saturate=False).then_inc(evicted, 1)
                eng.wait_ge(evicted, RING + (j + 1) * G)
                eng.copy(sums[:, bass.ds(j * G, G)], part[b][:, :]).then_inc(summed, 1)
            windows(eng, body)

        @block.sync
        def _(eng):
            def body(j, b, visit):
                eng.wait_ge(evicted, RING + (j + 1) * G)
                eng.dma_start(k["adj"][bass.ds(j, 1), :, :].squeeze(0),
                              out8[b][:, :, :].rearrange("p w n -> p (w n)").bitcast(U32)).then_inc(stored[b], 16)
            windows(eng, body)
            for b in range(2):
                eng.wait_ge(stored[b], 16 * ((W + 1 - b) // 2))




def load_nodes(eng, s, tile, x, done):
    full, rest = s.nodes // P, s.nodes % P
    eng.dma_start(tile[:, 0:full, :], x[0:full * P, :].rearrange("(w p) f -> p w f", p=P)).then_inc(done, 16)
    if rest:
        eng.dma_start(tile[0:rest, full, :], x[full * P:s.nodes, :]).then_inc(done, 16)
    return 32 if rest else 16


def prepare_phase(nc, s, c, k, v, x):
    ctx = ExitStack()
    with ctx:
        def sb(name, shape, dt):
            return ctx.enter_context(nc.sbuf_tensor(name, shape, dt))

        def sem(name):
            return ctx.enter_context(nc.semaphore(name))

        W = s.W
        inv_root = sb("p_inv_root", [P, W], FP32)
        most = sb("p_most", [P, 1], FP32)
        power = sb("p_power", [P, 1], FP32)
        scale = sb("p_scale", [P, 1], FP32)
        blank, loaded, rooted, own_dve, part, whole = (
            sem("pr_blank"), sem("pr_loaded"), sem("pr_rooted"), sem("pr_dve"), sem("pr_part"), sem("pr_whole"))
        z, z01, pieces = v["z"], v["z01"], v["pieces"][0]
        wide = lambda t: t[:, :].unsqueeze(2).broadcast_to([P, W, P])
        counts = [0]
        block = ctx.enter_context(nc.Block())

        @block.sync
        def _(eng):
            eng.wait_ge(blank, 1)
            counts[0] = load_nodes(eng, s, z, x, loaded)

        @block.scalar
        def _(eng):
            eng.activation(k["root"][:, :], k["deg"][:, :], ACT.Sqrt).then_inc(rooted, 1)

        @block.gpsimd
        def _(eng):
            eng.wait_ge(part, 1)
            eng.partition_all_reduce(power[:, :], most[:, :], P, bass.bass_isa.ReduceOp.max).then_inc(whole, 1)

        @block.vector
        def _(eng):
            ch = Chain(eng, own_dve)
            eng.memset(z[:, W - 1, :], 0.0).then_inc(blank, 1)
            ch.link(eng.reciprocal(k["keep"][:, :], k["deg"][:, :]))
            ch.add(eng.tensor_scalar(k["keep"][:, :], k["keep"][:, :], 1.0 - ALPHA, None, ALU.mult))
            eng.wait_ge(rooted, 1)
            ch.link(eng.reciprocal(inv_root[:, :], k["root"][:, :]))
            eng.wait_ge(loaded, counts[0])
            ch.link(eng.tensor_tensor(z[:, :, :], z[:, :, :], wide(inv_root), ALU.mult))
            eng.tensor_reduce(most[:, :], z[:, :, :], XY, ALU.max, apply_absolute_value=True).then_inc(part, 1)
            eng.wait_ge(whole, 1)
            bits, sbits = power[:, :].bitcast(I32), scale[:, :].bitcast(I32)
            ch.link(eng.tensor_scalar(bits, bits, 0x7F800000, None, ALU.bitwise_and))
            ch.link(eng.tensor_scalar(bits, bits, float(16 << 23), None, ALU.max))
            ch.link(eng.tensor_scalar(sbits, bits, -1.0, float((127 + 127 + 14) << 23), ALU.mult, ALU.add))
            ch.add(eng.tensor_scalar(k["unscale"][:, :].bitcast(I32), sbits, -1.0, float((127 + 127) << 23),
                                     ALU.mult, ALU.add))
            ch.link(eng.tensor_scalar(z[:, :, :], z[:, :, :], scale[:, 0:1], None, ALU.mult))
            ch.add(eng.tensor_scalar(z01[:, :, :], z[:, :, :], ALPHA, None, ALU.mult))
            ch.link(eng.tensor_copy(pieces[:, :, 0:P], z[:, :, :]))
            ch.link(eng.tensor_tensor(pieces[:, :, P:2 * P], z[:, :, :], pieces[:, :, 0:P], ALU.subtract))


def appnp_phase(nc, s, c, k, v, edge_rows):
    ctx = ExitStack()
    with ctx:
        def sb(name, shape, dt):
            return ctx.enter_context(nc.sbuf_tensor(name, shape, dt))

        def sem(name):
            return ctx.enter_context(nc.semaphore(name))

        W, CAP = s.W, s.CAP
        NB = max([b for b in range(3, 8) if W % b == 0] or [4])
        visits = [W // NB + (b < W % NB) for b in range(NB)]
        z, z01, pieces = v["z"], v["z01"], v["pieces"]
        matrix = [sb(f"matrix{b}", [P, W, P], FP8) for b in range(NB)]
        part = [sb(f"z_part{b}", [P, P], FP32) for b in range(NB)]
        psum = [ctx.enter_context(nc.psum_tensor(f"z_ps{b}", [P, 512], FP32)) for b in range(NB)]
        loaded = [sem(f"ap_loaded{b}") for b in range(NB)]
        summed = [sem(f"ap_summed{b}") for b in range(NB)]
        added = [sem(f"ap_added{b}") for b in range(NB)]
        scaled, own_dve, updated = sem("ap_scaled"), sem("ap_dve"), sem("ap_updated")
        meta = sb("g_meta", [P, CAP, 3], FP32)
        gathered = sb("g_gathered", [P, CAP, P], FP32)
        hot = sb("g_hot", [P, CAP, P], FP32)
        names = sb("g_names", [P, P], FP32)
        acc = sb("g_acc", [P, P], FP32)
        psg = ctx.enter_context(nc.psum_tensor("g_ps", [P, 512], FP32))
        EP, rounds = s.EP, W // NB
        ES = s.ET // STEPS
        CHUNKS = rounds // 2 * 2 + 1
        stride = ES // CHUNKS
        last = ES - stride * (CHUNKS - 1)
        assert s.ET % STEPS == 0 and stride > 0
        stage = [sb(f"stage{b}", [EP, last, ROW], FP32) for b in range(2)]
        place = [sb(f"place{b}", [EP, 2, last], I32) for b in range(2)]
        product = sb("product", [EP, last, P], FP32)
        most = sb("most_score", [P, 1], FP32)
        chunk_most = sb("chunk_most", [EP, 1], FP32)
        all_most = sb("all_most_score", [P, 1], FP32)
        begun_p, freed = sem("sc_begun_p"), sem("sc_freed")
        most_ready, most_all, stage_dve, filled, begun, ones_set = (
            sem("sc_most"), sem("sc_most_all"), sem("sc_dve"), sem("sc_filled"), sem("sc_begun"), sem("sc_ones"))
        fetched = [sem(f"sc_fetched{b}") for b in range(2)]
        scattered = sem("sc_scattered")
        edges = edge_rows.rearrange("(p t) f -> p t f", t=s.ET)
        g_saved, g_meta, g_rows, g_hot, g_sum, g_used, g_done, g_own, g_begun = (
            sem("ge_saved"), sem("ge_meta"), sem("ge_rows"), sem("ge_hot"), sem("ge_sum"), sem("ge_used"),
            sem("ge_done"), sem("ge_own"), sem("ge_begun"))
        block = ctx.enter_context(nc.Block())

        def is_dense(eng):
            return eng.value_load(k["dense"][0:1, 0:1], min_val=0, max_val=1) == 1

        def which_chunk(pair, par, half, u):
            step, i, n = pair * 2 + par, half * 2 + u, par * CHUNKS + u
            return step * CHUNKS + i, step * ES + i * stride, n % 2, pair * CHUNKS + half + n // 2

        def steps(eng, body, chunk=None):
            with eng.Fori(0, STEPS // 2) as pair:
                for par in range(2):
                    step = pair * 2 + par

                    def one_chunk(half, u, size):
                        if chunk:
                            chunk(*which_chunk(pair, par, half, u), size)

                    def nb_windows(i):
                        for b in range(NB):
                            body(step, par, i * NB + b, b, step * visits[b] + i)
                    if rounds > 1:
                        with eng.Fori(0, rounds // 2) as half:
                            for u in range(2):
                                one_chunk(half, u, stride)
                                nb_windows(half * 2 + u)
                    one_chunk(CHUNKS // 2, 0, last)
                    if rounds % 2:
                        nb_windows(rounds - 1)
                    for b in range(W % NB):
                        body(step, par, W - W % NB + b, b, step * visits[b] + rounds)

        def edge_chunks(eng, chunk):
            with eng.Fori(0, STEPS // 2) as pair:
                for par in range(2):
                    if CHUNKS > 1:
                        with eng.Fori(0, CHUNKS // 2) as half:
                            for u in range(2):
                                chunk(*which_chunk(pair, par, half, u), stride)
                    chunk(*which_chunk(pair, par, CHUNKS // 2, 0), last)

        def fetch(eng, n, first, b, visit, size):
            eng.wait_ge(freed, n + 1)
            eng.dma_start(stage[b][:, 0:size, 0:P], edges[:, bass.ds(first, size), :]).then_inc(fetched[b], 16)

        def fill(eng, n, first, b, visit, size):
            cols = slice(None), bass.ds(first, size)
            now = stage[b][:, 0:size, :]
            ch = Chain(eng, stage_dve)
            ch.n = n * 3 + 1
            ch.wait()
            eng.wait_ge(freed, n + 1)
            eng.sem_inc(begun, 1)
            for side in range(2):
                eng.tensor_copy(place[b][:, side, 0:size], k["slot"][side][cols])
                eng.tensor_copy(now[:, :, DST1 + side], k["end1"][side][cols])
            eng.tensor_copy(now[:, :, SRC].bitcast(I32), k["src_i"][cols])
            eng.wait_ge(fetched[b], 16 * (visit + 1))
            ch.link(eng.tensor_tensor(product[:, 0:size, :], now[:, :, 0:P],
                                      c["we"][0:EP, :].unsqueeze(1).broadcast_to([EP, size, P]), ALU.mult))
            eng.tensor_reduce(now[:, :, SCORE], product[:, 0:size, :], X, ALU.add).then_inc(filled, 1)
            eng.wait_ge(filled, n + 1)
            ch.link(eng.tensor_reduce(chunk_most[:, :], now[:, :, SCORE], X, ALU.max, apply_absolute_value=True))
            ch.add(eng.tensor_tensor(most[0:EP, :], most[0:EP, :], chunk_most[:, :], ALU.max))

        def scatter(eng, n, first, b, visit, size):
            eng.wait_ge(filled, n + 1)
            eng.sem_inc(begun_p, 1)
            for e in range(size):
                for side in range(2):
                    eng.indirect_dma_start(
                        k["list"][side], bass.IndirectOffsetOnAxis(ap=place[b][:, side, e:e + 1], axis=0),
                        stage[b][:, e, :], None).then_inc(scattered, 16)
            eng.wait_ge(scattered, 2 * 16 * (first + size))
            eng.sem_inc(freed, 1)

        def chunks(eng, body, step_start=lambda step: None):
            with eng.Fori(0, STEPS) as step:
                step_start(step)
                with eng.Fori(0, W) as w:
                    with eng.Fori(0, W) as ck:
                        body(step, ck, (step * W + w) * W + ck)

        @block.sync
        def _(eng):
            with eng.If(is_dense(eng)):
                def body(step, par, j, b, visit):
                    eng.wait_ge(summed[b], visit + 1)
                    eng.dma_start(matrix[b][:, :, :].rearrange("p w n -> p (w n)").bitcast(U32),
                                  k["adj"][bass.ds(j, 1), :, :].squeeze(0)).then_inc(loaded[b], 16)
                steps(eng, body, lambda *chunk: fetch(eng, *chunk))
            with eng.Else():
                edge_chunks(eng, lambda *chunk: fetch(eng, *chunk))
                eng.wait_ge(freed, 2 + STEPS * CHUNKS)
                listed = k["list"][0].rearrange("(w p q) f -> w p q f", p=P, q=CAP)

                def step_start(step):
                    eng.wait_ge(g_done, step * W + 1)
                    eng.dma_start(k["z_rows"].rearrange("(w p) f -> p w f", p=P), z[:, :, :]).then_inc(g_saved, 16)

                def body(step, ck, q):
                    eng.wait_ge(g_saved, 16 * (step + 1))
                    eng.wait_ge(g_used, q + 1)
                    eng.dma_start(meta[:, :, :], listed[bass.ds(ck, 1), :, :, DST1:SRC + 1].squeeze(0))\
                       .then_inc(g_meta, 16)
                chunks(eng, body, step_start)

        @block.gpsimd
        def _(eng):
            eng.sem_inc(freed, 2)
            edge_chunks(eng, lambda *chunk: scatter(eng, *chunk))
            with eng.If(is_dense(eng)):
                eng.drain()
            with eng.Else():
                def body(step, ck, q):
                    eng.wait_ge(g_meta, 16 * (q + 1))
                    eng.sem_inc(g_begun, 1)
                    for t in range(CAP):
                        eng.indirect_dma_start(gathered[:, t, :], None, k["z_rows"], bass.IndirectOffsetOnAxis(
                            ap=meta[:, t, 2:3].bitcast(I32), axis=0)).then_inc(g_rows, 16)
                chunks(eng, body)
                eng.wait_ge(g_rows, 16 * CAP * STEPS * W * W)
            eng.wait_ge(most_ready, 1)
            eng.partition_all_reduce(all_most[:, :], most[:, :], P, bass.bass_isa.ReduceOp.max).then_inc(most_all, 1)

        @block.tensor
        def _(eng):
            eng.sem_inc(updated, 1)
            for b in range(NB):
                eng.sem_inc(summed[b], 1)
                eng.sem_inc(added[b], 1)
            with eng.If(is_dense(eng)):
                def body(step, par, j, b, visit):
                    eng.wait_ge(updated, step * W + 1)
                    eng.wait_ge(loaded[b], 16 * (visit + 1))
                    eng.wait_ge(added[b], visit + 1)
                    out = psum[b][:, 0:2 * P]
                    eng.matmul(out, c["ident16"][:, :], pieces[par][:, bass.ds(j, 1), :].squeeze(1),
                               start=True, stop=False)
                    for w in range(W):
                        m = eng.matmul(out, matrix[b][:, w, :], pieces[par][:, w, :], start=False, stop=w == W - 1)
                    m.then_inc(summed[b], 1)
                steps(eng, body)
            with eng.Else():
                def body(step, ck, q):
                    eng.wait_ge(g_hot, q + 1)
                    eng.wait_ge(g_rows, 16 * CAP * (q + 1))
                    for t in range(CAP):
                        m = eng.matmul(psg[:, 0:P], hot[:, t, :], gathered[:, t, :], start=t == 0, stop=t == CAP - 1)
                    m.then_inc(g_sum, 1)
                chunks(eng, body)

        @block.scalar
        def _(eng):
            with eng.If(is_dense(eng)):
                def body(step, par, j, b, visit):
                    eng.wait_ge(summed[b], visit + 2)
                    eng.wait_ge(added[b], visit + 1)
                    eng.activation(part[b][:, :], psum[b][:, P:2 * P], ACT.Copy,
                                   scale=k["keep"][:, bass.ds(j, 1)]).then_inc(scaled, 1)
                steps(eng, body)
            with eng.Else():
                eng.drain()

        @block.vector
        def _(eng):
            eng.memset(most[:, :], 0.0).then_inc(stage_dve, 1)
            for b in range(2):
                eng.memset(stage[b][:, :, ONE:ONE + 1], 1.0)
            eng.sem_inc(own_dve, 1)
            with eng.If(is_dense(eng)):
                def body(step, par, j, b, visit):
                    n = step * W + j
                    now = z[:, bass.ds(j, 1), :].squeeze(1)
                    new = pieces[1 - par][:, bass.ds(j, 1), :].squeeze(1)
                    eng.wait_ge(scaled, n + 1)
                    eng.scalar_tensor_tensor(now, psum[b][:, 0:P], k["keep"][:, bass.ds(j, 1)], part[b][:, :],
                                             ALU.mult, ALU.add).then_inc(added[b], 1)
                    eng.wait_ge(added[b], visit + 2)
                    eng.tensor_tensor(now, now, z01[:, bass.ds(j, 1), :].squeeze(1), ALU.add).then_inc(own_dve, 1)
                    eng.wait_ge(own_dve, 2 * n + 2)
                    eng.tensor_copy(new[:, 0:P], now).then_inc(own_dve, 1)
                    eng.wait_ge(own_dve, 2 * n + 3)
                    eng.tensor_tensor(new[:, P:2 * P], now, new[:, 0:P], ALU.subtract).then_inc(updated, 1)
                steps(eng, body, lambda *chunk: fill(eng, *chunk))
            with eng.Else():
                edge_chunks(eng, lambda *chunk: fill(eng, *chunk))
                for ours in (g_own, g_done, g_used):
                    eng.sem_inc(ours, 1)
                per = 1 + 4 * W
                with eng.Fori(0, STEPS) as step:
                    eng.wait_ge(g_saved, 16 * (step + 1))
                    eng.wait_ge(g_own, step * per + 1)
                    eng.tensor_copy(names[:, :], c["row1"][:, :]).then_inc(g_own, 1)
                    with eng.Fori(0, W) as w:
                        own = step * per + 2 + 4 * w
                        eng.wait_ge(g_own, own)
                        eng.wait_ge(g_done, step * W + w + 1)
                        eng.memset(acc[:, :], 0.0).then_inc(g_own, 1)
                        with eng.Fori(0, W) as ck:
                            q = (step * W + w) * W + ck
                            eng.wait_ge(g_own, own + 1)
                            eng.wait_ge(g_meta, 16 * (q + 1))
                            eng.tensor_tensor(hot[:, :, :], names[:, :].unsqueeze(1).broadcast_to([P, CAP, P]),
                                              meta[:, :, 0:1].broadcast_to([P, CAP, P]),
                                              ALU.is_equal).then_inc(g_hot, 1)
                            eng.wait_ge(g_sum, q + 1)
                            eng.wait_ge(g_used, q + 1)
                            eng.tensor_tensor(acc[:, :], acc[:, :], psg[:, 0:P], ALU.add).then_inc(g_used, 1)
                        now = z[:, bass.ds(w, 1), :].squeeze(1)
                        eng.wait_ge(g_used, (step * W + w + 1) * W + 1)
                        eng.tensor_tensor(acc[:, :], acc[:, :], now, ALU.add).then_inc(g_own, 1)
                        eng.wait_ge(g_own, own + 2)
                        eng.tensor_scalar(acc[:, :], acc[:, :], k["keep"][:, bass.ds(w, 1)], None,
                                          ALU.mult).then_inc(g_own, 1)
                        eng.tensor_scalar(names[:, :], names[:, :], float(P), None, ALU.add).then_inc(g_own, 1)
                        eng.wait_ge(g_own, own + 4)
                        eng.tensor_tensor(now, acc[:, :], z01[:, bass.ds(w, 1), :].squeeze(1),
                                          ALU.add).then_inc(g_done, 1)
                    eng.wait_ge(g_done, (step + 1) * W + 1)
            eng.drain().then_inc(most_ready, 1)
            eng.wait_ge(most_all, 1)
            eng.tensor_scalar(k["lift"][:, :], all_most[:, :], 2.0, 1.0, ALU.mult, ALU.add)


def ring(eng, trips, body):
    if trips > 1:
        with eng.Fori(0, trips // 2) as i:
            for b in range(2):
                body(2 * i + b, b, i)
    if trips % 2:
        body(trips - 1, 0, trips // 2)


def window_chunks(eng, s, k, body):
    with eng.If(eng.value_load(k["by_window"][0:1, 0:1], min_val=0, max_val=1) == 0):
        with eng.Fori(0, s.W) as w:
            ring(eng, s.W, lambda ck, b, i: body(w, ck, w * s.W + ck, b, w * ((s.W + 1 - b) // 2) + i))
    with eng.Else():
        eng.drain()


def maxima_phase(nc, s, c, k):
    ctx = ExitStack()
    with ctx:
        def sb(name, shape, dt):
            return ctx.enter_context(nc.sbuf_tensor(name, shape, dt))

        def sem(name):
            return ctx.enter_context(nc.semaphore(name))

        W, CAP = s.W, s.CAP
        banks = -(-CAP // 4)
        meta = [sb(f"m_meta{b}", [P, 2, CAP, 3], FP32) for b in range(2)]
        masked = [sb(f"m_masked{b}", [P, 2, CAP, P], FP32) for b in range(2)]
        names = sb("m_names", [P, P], FP32)
        best = sb("m_best", [P, W], FP32)
        new_best = sb("m_new_best", [P, 1], FP32)
        cand = sb("m_cand", [P, 2 * banks], FP32)
        turned = sb("m_turned", [P, P], FP32)
        psum = [ctx.enter_context(nc.psum_tensor(f"m_ps{i}", [P, 512], FP32)) for i in range(banks)]
        pst = ctx.enter_context(nc.psum_tensor("m_pst", [P, 512], FP32))
        loaded = [sem(f"mx_loaded{b}") for b in range(2)]
        turns = [sem(f"mx_turns{b}") for b in range(2)]
        masks, reads, own_dve, final, turn, flat, stored = (
            sem("mx_masks"), sem("mx_reads"), sem("mx_dve"), sem("mx_final"), sem("mx_turn"), sem("mx_flat"),
            sem("mx_stored"))
        listed = [k["list"][n].rearrange("(w p q) f -> w p q f", p=P, q=CAP) for n in range(2)]
        PER = 5
        block = ctx.enter_context(nc.Block())

        @block.sync
        def _(eng):
            def body(w, ck, q, b, visit):
                eng.wait_ge(turns[b], 2 * visit)
                for n in range(2):
                    eng.dma_start(meta[b][:, n, :, :], listed[n][bass.ds(ck, 1), :, :, SCORE:SRC].squeeze(0))\
                       .then_inc(loaded[b], 16)
            window_chunks(eng, s, k, body)
            eng.wait_ge(flat, 1)
            eng.dma_start(k["node_rows"][:, 1, :], turned[0:W, :]).then_inc(stored, 16)
            eng.wait_ge(stored, 16)

        @block.vector
        def _(eng):
            ch = Chain(eng, own_dve)
            ch.link(eng.memset(best[:, :], -BIG))

            def body(w, ck, q, b, visit):
                ch.n = 1 + q * PER
                ch.link(eng.tensor_scalar(names[:, :], c["row1"][:, :], k["first_node"][:, bass.ds(w, 1)], None,
                                          ALU.add))
                eng.wait_ge(loaded[b], 32 * (visit + 1))
                eng.wait_ge(turns[b], 2 * visit)
                for n in range(2):
                    tiles = masked[b][:, n, :, :]
                    ch.link(eng.tensor_tensor(tiles, names[:, :].unsqueeze(1).broadcast_to([P, CAP, P]),
                                              meta[b][:, n, :, 1 + n:2 + n].broadcast_to([P, CAP, P]),
                                              ALU.not_equal))
                    eng.scalar_tensor_tensor(tiles, tiles, -BIG, meta[b][:, n, :, 0:1].broadcast_to([P, CAP, P]),
                                             ALU.mult, ALU.add).then_inc(masks, 1)
                for n in range(2):
                    eng.wait_ge(turns[b], 2 * visit + n + 1)
                    for g in range(banks):
                        t = min(4, CAP - 4 * g)
                        eng.tensor_reduce(cand[:, n * banks + g:n * banks + g + 1], psum[g][:, 0:t * P], X,
                                          ALU.max).then_inc(reads, 1)
                eng.wait_ge(reads, banks + 2 * banks * (q + 1))
                ch.link(eng.tensor_reduce(new_best[:, :], cand[:, :], X, ALU.max))
                now = best[:, bass.ds(w, 1)]
                ch.link(eng.tensor_tensor(now, now, new_best[:, :], ALU.max))
            window_chunks(eng, s, k, body)
            eng.drain().then_inc(final, 1)
            eng.wait_ge(turn, 1)
            eng.tensor_copy(turned[0:W, :], pst[0:W, 0:P]).then_inc(flat, 1)

        @block.tensor
        def _(eng):
            eng.sem_inc(reads, banks)

            def body(w, ck, q, b, visit):
                for n in range(2):
                    eng.wait_ge(masks, 2 * q + n + 1)
                    for t in range(CAP):
                        if t % 4 == 0:
                            eng.wait_ge(reads, (2 * q + n) * banks + t // 4 + 1)
                        m = eng.transpose(psum[t // 4][:, (t % 4) * P:(t % 4 + 1) * P], masked[b][:, n, t, :],
                                          c["ident"][:, :])
                    m.then_inc(turns[b], 1)
            window_chunks(eng, s, k, body)
            eng.wait_ge(final, 1)
            eng.transpose(pst[0:W, 0:P], best[:, :], c["ident"][:, :]).then_inc(turn, 1)


def layer_norm(eng, ch, s, t, sq, mean, var, root_sem, ready_sem):
    wide = lambda a: a[:, :].unsqueeze(2).broadcast_to([P, s.W, P])
    ch.link(eng.tensor_reduce(mean[:, :], t[:, :, :], X, ALU.add))
    ch.link(eng.tensor_scalar(mean[:, :], mean[:, :], 1.0 / P, None, ALU.mult))
    ch.link(eng.tensor_tensor(t[:, :, :], t[:, :, :], wide(mean), ALU.subtract))
    ch.link(eng.tensor_tensor(sq[:, :, :], t[:, :, :], t[:, :, :], ALU.mult))
    ch.link(eng.tensor_reduce(var[:, :], sq[:, :, :], X, ALU.add))
    eng.tensor_scalar(var[:, :], var[:, :], 1.0 / P, EPS, ALU.mult, ALU.add).then_inc(ready_sem, 1)
    eng.wait_ge(root_sem, 1)
    ch.link(eng.reciprocal(var[:, :], var[:, :]))
    ch.link(eng.tensor_tensor(t[:, :, :], t[:, :, :], wide(var), ALU.mult))


def nodes_phase(nc, s, c, k, v, x):
    ctx = ExitStack()
    with ctx:
        def sb(name, shape, dt):
            return ctx.enter_context(nc.sbuf_tensor(name, shape, dt))

        def sem(name):
            return ctx.enter_context(nc.semaphore(name))

        W = s.W
        z, other = v["z"], v["z01"]
        mean, var, score = sb("n_mean", [P, W], FP32), sb("n_var", [P, W], FP32), v["score"]
        turned = sb("n_turned", [P, P], FP32)
        pst = ctx.enter_context(nc.psum_tensor("n_pst", [P, 512], FP32))
        loaded, own_dve, varied, rooted, scored, turn, flat, stored = (
            sem("no_loaded"), sem("no_dve"), sem("no_varied"), sem("no_rooted"), sem("no_scored"), sem("no_turn"),
            sem("no_flat"), sem("no_stored"))
        wide = lambda a: a[:, :].unsqueeze(2).broadcast_to([P, W, P])
        counts = [0]
        block = ctx.enter_context(nc.Block())

        @block.sync
        def _(eng):
            counts[0] = load_nodes(eng, s, other, x, loaded)
            eng.wait_ge(flat, 1)
            eng.dma_start(k["node_rows"][:, 0, :], turned[0:W, :]).then_inc(stored, 16)
            eng.wait_ge(stored, 16)

        @block.scalar
        def _(eng):
            eng.wait_ge(varied, 1)
            eng.activation(var[:, :], var[:, :], ACT.Sqrt).then_inc(rooted, 1)

        @block.tensor
        def _(eng):
            eng.wait_ge(scored, 1)
            eng.transpose(pst[0:W, 0:P], score[:, :], c["ident"][:, :]).then_inc(turn, 1)

        @block.vector
        def _(eng):
            ch = Chain(eng, own_dve)
            ch.link(eng.tensor_tensor(z[:, :, :], z[:, :, :], wide(k["root"]), ALU.mult))
            ch.link(eng.tensor_scalar(z[:, :, :], z[:, :, :], k["unscale"][:, 0:1], 0.0, ALU.mult, ALU.max))
            eng.wait_ge(loaded, counts[0])
            ch.link(eng.tensor_tensor(z[:, :, :], z[:, :, :], other[:, :, :], ALU.add))
            layer_norm(eng, ch, s, z, other, mean, var, rooted, varied)
            ch.link(eng.tensor_tensor(other[:, :, :], z[:, :, :],
                                      c["wn"][:, :].unsqueeze(1).broadcast_to([P, W, P]), ALU.mult))
            ch.link(eng.tensor_reduce(score[:, :], other[:, :, :], X, ALU.add))
            eng.tensor_scalar(score[:, :], score[:, :], c["b"][:, 0:1], None, ALU.add).then_inc(scored, 1)
            eng.wait_ge(turn, 1)
            eng.tensor_copy(turned[0:W, :], pst[0:W, 0:P]).then_inc(flat, 1)


def attention_phase(nc, s, c, k, v):
    ctx = ExitStack()
    with ctx:
        def sb(name, shape, dt):
            return ctx.enter_context(nc.sbuf_tensor(name, shape, dt))

        def sem(name):
            return ctx.enter_context(nc.semaphore(name))

        W, CAP = s.W, s.CAP
        T = 2 * CAP
        acc, total = v["z01"], v["total"]
        rows = [sb(f"t_rows{b}", [P, 2, CAP, ROW], FP32) for b in range(2)]
        tables = [sb(f"t_tables{b}", [P, 2, P], FP32) for b in range(2)]
        weights = sb("t_weights", [P, 2, CAP, P], FP32)
        waste = sb("t_waste", [P, 2, P], FP32)
        names = sb("t_names", [P, P], FP32)
        names_p = sb("t_names_p", [P, P], FP32)
        own = [sb(f"t_own{b}", [P, 2, CAP], FP32) for b in range(2)]
        top = [sb(f"t_top{b}", [P, 2, CAP], FP32) for b in range(2)]
        score = [sb(f"t_score{b}", [P, 2, CAP], FP32) for b in range(2)]
        weight = [sb(f"t_weight{b}", [P, 2, CAP], FP32) for b in range(2)]
        sums = [sb(f"t_sums{b}", [P, P + 1], FP32) for b in range(2)]
        psum = [ctx.enter_context(nc.psum_tensor(f"t_ps{b}", [P, 512], FP32)) for b in range(2)]
        loaded = [sem(f"at_loaded{b}") for b in range(2)]
        summed = [sem(f"at_summed{b}") for b in range(2)]
        own_dve, gathered, scored, weighed, hot, read, added, begun, named, blank = (
            sem("at_dve"), sem("at_gathered"), sem("at_scored"), sem("at_weighed"), sem("at_hot"), sem("at_read"),
            sem("at_added"), sem("at_begun"), sem("at_named"), sem("at_blank"))
        listed = [k["list"][n].rearrange("(w p q) f -> w p (q f)", p=P, q=CAP) for n in range(2)]
        PER = 6
        block = ctx.enter_context(nc.Block())

        @block.sync
        def _(eng):
            def body(w, ck, q, b, visit):
                eng.wait_ge(summed[b], visit)
                for n in range(2):
                    eng.dma_start(rows[b][:, n, :, :].rearrange("p q f -> p (q f)"),
                                  listed[n][bass.ds(ck, 1), :, :].squeeze(0)).then_inc(loaded[b], 16)
                eng.dma_start(tables[b][:, :, :],
                              k["node_rows"][bass.ds(w, 1), :, :].broadcast_to([P, 2, P])).then_inc(loaded[b], 16)
            window_chunks(eng, s, k, body)

        @block.vector
        def _(eng):
            ch = Chain(eng, own_dve)

            def body(w, ck, q, b, visit):
                ch.n = q * PER
                ch.wait()
                eng.wait_ge(gathered, 2 * T * q)
                ch.link(eng.tensor_scalar(names[:, :], c["row1"][:, :], k["first_node"][:, bass.ds(w, 1)], None,
                                          ALU.add))
                eng.wait_ge(loaded[b], 48 * (visit + 1))
                for t in range(T):
                    n, i = t // CAP, t % CAP
                    for m, into in enumerate((own, top)):
                        if t:
                            eng.wait_ge(gathered, 2 * (T * q + t - 1) + m + 1)
                        eng.scalar_tensor_tensor(waste[:, m, :], names[:, :], rows[b][:, n, i, DST1 + n:DST1 + n + 1],
                                                 tables[b][:, m, :], ALU.is_equal, ALU.mult,
                                                 accum_out=into[b][:, n, i:i + 1]).then_inc(gathered, 1)
                eng.wait_ge(gathered, 2 * T * (q + 1))
                edge = rows[b][:, :, :, SCORE]
                ch.add(eng.tensor_tensor(score[b][:, :, :], own[b][:, :, :], edge, ALU.add))
                ch.link(eng.tensor_tensor(top[b][:, :, :], own[b][:, :, :], top[b][:, :, :], ALU.add))
                ch.add(eng.scalar_tensor_tensor(score[b][:, :, :], score[b][:, :, :], SLOPE, score[b][:, :, :],
                                                ALU.mult, ALU.max))
                ch.link(eng.scalar_tensor_tensor(top[b][:, :, :], top[b][:, :, :], SLOPE, top[b][:, :, :],
                                                 ALU.mult, ALU.max))
                ch.link(eng.tensor_tensor(score[b][:, :, :], score[b][:, :, :], top[b][:, :, :], ALU.subtract))
                eng.tensor_scalar(score[b][:, :, :], score[b][:, :, :], 0.0, None, ALU.min).then_inc(scored, 1)
                eng.wait_ge(scored, q + 1)
            window_chunks(eng, s, k, body)

        @block.scalar
        def _(eng):
            def body(w, ck, q, b, visit):
                eng.wait_ge(scored, q + 1)
                eng.activation(weight[b][:, :, :], score[b][:, :, :], ACT.Exp).then_inc(weighed, 1)
                eng.wait_ge(summed[b], visit + 1)
                eng.copy(sums[b][:, :], psum[b][:, 0:P + 1]).then_inc(read, 1)
            window_chunks(eng, s, k, body)

        @block.gpsimd
        def _(eng):
            eng.memset(acc[:, :, :], 0.0)
            eng.memset(total[:, :], 0.0).then_inc(blank, 1)
            eng.wait_ge(blank, 1)

            def body(w, ck, q, b, visit):
                eng.wait_ge(hot, T * q)
                eng.sem_inc(begun, 1)
                eng.tensor_tensor(names_p[:, :], c["row1"][:, :],
                                  k["first_node"][:, bass.ds(w, 1)].broadcast_to([P, P]), ALU.add).then_inc(named, 1)
                eng.wait_ge(named, q + 1)
                eng.wait_ge(weighed, q + 1)
                eng.sem_inc(begun, 1)
                for t in range(T):
                    n, i = t // CAP, t % CAP
                    eng.tensor_scalar(weights[:, n, i, :], names_p[:, :], rows[b][:, n, i, DST1 + n:DST1 + n + 1],
                                      weight[b][:, n, i:i + 1], ALU.is_equal, ALU.mult).then_inc(hot, 1)
                eng.wait_ge(read, q + 1)
                eng.wait_ge(added, q)
                eng.sem_inc(begun, 1)
                now, now_total = acc[:, bass.ds(w, 1), :].squeeze(1), total[:, bass.ds(w, 1)]
                eng.tensor_tensor(now, now, sums[b][:, 0:P], ALU.add)
                eng.tensor_tensor(now_total, now_total, sums[b][:, P:P + 1], ALU.add).then_inc(added, 1)
            window_chunks(eng, s, k, body)

        @block.tensor
        def _(eng):
            def body(w, ck, q, b, visit):
                for t in range(T):
                    n, i = t // CAP, t % CAP
                    eng.wait_ge(hot, T * q + t + 1)
                    m = eng.matmul(psum[b][:, 0:P + 1], weights[:, n, i, :], rows[b][:, n, i, 0:P + 1],
                                   start=t == 0, stop=t == T - 1)
                m.then_inc(summed[b], 1)
            window_chunks(eng, s, k, body)


def by_three(eng, start, stop, body):
    rounds = (stop - start) // 3
    if rounds > 1:
        with eng.Fori(0, rounds) as i:
            for r in range(start, start + 3):
                body(i * 3 + r, r % 3, i + r // 3)
        start = start + 3 * rounds
    for w in range(start, stop):
        body(w, w % 3, w // 3)


def after(w, b, visit):
    return w + 1, (b + 1) % 3, visit + (b + 1) // 3


def windows_phase(nc, s, c, k, v):
    ctx = ExitStack()
    with ctx:
        def sb(name, shape, dt):
            return ctx.enter_context(nc.sbuf_tensor(name, shape, dt))

        def sem(name):
            return ctx.enter_context(nc.semaphore(name))

        W, CAP = s.W, s.CAP
        sums, totals = v["z01"], v["total"]
        GROUPS = [(n, t, min(t + 4, CAP)) for n in range(2) for t in range(0, CAP, 4)]
        NG = len(GROUPS)
        rows = [sb(f"w_rows{b}", [P, 2, CAP, ROW], FP32) for b in range(3)]
        hot = [sb(f"w_hot{b}", [P, 2, CAP, P], BF16) for b in range(3)]
        lifted = [sb(f"w_lifted{b}", [P, 2, CAP], FP32) for b in range(3)]
        place = sb("w_place", [P, 2, CAP], BF16)
        hot_turned = sb("w_hot_turned", [P, 2, CAP, P], BF16)
        scores = sb("w_scores", [P, 2, CAP, P], FP32)
        weights = sb("w_weights", [P, 2, CAP, P], FP32)
        cand = sb("w_cand", [P, NG], FP32)
        best = sb("w_best", [P, 1], FP32)
        pair = sb("w_pair", [P, 2], FP32)
        rest = sb("w_rest", [P, 2], FP32)
        pieces = sb("w_pieces", [P, 3, 2], BF16)
        edge_pair = sb("w_edge_pair", [P, 2 * CAP, 2], FP32)
        score = sb("w_score", [P, 2, CAP], FP32)
        weight = sb("w_weight", [P, 2, CAP], FP32)
        rowb = sb("w_row", [P, P], BF16)
        identb = sb("w_ident", [P, P], BF16)
        ps_hot = [ctx.enter_context(nc.psum_tensor(f"w_ps_hot{i}", [P, 512], FP32)) for i in range(2)]
        ps_max = [ctx.enter_context(nc.psum_tensor(f"w_ps_max{i}", [P, 512], FP32)) for i in range(3)]
        ps_pair = ctx.enter_context(nc.psum_tensor("w_ps_pair", [P, 512], FP32))
        ps_sum = ctx.enter_context(nc.psum_tensor("w_ps_sum", [P, 512], FP32))
        loaded = [sem(f"wi_loaded{b}") for b in range(3)]
        own_dve, hots, scored_a, scored_p, hot_turns, hot_copied, max_turns, max_read = (
            sem("wi_dve"), sem("wi_hots"), sem("wi_scored_a"), sem("wi_scored_p"), sem("wi_hot_turns"),
            sem("wi_hot_copied"), sem("wi_max_turns"), sem("wi_max_read"))
        tabled, paired, pair_read, ready, weighed, halves, weighted, copied, consts, begun = (
            sem("wi_tabled"), sem("wi_paired"), sem("wi_pair_read"), sem("wi_ready"), sem("wi_weighed"),
            sem("wi_halves"), sem("wi_weighted"), sem("wi_copied"), sem("wi_consts"), sem("wi_begun"))
        FREE = 6
        listed = [k["list"][n].rearrange("(w p q) f -> w p (q f)", p=P, q=CAP) for n in range(2)]
        block = ctx.enter_context(nc.Block())

        def by_window(eng):
            return eng.value_load(k["by_window"][0:1, 0:1], min_val=0, max_val=1) == 1

        @block.sync
        def _(eng):
            with eng.If(by_window(eng)):
                def body(w, b, visit):
                    eng.wait_ge(halves, 2 * w + 2)
                    for n in range(2):
                        eng.dma_start(rows[b][:, n, :, :].rearrange("p q f -> p (q f)"),
                                      listed[n][bass.ds(w, 1), :, :].squeeze(0)).then_inc(loaded[b], 16)
                by_three(eng, 0, W, body)
            with eng.Else():
                eng.drain()

        @block.vector
        def _(eng):
            with eng.If(by_window(eng)):
                ch = Chain(eng, own_dve)
                ch.add(eng.tensor_copy(rowb[:, :], c["row"][:, :]))
                eng.tensor_copy(identb[:, :], c["ident"][:, :]).then_inc(consts, 1)
                HOT, PAIR, MAX = 2, 2, 8
                PER = HOT + PAIR + MAX

                def one_hot(w, b, visit):
                    eng.wait_ge(loaded[b], 32 * (visit + 1))
                    ch.wait()
                    for n in range(2):
                        ch.add(eng.tensor_scalar(place[:, n, :], rows[b][:, n, :, DST1 + n],
                                                 k["first_node"][:, bass.ds(w, 1)], 1.0, ALU.subtract, ALU.subtract))
                    for n in range(2):
                        eng.tensor_scalar(lifted[b][:, n, :], rows[b][:, n, :, SCORE], k["lift"][:, 0:1], None,
                                          ALU.add)
                    ch.wait()
                    for n in range(2):
                        eng.tensor_tensor(hot[b][:, n, :, :], rowb[:, :].unsqueeze(1).broadcast_to([P, CAP, P]),
                                          place[:, n, :].unsqueeze(2).broadcast_to([P, CAP, P]),
                                          ALU.is_equal).then_inc(hots, 1)

                def maxima(w, b, visit):
                    for g, (n, t, end) in enumerate(GROUPS):
                        eng.wait_ge(max_turns, NG * w + g + 2)
                        eng.tensor_reduce(cand[:, g:g + 1], ps_max[g % 3][:, 0:(end - t) * P], X,
                                          ALU.max).then_inc(max_read, 1)
                    eng.wait_ge(max_read, 3 + NG * (w + 1))
                    ch.add(eng.tensor_copy(pair[:, 0:1], v["score"][:, bass.ds(w, 1)]))
                    ch.link(eng.tensor_reduce(best[:, :], cand[:, :], X, ALU.max))
                    ch.link(eng.tensor_scalar(best[:, :], best[:, :], k["lift"][:, 0:1], pair[:, 0:1],
                                              ALU.subtract, ALU.add))
                    ch.link(eng.scalar_tensor_tensor(pair[:, 1:2], best[:, :], SLOPE, best[:, :], ALU.mult, ALU.max))
                    ch.link(eng.tensor_copy(pieces[:, 0, :], pair[:, :]))
                    ch.link(eng.tensor_tensor(rest[:, :], pair[:, :], pieces[:, 0, :], ALU.subtract))
                    ch.link(eng.tensor_copy(pieces[:, 1, :], rest[:, :]))
                    ch.link(eng.tensor_tensor(rest[:, :], rest[:, :], pieces[:, 1, :], ALU.subtract))
                    eng.tensor_copy(pieces[:, 2, :], rest[:, :]).then_inc(tabled, 1)

                def weigh(w, b, visit):
                    eng.wait_ge(paired, w + 1)
                    eng.tensor_reduce(edge_pair[:, :, :],
                                      ps_pair[:, 0:12 * CAP].rearrange("p (t k a) -> p t a k", k=3, a=2), X,
                                      ALU.add).then_inc(pair_read, 1)
                    eng.wait_ge(pair_read, w + 2)
                    both = edge_pair[:, :, :].rearrange("p (n t) a -> p n t a", n=2)
                    ch.link(eng.tensor_tensor(score[:, :, :], both[:, :, :, 0], rows[b][:, :, :, SCORE], ALU.add))
                    ch.link(eng.scalar_tensor_tensor(score[:, :, :], score[:, :, :], SLOPE, score[:, :, :],
                                                     ALU.mult, ALU.max))
                    eng.tensor_tensor(score[:, :, :], score[:, :, :], both[:, :, :, 1],
                                      ALU.subtract).then_inc(ready, 1)
                    eng.wait_ge(weighed, w + 1)
                    for n in range(2):
                        eng.wait_ge(halves, 2 * (w - 1) + n + 1 + FREE)
                        eng.tensor_tensor(weights[:, n, :, :], hot[b][:, n, :, :],
                                          weight[:, n, :].unsqueeze(2).broadcast_to([P, CAP, P]),
                                          ALU.mult).then_inc(weighted, 1)

                eng.wait_ge(consts, 1)
                one_hot(0, 0, 0)
                maxima(0, 0, 0)
                counted = ch.n

                def body(w, b, visit):
                    ch.n = counted + w * PER
                    one_hot(*after(w, b, visit))
                    weigh(w, b, visit)
                    maxima(*after(w, b, visit))
                by_three(eng, 0, W - 1, body)
                ch.n = counted + (W - 1) * PER
                weigh(W - 1, (W - 1) % 3, (W - 1) // 3)
            with eng.Else():
                eng.drain()

        @block.scalar
        def _(eng):
            with eng.If(by_window(eng)):
                eng.sem_inc(hot_copied, 2)
                eng.sem_inc(copied, 1)

                def spread(w, b, visit):
                    eng.wait_ge(hots, 2 * w + 1)
                    eng.wait_ge(max_turns, NG * w + 1)
                    for g, (n, t, end) in enumerate(GROUPS):
                        for i in range(t, end if n == 0 else t):
                            m = eng.activation(scores[:, n, i, :], hot[b][:, n, i, :], ACT.Copy,
                                               scale=lifted[b][:, n, i:i + 1])
                        if n == 0:
                            m.then_inc(scored_a, 1)
                        eng.wait_ge(hot_turns, NG * w + g + 1)
                        eng.copy(hot_turned[:, n, t:end, :].rearrange("p t n -> p (t n)"),
                                 ps_hot[g % 2][:, 0:(end - t) * P]).then_inc(hot_copied, 1)

                def exponent(w):
                    eng.wait_ge(ready, w + 1)
                    eng.activation(weight[:, :, :], score[:, :, :], ACT.Exp).then_inc(weighed, 1)

                def take_sums(w):
                    eng.wait_ge(halves, 2 * w + 2 + FREE)
                    eng.sem_inc(begun, 1)
                    eng.copy(sums[:, bass.ds(w, 1), :].squeeze(1), ps_sum[:, 0:P])
                    eng.copy(totals[:, bass.ds(w, 1)], ps_sum[:, P:P + 1]).then_inc(copied, 1)

                spread(0, 0, 0)
                exponent(0)
                spread(1, 1, 0)

                def body(w, b, visit):
                    exponent(w)
                    spread(*after(w, b, visit))
                    take_sums(w - 1)
                by_three(eng, 1, W - 1, body)
                exponent(W - 1)
                take_sums(W - 2)
                take_sums(W - 1)
            with eng.Else():
                eng.drain()

        @block.gpsimd
        def _(eng):
            with eng.If(by_window(eng)):
                def body(w, b, visit):
                    eng.wait_ge(hots, 2 * w + 2)
                    eng.wait_ge(max_turns, NG * w + 1)
                    eng.sem_inc(begun, 1)
                    eng.tensor_tensor(scores[:, 1, :, :], hot[b][:, 1, :, :],
                                      lifted[b][:, 1, :].unsqueeze(2).broadcast_to([P, CAP, P]),
                                      ALU.mult).then_inc(scored_p, 1)
                by_three(eng, 0, W, body)
            with eng.Else():
                eng.drain()

        @block.tensor
        def _(eng):
            with eng.If(by_window(eng)):
                eng.wait_ge(consts, 1)
                eng.sem_inc(max_read, 3)
                eng.sem_inc(pair_read, 1)
                eng.sem_inc(halves, FREE)
                eng.sem_inc(max_turns, 1)

                def turn(w, b, visit):
                    for g, (n, t, end) in enumerate(GROUPS):
                        if t == 0:
                            eng.wait_ge(hots, 2 * w + n + 1)
                        eng.wait_ge(hot_copied, NG * w + g + 1)
                        for i in range(t, end):
                            m = eng.matmul(ps_hot[g % 2][:, (i - t) * P:(i - t + 1) * P], hot[b][:, n, i, :],
                                           identb[:, :], start=True, stop=True)
                        m.then_inc(hot_turns, 1)
                        if n == 0:
                            eng.wait_ge(scored_a, NG // 2 * w + g + 1)
                        elif t == 0:
                            eng.wait_ge(scored_p, w + 1)
                        eng.wait_ge(max_read, NG * w + g + 1)
                        for i in range(t, end):
                            m = eng.transpose(ps_max[g % 3][:, (i - t) * P:(i - t + 1) * P], scores[:, n, i, :],
                                              c["ident"][:, :])
                        m.then_inc(max_turns, 1)

                def look_up(w, b, visit):
                    eng.wait_ge(tabled, w + 1)
                    eng.wait_ge(hot_copied, NG * (w + 1) + 2)
                    eng.wait_ge(pair_read, w + 1)
                    for n in range(2):
                        for i in range(CAP):
                            at = 6 * (n * CAP + i)
                            m = eng.matmul(ps_pair[:, at:at + 6], hot_turned[:, n, i, :],
                                           pieces[:, :, :].rearrange("p k a -> p (k a)"), start=True, stop=True)
                    m.then_inc(paired, 1)

                def sum_up(w, b, visit):
                    eng.wait_ge(copied, w + 1)
                    for n in range(2):
                        eng.wait_ge(weighted, 2 * w + n + 1)
                        for i in range(CAP):
                            m = eng.matmul(ps_sum[:, 0:P + 1], weights[:, n, i, :], rows[b][:, n, i, 0:P + 1],
                                           start=n == 0 and i == 0, stop=n == 1 and i == CAP - 1)
                        m.then_inc(halves, 1)

                turn(0, 0, 0)
                look_up(0, 0, 0)

                def body(w, b, visit):
                    turn(*after(w, b, visit))
                    look_up(*after(w, b, visit))
                    sum_up(w, b, visit)
                by_three(eng, 0, W - 1, body)
                sum_up(W - 1, (W - 1) % 3, (W - 1) // 3)
            with eng.Else():
                eng.drain()


def output_phase(nc, s, c, k, v, out):
    ctx = ExitStack()
    with ctx:
        def sb(name, shape, dt):
            return ctx.enter_context(nc.sbuf_tensor(name, shape, dt))

        def sem(name):
            return ctx.enter_context(nc.semaphore(name))

        W = s.W
        x1, t = v["z"], v["z01"]
        mean, var = sb("o_mean", [P, W], FP32), sb("o_var", [P, W], FP32)
        none, some, inv = sb("o_none", [P, W], FP32), sb("o_some", [P, W], FP32), sb("o_inv", [P, W], FP32)
        own_dve, ready, gelu, varied, rooted, normed, stored = (
            sem("ou_dve"), sem("ou_ready"), sem("ou_gelu"), sem("ou_varied"), sem("ou_rooted"), sem("ou_normed"),
            sem("ou_stored"))
        wide = lambda a: a[:, :].unsqueeze(2).broadcast_to([P, W, P])
        block = ctx.enter_context(nc.Block())

        @block.vector
        def _(eng):
            ch = Chain(eng, own_dve)
            total = v["total"][:, :]
            ch.link(eng.tensor_scalar(some[:, :], total, 0.0, None, ALU.is_gt))
            ch.link(eng.tensor_scalar(none[:, :], some[:, :], -1.0, 1.0, ALU.mult, ALU.add))
            ch.link(eng.tensor_tensor(inv[:, :], total, none[:, :], ALU.add))
            ch.link(eng.reciprocal(inv[:, :], inv[:, :]))
            eng.tensor_tensor(t[:, :, :], t[:, :, :], wide(inv), ALU.mult).then_inc(ready, 1)
            eng.wait_ge(gelu, 1)
            ch.link(eng.tensor_scalar(none[:, :], none[:, :], 1.0, None, ALU.add))
            ch.link(eng.tensor_tensor(x1[:, :, :], x1[:, :, :], wide(none), ALU.mult))
            ch.link(eng.tensor_tensor(t[:, :, :], t[:, :, :], x1[:, :, :], ALU.add))
            layer_norm(eng, ch, s, t, x1, mean, var, rooted, varied)
            eng.drain().then_inc(normed, 1)

        @block.scalar
        def _(eng):
            eng.wait_ge(ready, 1)
            eng.activation(t[:, :, :], t[:, :, :], ACT.Gelu).then_inc(gelu, 1)
            eng.wait_ge(varied, 1)
            eng.activation(var[:, :], var[:, :], ACT.Sqrt).then_inc(rooted, 1)

        @block.sync
        def _(eng):
            eng.wait_ge(normed, 1)
            full, rest = s.nodes // P, s.nodes % P
            eng.dma_start(out[0:full * P, :].rearrange("(w p) f -> p w f", p=P), t[:, 0:full, :]).then_inc(stored, 16)
            if rest:
                eng.dma_start(out[full * P:s.nodes, :], t[0:rest, full, :]).then_inc(stored, 16)
            eng.wait_ge(stored, 32 if rest else 16)


def gnn_kernel(nc, x, src, dst, edge_rows, att_w, att_b, out):
    s = Shapes(x.shape[0], src.shape[0])
    ctx = ExitStack()
    with ctx:
        def sb(name, shape, dt):
            return ctx.enter_context(nc.sbuf_tensor(name, shape, dt))

        c, k = constants(nc, sb, s), kept(nc, sb, s)
        v = {"z": sb("v_z", [P, s.W, P], FP32), "z01": sb("v_z01", [P, s.W, P], FP32),
             "score": sb("v_score", [P, s.W], FP32), "total": sb("v_total", [P, s.W], FP32)}
        with ExitStack() as steps:
            def sb_steps(name, shape, dt):
                return steps.enter_context(nc.sbuf_tensor(name, shape, dt))

            of_edges(nc, sb_steps, s, k)
            slots_phase(nc, s, c, k, src, dst, att_w, att_b)
            adjacency_phase(nc, s, c, k)
            v["pieces"] = [sb_steps(f"v_pieces{n}", [P, s.W, 2 * P], FP16) for n in range(2)]
            prepare_phase(nc, s, c, k, v, x)
            appnp_phase(nc, s, c, k, v, edge_rows)
        nodes_phase(nc, s, c, k, v, x)
        maxima_phase(nc, s, c, k)
        attention_phase(nc, s, c, k, v)
        windows_phase(nc, s, c, k, v)
        output_phase(nc, s, c, k, v, out)


_INS = ["x", "src", "dst", "edge_attr_128", "L1_gnn_W_att_w", "L1_gnn_W_att_b"]


def kernel(**inputs):
    import numpy as _np
    import concourse.bacc as _bacc
    from concourse import mybir as _mybir
    from concourse.bass_utils import run_bass_kernel_spmd as _run

    nc = _bacc.Bacc("TRN2", target_bir_lowering=False, num_devices=1)
    arrays, args = {}, []
    for name in _INS:
        a = _np.ascontiguousarray(inputs[name])
        arrays[f"in_{name}_dram"] = a
        args.append(nc.dram_tensor(f"in_{name}_dram", a.shape, _mybir.dt.from_np(a.dtype), kind="ExternalInput").ap())
    shape = inputs["x"].shape
    args.append(nc.dram_tensor("out_dram", shape, _mybir.dt.float32, kind="ExternalOutput").ap())
    gnn_kernel(nc, *args)
    r = _run(nc, [arrays], core_ids=[0])
    return r.results[0]["out_dram"]
```

```python
import concourse.bass as bass
from concourse import mybir
from contextlib import ExitStack

P = 128
FINE = 8
KEY_ROWS = 2
SHIFT_BITS = 5
SHIFTS = P >> SHIFT_BITS
SRC_BITS = 13
MOST_EQUAL = 15.0
STEPS = 10
ALPHA = 0.1
SLOPE = 0.2
EPS = 1e-5
BIG = 1e30
ONE, SCORE, DST1, SRC1, SRC = 128, 129, 130, 131, 132
ROW = 133

FP32, FP16, BF16 = mybir.dt.float32, mybir.dt.float16, mybir.dt.bfloat16
FP8, I32, U32, U16, U8 = mybir.dt.float8e4, mybir.dt.int32, mybir.dt.uint32, mybir.dt.uint16, mybir.dt.uint8
ALU = mybir.AluOpType
ACT = mybir.ActivationFunctionType
X = mybir.AxisListType.X
XY = mybir.AxisListType.XY


class Shapes:

    def __init__(self, n_nodes, n_edges):
        self.nodes, self.edges = n_nodes, n_edges
        self.EP = max(p for p in range(1, P + 1) if n_edges % p == 0)
        self.ET = n_edges // self.EP
        self.CH = max(c for c in range(1, 26) if self.ET % (2 * c) == 0)
        self.W = -(-n_nodes // P)
        mean = n_edges * P / n_nodes
        self.CAP = int(-(-(mean + 5 * mean ** 0.5) // P))
        self.WS = self.CAP * P
        assert self.W * self.WS >= n_edges and n_nodes < 1 << SRC_BITS
        self.FW = self.W * P // FINE
        self.FG = -(-self.FW // P)
        self.W8 = 8 * self.FG
        self.KR = n_edges // P + KEY_ROWS
        self.FC = FINE * self.W
        self.PAD = self.W * P
        self.PZ = P // 4


class Chain:

    def __init__(self, eng, sem):
        self.eng, self.sem, self.n = eng, sem, 0

    def add(self, ins):
        ins.then_inc(self.sem, 1)
        self.n = self.n + 1

    def wait(self):
        self.eng.wait_ge(self.sem, self.n)

    def link(self, ins):
        self.add(ins)
        self.wait()


def constants(nc, sb, s):
    c = {}
    c["row"] = sb("c_row", [P, P], FP32)
    c["row1"] = sb("c_row1", [P, P], FP32)
    c["col"] = sb("c_col", [P, 1], FP32)
    c["ident"] = sb("c_ident", [P, P], FP32)
    c["ident16"] = sb("c_ident16", [P, P], FP16)
    c["ones"] = sb("c_ones", [P, P], FP32)
    c["before"] = sb("c_before", [P, P], FP32)
    c["we"] = sb("c_we", [P, P], FP32)
    c["wn"] = sb("c_wn", [P, P], FP32)
    c["b"] = sb("c_b", [P, 1], FP32)
    return c


def slots_phase(nc, s, c, k, src, dst, att_w, att_b):
    ctx = ExitStack()
    with ctx:
        def sb(name, shape, dt):
            return ctx.enter_context(nc.sbuf_tensor(name, shape, dt))

        def sem(name):
            return ctx.enter_context(nc.semaphore(name))

        EP, ET, W = s.EP, s.ET, s.W
        ends = [sb("end_dst", [EP, ET + 1], I32), sb("end_src", [EP, ET + 1], I32)]
        window, first = k["window"], k["first"]
        low = sb("low_dst", [EP, ET], FP16)
        tmp_i = sb("tmp_i", [EP, ET], I32)
        above = sb("above", [EP, ET], FP32)
        U = max(u for u in range(1, 9) if W % u == 0)
        signs = sb("signs", [EP, U, ET], FP16)
        tail = sb("tail_keys", [1, s.KR * P - s.edges + P], I32)
        key = sb("keys", [EP, ET], I32)
        total = [sb("tot_d", [P, W], FP32), sb("tot_s", [P, W], FP32)]
        balance = [sb("balance_d", [EP, W + 1], FP32), sb("balance_s", [EP, W + 1], FP32)]
        half_on = sb("half_on", [P, W], FP32)
        wins = [sb("wins_d", [P, W], FP32), sb("wins_s", [P, W], FP32)]
        winbase = sb("winbase", [P, W], FP32)
        onesw = sb("onesw", [P, s.W8], FP32)
        wstart = sb("wstart", [P, W + 1], FP32)
        most = sb("most", [P, 8], FP32)
        hot_lo = sb("hot_lo", [EP, 2, s.CH, P], FP16)
        hot_hi = sb("hot_hi", [EP, 2, s.CH, W], FP16)
        r8 = sb("row8", [P, P], FP32)
        below = sb("below", [P, P], FP32)
        group = sb("group", [P, P], FP32)
        wrow = sb("wrow", [P, s.W8], FP32)
        q16i = sb("q16i", [P, 1], I32)
        q16 = sb("q16", [P, 1], FP32)
        mask8 = sb("mask8", [P, s.W8], FP32)
        at8 = sb("at8", [P, s.W8], FP32)
        start8 = sb("start8", [P, s.FG], FP32)
        start8i = sb("start8i", [P, s.FG], I32)
        row8i = sb("row8i", [P, s.FG], I32)
        rowf = sb("rowf", [P, s.FG], FP32)
        c8 = sb("c8", [P, W], FP32)
        row16 = sb("row16", [P, P], FP16)
        wrow16 = sb("wrow16", [P, W], FP16)
        ps_deg = ctx.enter_context(nc.psum_tensor("ps_deg", [P, 512], FP32))
        ps = [ctx.enter_context(nc.psum_tensor(f"ps_tot{i}", [P, 512], FP32)) for i in range(4)]

        loaded, consts, own_dve, hots, hist, summed, totals = (
            sem("sl_loaded"), sem("sl_consts"), sem("sl_dve"), sem("sl_hots"), sem("sl_hist"),
            sem("sl_summed"), sem("sl_totals"))
        stored, keyed, degs = sem("sl_stored"), sem("sl_keyed"), sem("sl_degs")
        memd = sem("sl_memd")
        zeros = k["zeros"]
        zeroed, blank, windowed, counted, begun = (
            sem("sl_zeroed"), sem("sl_blank"), sem("sl_windowed"), sem("sl_counted"), sem("sl_begun"))
        lists = [k["list"][n].rearrange("(w p q) f -> w p (q f)", p=P, q=s.CAP) for n in range(2)]
        block = ctx.enter_context(nc.Block())

        @block.scalar
        def _(eng):
            eng.wait_ge(windowed, 1)
            eng.sem_inc(counted, 1)
            for n in range(2):
                with eng.Fori(0, W // U) as i:
                    eng.wait_ge(counted, n * W + i * U + 1)
                    eng.sem_inc(begun, 1)
                    for u in range(U):
                        h = i * U + u
                        eng.activation(signs[:, u, :], window[n][:, :], ACT.Sign, scale=-1.0,
                                       bias=half_on[0:EP, bass.ds(h, 1)],
                                       accum_out=balance[n][:, bass.ds(h + 1, 1)]).then_inc(counted, 1)

        @block.sync
        def _(eng):
            eng.wait_ge(memd, 1)
            d = dst.rearrange("(p t) -> p t", t=ET)
            eng.dma_start(ends[0][:, 0:ET], d).then_inc(loaded, 16)
            eng.dma_start(ends[0][0:EP - 1, ET:ET + 1], d[1:EP, 0:1],
                          allow_slow_non_contiguous=True).then_inc(loaded, 16)
            eng.dma_start(ends[1][:, 0:ET], src.rearrange("(p t) -> p t", t=ET)).then_inc(loaded, 16)
            w2 = att_w.rearrange("(a n) -> a n", a=2)
            eng.dma_start(c["wn"][:, :], w2[0:1, :].broadcast_to([P, P])).then_inc(loaded, 16)
            eng.dma_start(c["we"][:, :], w2[1:2, :].broadcast_to([P, P])).then_inc(loaded, 16)
            eng.dma_start(c["b"][:, :], att_b.rearrange("(a n) -> a n", a=1).broadcast_to([P, 1])).then_inc(loaded, 16)
            eng.wait_ge(keyed, 1)
            for i in range(SHIFTS):
                skip = i << SHIFT_BITS
                flat = k["keys"][i * s.KR:(i + 1) * s.KR, :].rearrange("r c -> (r c)")
                begin = flat[0:ET - skip].rearrange("(a n) -> a n", a=1)
                middle = flat[ET - skip:s.edges - skip].rearrange("(p t) -> p t", t=ET)
                end = flat[s.edges - skip:s.KR * P].rearrange("(a n) -> a n", a=1)
                eng.dma_start(begin, key[0:1, skip:ET]).then_inc(stored, 16)
                eng.dma_start(middle, key[1:EP, :]).then_inc(stored, 16)
                eng.dma_start(end, tail[:, 0:end.shape[1]]).then_inc(stored, 16)
            eng.wait_ge(blank, 1)
            with eng.Fori(0, W) as w:
                for n in range(2):
                    eng.dma_start(lists[n][bass.ds(w, 1), 0:s.PZ, :].squeeze(0),
                                  zeros[0:s.PZ, :]).then_inc(zeroed, 16)
            eng.wait_ge(stored, 16 * 3 * SHIFTS)
            eng.wait_ge(zeroed, 16 * 2 * W)

        @block.gpsimd
        def _(eng):
            def iota(out, pattern, base, mult):
                eng.iota(out, pattern, base=base, channel_multiplier=mult,
                         allow_small_or_imprecise_dtypes=True).then_inc(consts, 1)
            iota(c["row"][:, :], [[1, P]], 0, 0)
            iota(c["row1"][:, :], [[1, P]], 1, 0)
            iota(c["col"][:, :], [[0, 1]], 0, 1)
            iota(winbase[:, :], [[s.WS, W]], -1, 0)
            iota(r8[:, :], [[0, P // 16], [FINE, 16]], 0, 0)
            iota(wrow[:, :], [[0, s.FG], [1, 8]], 0, 0)
            iota(q16i[:, :], [[0, 1]], 0, 1)
            iota(row16[:, :], [[1, P]], 0, 0)
            iota(wrow16[:, :], [[1, W]], 0, 0)
            iota(k["base8"][:, :], [[FINE * P, s.FG]], 0, FINE)
            iota(k["first_node"][:, :], [[P, W]], 0, 0)
            iota(k["wcol"][:, :], [[1, W]], 0, 0)

        N_CONSTS = 12

        @block.vector
        def _(eng):
            ch = Chain(eng, own_dve)
            eng.memset(ends[0][:, ET:ET + 1], 1 << SRC_BITS).then_inc(memd, 1)
            eng.memset(k["spare_row"][:, :], 0)
            eng.memset(zeros[:, :], 0.0).then_inc(blank, 1)
            ch.add(eng.memset(c["ones"][:, :], 1.0))
            for n in range(2):
                ch.add(eng.memset(balance[n][:, 0:1], -float(ET)))
            ch.add(eng.memset(k["flags"][:, :], 0.0))
            ch.add(eng.memset(onesw[:, :], 1.0))
            ch.add(eng.memset(tail[:, :], (1 << SRC_BITS) - 1 << SRC_BITS))
            for t in total:
                ch.add(eng.memset(t[:, :], 0.0))
            ch.add(eng.memset(most[:, :], 0.0))
            ch.add(eng.memset(c8[:, :], 0.0))
            ch.add(eng.memset(at8[:, :], 0.0))
            eng.wait_ge(consts, N_CONSTS)
            ch.add(eng.tensor_scalar(c["ident"][:, :], c["row"][:, :], c["col"][:, 0:1], None, ALU.is_equal))
            ch.add(eng.tensor_scalar(c["ident16"][:, :], c["row"][:, :], c["col"][:, 0:1], None, ALU.is_equal))
            ch.add(eng.tensor_scalar(c["before"][:, :], c["row"][:, :], c["col"][:, 0:1], None, ALU.is_gt))
            ch.add(eng.tensor_scalar(below[:, :], r8[:, :], c["col"][:, 0:1], None, ALU.is_gt))
            ch.add(eng.tensor_scalar(group[:, :], r8[:, :], float(FINE), c["col"][:, 0:1], ALU.add, ALU.is_gt))
            ch.link(eng.tensor_scalar(q16i[:, :], q16i[:, :], 4, None, ALU.logical_shift_right))
            ch.add(eng.tensor_tensor(group[:, :], group[:, :], below[:, :], ALU.subtract))
            ch.link(eng.tensor_copy(q16[:, :], q16i[:, :]))
            ch.add(eng.tensor_scalar(mask8[:, :], wrow[:, :], q16[:, 0:1], None, ALU.is_equal))
            ch.add(eng.tensor_scalar(half_on[:, :], k["wcol"][:, :], 0.5, None, ALU.add))
            eng.wait_ge(loaded, 16 * 6)
            for n in range(2):
                ch.link(eng.tensor_scalar(tmp_i[:, :], ends[n][:, 0:ET], 7, None, ALU.logical_shift_right))
                ch.link(eng.tensor_copy(window[n][:, :], tmp_i[:, :]))
                ch.add(eng.tensor_scalar(k["end1"][n][:, :], ends[n][:, 0:ET], 1.0, None, ALU.add))
            eng.drain().then_inc(windowed, 1)
            ch.link(eng.tensor_scalar(tmp_i[:, :], ends[0][:, 0:ET], P - 1, None, ALU.bitwise_and))
            ch.add(eng.tensor_copy(low[:, :], tmp_i[:, :]))
            ch.add(eng.tensor_copy(k["src_i"][:, :], ends[1][:, 0:ET]))
            ch.link(eng.tensor_scalar(key[:, :], ends[0][:, 0:ET], SRC_BITS, None, ALU.logical_shift_left))
            eng.tensor_tensor(key[:, :], key[:, :], ends[1][:, 0:ET], ALU.bitwise_or).then_inc(keyed, 1)
            ch.link(eng.tensor_tensor(above[:, :], ends[0][:, 0:ET], ends[0][:, 1:ET + 1], ALU.is_gt))
            ch.link(eng.tensor_reduce(most[0:EP, 0:1], above[:, :], X, ALU.add))

            n_ch = ET // (2 * s.CH)
            with eng.Fori(0, n_ch) as i:
                for b in range(2):
                    eng.wait_ge(hist, i * 2 + b + 1)
                    cols = slice(None), bass.ds((i * 2 + b) * s.CH, s.CH)
                    eng.tensor_tensor(hot_lo[:, b, :, :], row16[0:EP, :].unsqueeze(1).broadcast_to([EP, s.CH, P]),
                                      low[cols].unsqueeze(2).broadcast_to([EP, s.CH, P]),
                                      ALU.is_equal).then_inc(hots, 1)
                    eng.tensor_tensor(hot_hi[:, b, :, :], wrow16[0:EP, :].unsqueeze(1).broadcast_to([EP, s.CH, W]),
                                      window[0][cols].unsqueeze(2).broadcast_to([EP, s.CH, W]),
                                      ALU.is_equal).then_inc(hots, 1)

            eng.wait_ge(counted, 2 * W + 1)
            for n in range(2):
                ch.add(eng.tensor_tensor(total[n][0:EP, :], balance[n][:, 1:W + 1], balance[n][:, 0:W],
                                         ALU.subtract))
            ch.wait()
            for n in range(2):
                ch.add(eng.tensor_scalar(total[n][0:EP, :], total[n][0:EP, :], 0.5, None, ALU.mult))
            eng.drain().then_inc(totals, 1)

            eng.wait_ge(summed, 2)
            for n in range(2):
                ch.add(eng.tensor_tensor(first[n][:, :], ps[0][:, n * W:(n + 1) * W], winbase[:, :], ALU.add))
                ch.add(eng.tensor_copy(wins[n][:, :], ps[1][:, n * W:(n + 1) * W]))
            ch.link(eng.memset(wstart[:, 0:1], 0.0))
            ch.add(eng.tensor_scalar(k["flags"][:, 2:3], ps[2][:, 0:1], 0.0, None, ALU.is_equal))
            for n in range(2):
                ch.add(eng.tensor_reduce(most[:, 2 + n:3 + n], wins[n][:, :], X, ALU.max))
            ch.link(eng.tensor_tensor_scan(wstart[:, 1:W + 1], onesw[:, 0:W], wins[0][:, :], 0.0, ALU.mult, ALU.add))
            ch.link(eng.tensor_tensor(most[:, 4:5], most[:, 2:3], most[:, 3:4], ALU.max))
            ch.link(eng.tensor_scalar(k["flags"][:, 0:1], most[:, 4:5], float(s.WS), None, ALU.is_le))

            eng.wait_ge(hist, 2 * n_ch + 2)
            ch.add(eng.tensor_scalar(k["deg"][:, :], ps_deg[:, 0:W], 1.0, None, ALU.add))
            eng.tensor_copy(k["deg0"][:, :], ps_deg[:, 0:W]).then_inc(degs, 1)
            eng.wait_ge(summed, 3)
            ch.link(eng.tensor_tensor(at8[:, 0:W], ps[3][:, 0:W], wstart[:, 0:W], ALU.add))
            ch.link(eng.tensor_tensor(at8[:, :], at8[:, :], mask8[:, :], ALU.mult))
            ch.link(eng.tensor_reduce(start8[:, :], at8[:, :].rearrange("p (g w) -> p g w", w=8), X, ALU.add))
            ch.link(eng.tensor_copy(start8i[:, :], start8[:, :]))
            ch.add(eng.tensor_scalar(row8i[:, :], start8i[:, :], 7, None, ALU.logical_shift_right))
            ch.link(eng.tensor_scalar(start8i[:, :], start8i[:, :], SHIFT_BITS, None, ALU.logical_shift_right))
            ch.link(eng.tensor_scalar(start8i[:, :], start8i[:, :], SHIFTS - 1, None, ALU.bitwise_and))
            ch.add(eng.tensor_copy(rowf[:, :], row8i[:, :]))
            ch.link(eng.tensor_copy(start8[:, :], start8i[:, :]))
            ch.link(eng.scalar_tensor_tensor(rowf[:, :], start8[:, :], float(s.KR), rowf[:, :], ALU.mult, ALU.add))
            for r in range(KEY_ROWS):
                ch.add(eng.tensor_scalar(k["keyrow"][:, r, :], rowf[:, :], float(r), None, ALU.add))
            ch.link(eng.tensor_copy(c8[:, :], ps[3][:, W:2 * W]))
            ch.link(eng.tensor_reduce(k["most8"][:, :], c8[:, :], X, ALU.max))

        @block.tensor
        def _(eng):
            eng.sem_inc(hist, 2)
            n_ch = ET // (2 * s.CH)

            def chunk(b, n, first, last):
                eng.wait_ge(hots, 2 * n + 2)
                for t in range(s.CH):
                    m = eng.matmul(ps_deg[:, 0:W], hot_lo[:, b, t, :], hot_hi[:, b, t, :],
                                   start=first and t == 0, stop=last and t == s.CH - 1)
                m.then_inc(hist, 1)
            chunk(0, 0, True, False)
            chunk(1, 1, False, n_ch == 1)
            if n_ch > 1:
                if n_ch > 2:
                    with eng.Fori(1, n_ch - 1) as i:
                        chunk(0, i * 2, False, False)
                        chunk(1, i * 2 + 1, False, False)
                chunk(0, 2 * n_ch - 2, False, False)
                chunk(1, 2 * n_ch - 1, False, True)
            eng.wait_ge(totals, 1)
            for n in range(2):
                eng.matmul(ps[0][:, n * W:(n + 1) * W], c["before"][:, :], total[n][:, :], start=True, stop=True)
                eng.matmul(ps[1][:, n * W:(n + 1) * W], c["ones"][:, :], total[n][:, :], start=True, stop=True)
            eng.matmul(ps[2][:, 0:1], c["ones"][:, :], most[:, 0:1], start=True, stop=True).then_inc(summed, 2)
            eng.wait_ge(degs, 1)
            eng.matmul(ps[3][:, 0:W], below[:, :], k["deg0"][:, :], start=True, stop=True)
            eng.matmul(ps[3][:, W:2 * W], group[:, :], k["deg0"][:, :], start=True, stop=True).then_inc(summed, 1)


def credit(eng, k, row, sem):
    eng.dma_start(k["spare"][row:row + 1, :], k["spare_row"][0:1, :]).then_inc(sem, 16)


def kept(nc, sb, s):
    k = {}
    k["wcol"] = sb("k_wcol", [P, s.W], FP32)
    k["base8"] = sb("k_base8", [P, s.FG], FP32)
    k["deg"] = sb("k_deg", [P, s.W], FP32)
    k["deg0"] = sb("k_deg0", [P, s.W], FP32)
    k["keyrow"] = sb("k_keyrow", [P, KEY_ROWS, s.FG], I32)
    k["most8"] = sb("k_most8", [P, 1], FP32)
    k["flags"] = sb("k_flags", [P, 4], FP32)
    k["list"] = [nc.dram_tensor(f"edge_list_{n}", [s.W * s.WS, ROW], FP32).ap() for n in ("dst", "src")]
    k["root"] = sb("k_root", [P, s.W], FP32)
    k["keep"] = sb("k_keep", [P, s.W], FP32)
    k["unscale"] = sb("k_unscale", [P, 1], FP32)
    k["first_node"] = sb("k_first_node", [P, s.W], FP32)
    k["node_rows"] = nc.dram_tensor("node_rows", [s.W, 2, P], FP32).ap()
    k["z_rows"] = nc.dram_tensor("z_rows", [s.PAD, P], FP32).ap()
    k["adj"] = nc.dram_tensor("adjacency", [s.W, P, s.W * P // 4], U32).ap()
    k["lift"] = sb("k_lift", [P, 1], FP32)
    k["spare"] = nc.dram_tensor("spare", [4, 16], I32).ap()
    k["spare_row"] = sb("k_spare", [1, 16], I32)
    k["dense"] = sb("k_dense", [P, 1], I32)
    k["by_window"] = sb("k_by_window", [P, 1], I32)
    k["keys"] = nc.dram_tensor("edge_keys", [SHIFTS * s.KR, P], I32).ap()
    return k


def of_edges(nc, sb, s, k):
    k["slot"] = [sb("k_slot_d", [s.EP, s.ET], I32), sb("k_slot_s", [s.EP, s.ET], I32)]
    k["end1"] = [sb("k_dst1", [s.EP, s.ET], FP32), sb("k_src1", [s.EP, s.ET], FP32)]
    k["src_i"] = sb("k_src_i", [s.EP, s.ET], I32)
    k["window"] = [sb("k_win_dst", [s.EP, s.ET], FP16), sb("k_win_src", [s.EP, s.ET], FP16)]
    k["first"] = [sb("k_first_d", [P, s.W], FP32), sb("k_first_s", [P, s.W], FP32)]


def adjacency_phase(nc, s, c, k):
    ctx = ExitStack()
    with ctx:
        def sb(name, shape, dt):
            return ctx.enter_context(nc.sbuf_tensor(name, shape, dt))

        def sem(name):
            return ctx.enter_context(nc.semaphore(name))

        W, FG, FC, R = s.W, s.FG, s.FC, KEY_ROWS
        RING = 4
        G = P // FINE
        NK = FG * R * P
        key = sb("a_key", [P, FG, R, P], I32)
        tmp = sb("a_tmp", [P, FG, R, P], I32)
        lowf = sb("a_lowf", [P, FG, R, P], FP32)
        node = sb("a_node", [P, FG, R, P], FP32)
        column = sb("a_column", [P, FG, R, P], FP32)
        inside = sb("a_inside", [P, FG, R, P], FP32)
        turned = [sb(f"a_turned{n}", [P, R, FG * P], FP32) for n in range(2)]
        hot_low = sb("a_hot_low", [P, RING, R, P], FP16)
        hot_col = sb("a_hot_col", [P, RING, R, FC], FP16)
        cols = sb("a_cols", [P, FC], FP16)
        row16 = sb("a_row16", [P, P], FP16)
        out8 = [sb(f"a_out{b}", [P, W, P], FP8) for b in range(2)]
        part = [sb(f"a_part{b}", [P, G], FP32) for b in range(2)]
        sums = sb("a_sums", [P, W * G], FP32)
        most = sb("a_most", [P, 4], FP32)
        allmost = sb("a_allmost", [P, 4], FP32)
        flat = lambda t: t[:, :, :, :].rearrange("p g r e -> p (g r e)")
        psum = [ctx.enter_context(nc.psum_tensor(f"a_ps{i}", [P, 512], FP32)) for i in range(RING)]
        pst = [ctx.enter_context(nc.psum_tensor(f"a_pst{i}", [P, 512], FP32)) for i in range(2)]

        gathered, consts, own_dve, ready, turn, copied = (
            sem("ad_gathered"), sem("ad_consts"), sem("ad_dve"), sem("ad_ready"), sem("ad_turn"), sem("ad_copied"))
        begun, begun_p, zeroed = sem("ad_begun"), sem("ad_begun_p"), sem("ad_zeroed")
        lists = [k["list"][n].rearrange("(w p q) f -> w p (q f)", p=P, q=s.CAP) for n in range(2)]
        hot, built, evicted, summed, most_ready, most_all = (
            sem("ad_hot"), sem("ad_built"), sem("ad_evicted"), sem("ad_summed"), sem("ad_most"), sem("ad_most_all"))
        stored = [sem(f"ad_stored{b}") for b in range(2)]
        turns = [(g, r, n) for g in range(FG) for r in range(R) for n in range(2)]
        block = ctx.enter_context(nc.Block())

        def windows(eng, body):
            if W > 1:
                with eng.Fori(0, W // 2) as i:
                    for b in range(2):
                        body(2 * i + b, b, i)
            if W % 2:
                body(W - 1, 0, W // 2)

        @block.gpsimd
        def _(eng):
            eng.iota(cols[:, :], [[1, FC]], base=0, channel_multiplier=0,
                     allow_small_or_imprecise_dtypes=True).then_inc(consts, 1)
            eng.iota(row16[:, :], [[1, P]], base=0, channel_multiplier=0,
                     allow_small_or_imprecise_dtypes=True).then_inc(consts, 1)
            for g in range(FG):
                for r in range(R):
                    eng.indirect_dma_start(
                        key[:, g, r, :], None, k["keys"],
                        bass.IndirectOffsetOnAxis(ap=k["keyrow"][:, r, g:g + 1], axis=0)).then_inc(gathered, 16)
            eng.wait_ge(gathered, 16 * FG * R)

            def body(j, b, visit):
                eng.wait_ge(evicted, RING + j * G + 1)
                eng.sem_inc(begun_p, 1)
                for n in range(2):
                    eng.dma_start(lists[n][bass.ds(j, 1), s.PZ:P, :].squeeze(0),
                                  k["zeros"][s.PZ:P, :]).then_inc(zeroed, 16)
            windows(eng, body)
            eng.wait_ge(zeroed, 16 * 2 * W)
            eng.wait_ge(most_ready, 1)
            eng.partition_all_reduce(allmost[:, :], most[:, :], P, bass.bass_isa.ReduceOp.max).then_inc(most_all, 1)

        @block.vector
        def _(eng):
            ch = Chain(eng, own_dve)
            ch.add(eng.memset(most[:, :], 0.0))
            eng.wait_ge(gathered, 16 * FG * R)
            ch.link(eng.tensor_scalar(flat(tmp), flat(key), SRC_BITS, None, ALU.logical_shift_right))
            ch.add(eng.tensor_copy(flat(node), flat(tmp)))
            ch.link(eng.tensor_scalar(flat(key), flat(key), (1 << SRC_BITS) - 1, None, ALU.bitwise_and))
            ch.link(eng.tensor_scalar(flat(tmp), flat(key), P - 1, None, ALU.bitwise_and))
            eng.tensor_copy(flat(lowf), flat(tmp)).then_inc(ready, 1)
            ch.link(eng.tensor_scalar(flat(key), flat(key), 7, None, ALU.logical_shift_right))
            eng.wait_ge(ready, 1)
            ch.add(eng.tensor_copy(flat(column), flat(key)))
            for g in range(FG):
                ch.add(eng.tensor_scalar(node[:, g, :, :], node[:, g, :, :], k["base8"][:, g:g + 1], None,
                                         ALU.subtract))
            ch.wait()
            ch.add(eng.tensor_scalar(flat(inside), flat(node), 0.0, None, ALU.is_ge))
            ch.link(eng.scalar_tensor_tensor(flat(column), flat(column), float(FINE), flat(node), ALU.mult, ALU.add))
            ch.link(eng.scalar_tensor_tensor(flat(inside), flat(node), float(FINE - 1), flat(inside),
                                             ALU.is_le, ALU.mult))
            ch.link(eng.tensor_scalar(flat(inside), flat(inside), -1024.0, 1024.0, ALU.mult, ALU.add))
            eng.tensor_tensor(flat(column), flat(column), flat(inside), ALU.add).then_inc(ready, 1)
            eng.wait_ge(consts, 2)
            eng.wait_ge(copied, 2 + len(turns))

            def body(j, b, visit):
                for g in range(G):
                    n = j * G + g
                    r0 = g % RING
                    eng.wait_ge(built, n + 1)
                    for r in range(R):
                        eng.tensor_scalar(hot_low[:, r0, r, :], row16[:, :], turned[0][:, r, bass.ds(n, 1)],
                                          None, ALU.is_equal)
                        ins = eng.tensor_scalar(hot_col[:, r0, r, :], cols[:, :], turned[1][:, r, bass.ds(n, 1)],
                                                None, ALU.is_equal)
                    ins.then_inc(hot, 1)
            windows(eng, body)
            eng.wait_ge(summed, W + 1)
            ch.add(eng.tensor_reduce(most[:, 0:1], sums[:, :], X, ALU.max))
            eng.tensor_copy(most[:, 1:2], k["most8"][:, :]).then_inc(most_ready, 1)
            eng.wait_ge(most_all, 1)
            ch.link(eng.tensor_scalar(most[:, 2:3], allmost[:, 0:1], MOST_EQUAL, None, ALU.is_le))
            ch.link(eng.tensor_scalar(most[:, 3:4], allmost[:, 1:2], float(R * P - P // SHIFTS), None, ALU.is_le))
            ch.link(eng.tensor_tensor(most[:, 2:3], most[:, 2:3], most[:, 3:4], ALU.mult))
            ch.link(eng.tensor_tensor(most[:, 2:3], most[:, 2:3], k["flags"][:, 2:3], ALU.mult))
            ch.link(eng.tensor_copy(k["dense"][:, :], most[:, 2:3]))
            ch.link(eng.tensor_copy(k["by_window"][:, :], k["flags"][:, 0:1]))

        @block.tensor
        def _(eng):
            eng.sem_inc(built, RING)
            eng.wait_ge(ready, 2)
            for i, (g, r, n) in enumerate(turns):
                eng.wait_ge(copied, i + 1)
                eng.transpose(pst[i % 2][:, 0:P], (lowf, column)[n][:, g, r, :], c["ident"][:, :]).then_inc(turn, 1)

            def body(j, b, visit):
                for g in range(G):
                    n = j * G + g
                    eng.wait_ge(hot, n + 1)
                    eng.wait_ge(evicted, n + 1)
                    for r in range(R):
                        m = eng.matmul(psum[g % RING][:, 0:FC], hot_low[:, g % RING, r, :], hot_col[:, g % RING, r, :],
                                       start=r == 0, stop=r == R - 1)
                    m.then_inc(built, 1)
            windows(eng, body)

        @block.scalar
        def _(eng):
            eng.sem_inc(copied, 2)
            eng.sem_inc(summed, 1)
            for i, (g, r, n) in enumerate(turns):
                eng.wait_ge(turn, i + 1)
                eng.copy(turned[n][:, r, g * P:(g + 1) * P], pst[i % 2][:, 0:P]).then_inc(copied, 1)
            eng.sem_inc(evicted, RING)

            def body(j, b, visit):
                eng.wait_ge(stored[b], 16 * visit + 16)
                eng.wait_ge(summed, j + 1)
                for g in range(G):
                    n = j * G + g
                    eng.wait_ge(built, RING + n + 1)
                    eng.sem_inc(begun, 1)
                    eng.activation(out8[b][:, :, FINE * g:FINE * (g + 1)],
                                   psum[g % RING][:, 0:FC].rearrange("p (w f) -> p w f", f=FINE), ACT.Copy,
                                   accum_out=part[b][:, g:g + 1], saturate=False).then_inc(evicted, 1)
                eng.wait_ge(evicted, RING + (j + 1) * G)
                eng.copy(sums[:, bass.ds(j * G, G)], part[b][:, :]).then_inc(summed, 1)
            windows(eng, body)

        @block.sync
        def _(eng):
            def body(j, b, visit):
                eng.wait_ge(evicted, RING + (j + 1) * G)
                eng.dma_start(k["adj"][bass.ds(j, 1), :, :].squeeze(0),
                              out8[b][:, :, :].rearrange("p w n -> p (w n)").bitcast(U32)).then_inc(stored[b], 16)
            for b in range(2):
                credit(eng, k, b, stored[b])
            windows(eng, body)
            for b in range(2):
                eng.wait_ge(stored[b], 16 * ((W + 1 - b) // 2) + 16)




def load_nodes(eng, s, tile, x, done):
    full, rest = s.nodes // P, s.nodes % P
    eng.dma_start(tile[:, 0:full, :], x[0:full * P, :].rearrange("(w p) f -> p w f", p=P)).then_inc(done, 16)
    if rest:
        eng.dma_start(tile[0:rest, full, :], x[full * P:s.nodes, :]).then_inc(done, 16)
    return 32 if rest else 16


def prepare_phase(nc, s, c, k, v, x):
    ctx = ExitStack()
    with ctx:
        def sb(name, shape, dt):
            return ctx.enter_context(nc.sbuf_tensor(name, shape, dt))

        def sem(name):
            return ctx.enter_context(nc.semaphore(name))

        W = s.W
        inv_root = sb("p_inv_root", [P, W], FP32)
        most = sb("p_most", [P, 1], FP32)
        power = sb("p_power", [P, 1], FP32)
        scale = sb("p_scale", [P, 1], FP32)
        blank, loaded, rooted, own_dve, part, whole = (
            sem("pr_blank"), sem("pr_loaded"), sem("pr_rooted"), sem("pr_dve"), sem("pr_part"), sem("pr_whole"))
        z, z01, pieces = v["z"], v["z01"], v["pieces"][0]
        wide = lambda t: t[:, :].unsqueeze(2).broadcast_to([P, W, P])
        counts = [0]
        block = ctx.enter_context(nc.Block())

        @block.sync
        def _(eng):
            eng.wait_ge(blank, 1)
            counts[0] = load_nodes(eng, s, z, x, loaded)

        @block.scalar
        def _(eng):
            eng.activation(k["root"][:, :], k["deg"][:, :], ACT.Sqrt).then_inc(rooted, 1)

        @block.gpsimd
        def _(eng):
            eng.wait_ge(part, 1)
            eng.partition_all_reduce(power[:, :], most[:, :], P, bass.bass_isa.ReduceOp.max).then_inc(whole, 1)

        @block.vector
        def _(eng):
            ch = Chain(eng, own_dve)
            eng.memset(z[:, W - 1, :], 0.0).then_inc(blank, 1)
            ch.link(eng.reciprocal(k["keep"][:, :], k["deg"][:, :]))
            ch.add(eng.tensor_scalar(k["keep"][:, :], k["keep"][:, :], 1.0 - ALPHA, None, ALU.mult))
            eng.wait_ge(rooted, 1)
            ch.link(eng.reciprocal(inv_root[:, :], k["root"][:, :]))
            eng.wait_ge(loaded, counts[0])
            ch.link(eng.tensor_tensor(z[:, :, :], z[:, :, :], wide(inv_root), ALU.mult))
            eng.tensor_reduce(most[:, :], z[:, :, :], XY, ALU.max, apply_absolute_value=True).then_inc(part, 1)
            eng.wait_ge(whole, 1)
            bits, sbits = power[:, :].bitcast(I32), scale[:, :].bitcast(I32)
            ch.link(eng.tensor_scalar(bits, bits, 0x7F800000, None, ALU.bitwise_and))
            ch.link(eng.tensor_scalar(bits, bits, float(16 << 23), None, ALU.max))
            ch.link(eng.tensor_scalar(sbits, bits, -1.0, float((127 + 127 + 14) << 23), ALU.mult, ALU.add))
            ch.add(eng.tensor_scalar(k["unscale"][:, :].bitcast(I32), sbits, -1.0, float((127 + 127) << 23),
                                     ALU.mult, ALU.add))
            ch.link(eng.tensor_scalar(z[:, :, :], z[:, :, :], scale[:, 0:1], None, ALU.mult))
            ch.add(eng.tensor_scalar(z01[:, :, :], z[:, :, :], ALPHA, None, ALU.mult))
            ch.link(eng.tensor_copy(pieces[:, :, 0:P], z[:, :, :]))
            ch.link(eng.tensor_tensor(pieces[:, :, P:2 * P], z[:, :, :], pieces[:, :, 0:P], ALU.subtract))


def appnp_phase(nc, s, c, k, v, edge_rows):
    ctx = ExitStack()
    with ctx:
        def sb(name, shape, dt):
            return ctx.enter_context(nc.sbuf_tensor(name, shape, dt))

        def sem(name):
            return ctx.enter_context(nc.semaphore(name))

        W, CAP = s.W, s.CAP
        NB = max([b for b in range(3, 8) if W % b == 0] or [4])
        visits = [W // NB + (b < W % NB) for b in range(NB)]
        z, z01, pieces = v["z"], v["z01"], v["pieces"]
        space = sb("space", [P, max(NB * W * P // 4, 2 * CAP * P)], FP32)
        matrices = space[:, 0:NB * W * P // 4].bitcast(FP8).rearrange("p (b w n) -> p b w n", b=NB, w=W)
        matrix = [matrices[:, b, :, :] for b in range(NB)]
        part = [sb(f"z_part{b}", [P, P], FP32) for b in range(NB)]
        psum = [ctx.enter_context(nc.psum_tensor(f"z_ps{b}", [P, 512], FP32)) for b in range(NB)]
        loaded = [sem(f"ap_loaded{b}") for b in range(NB)]
        summed = [sem(f"ap_summed{b}") for b in range(NB)]
        added = [sem(f"ap_added{b}") for b in range(NB)]
        scaled, own_dve, updated = sem("ap_scaled"), sem("ap_dve"), sem("ap_updated")
        meta = sb("g_meta", [P, CAP, 3], FP32)
        gathered = space[:, 0:CAP * P].rearrange("p (t f) -> p t f", f=P)
        hot = space[:, CAP * P:2 * CAP * P].rearrange("p (t n) -> p t n", n=P)
        names = sb("g_names", [P, P], FP32)
        acc = sb("g_acc", [P, P], FP32)
        psg = ctx.enter_context(nc.psum_tensor("g_ps", [P, 512], FP32))
        EP, rounds = s.EP, W // NB
        LIST_STEPS = STEPS - 2
        ES = s.ET // LIST_STEPS
        left = s.ET - ES * LIST_STEPS
        CHUNKS = rounds // 2 * 2 + 1
        stride = ES // CHUNKS
        last = ES - stride * (CHUNKS - 1)
        assert stride > 0 and left <= last
        stage = [sb(f"stage{b}", [EP, last, ROW], FP32) for b in range(2)]
        place = [sb(f"place{b}", [EP, 2, last], I32) for b in range(2)]
        product = sb("product", [EP, last, P], FP32)
        most = sb("most_score", [P, 1], FP32)
        chunk_most = sb("chunk_most", [EP, 1], FP32)
        all_most = sb("all_most_score", [P, 1], FP32)
        same = sb("same", [EP, s.ET], BF16)
        ones_e = sb("ones_e", [EP, s.ET], BF16)
        count = sb("count", [EP, s.ET], FP32)
        own = sb("own_order", [EP, s.ET], FP32)
        slot = [k["slot"][n][:, :].bitcast(FP32) for n in range(2)]
        slot_dve, ordered = sem("sc_slot_dve"), sem("sc_ordered")
        begun_p, freed = sem("sc_begun_p"), sem("sc_freed")
        most_ready, most_all, stage_dve, filled, begun = (
            sem("sc_most"), sem("sc_most_all"), sem("sc_dve"), sem("sc_filled"), sem("sc_begun"))
        fetched = [sem(f"sc_fetched{b}") for b in range(2)]
        scattered = sem("sc_scattered")
        edges = edge_rows.rearrange("(p t) f -> p t f", t=s.ET)
        g_saved, g_meta, g_rows, g_hot, g_sum, g_used, g_done, g_own, g_begun = (
            sem("ge_saved"), sem("ge_meta"), sem("ge_rows"), sem("ge_hot"), sem("ge_sum"), sem("ge_used"),
            sem("ge_done"), sem("ge_own"), sem("ge_begun"))
        g_ready = sem("ge_ready")
        block = ctx.enter_context(nc.Block())

        def is_dense(eng):
            return eng.value_load(k["dense"][0:1, 0:1], min_val=0, max_val=1) == 1

        def which_chunk(pair, par, half, u):
            step, i, n = pair * 2 + par, half * 2 + u, par * CHUNKS + u
            return step * CHUNKS + i, step * ES + i * stride, n % 2, pair * CHUNKS + half + n // 2

        left_over = LIST_STEPS * CHUNKS, LIST_STEPS * ES, 0, LIST_STEPS // 2 * CHUNKS

        def steps(eng, body, chunk=None, after_list=None):
            def one_step(step, par, chunk_at):
                def nb_windows(i):
                    for b in range(NB):
                        body(step, par, i * NB + b, b, step * visits[b] + i)
                if rounds > 1:
                    with eng.Fori(0, rounds // 2) as half:
                        for u in range(2):
                            chunk_at(half, u, stride)
                            nb_windows(half * 2 + u)
                chunk_at(CHUNKS // 2, 0, last)
                if rounds % 2:
                    nb_windows(rounds - 1)
                for b in range(W % NB):
                    body(step, par, W - W % NB + b, b, step * visits[b] + rounds)

            for par in range(2):
                one_step(par, par, lambda half, u, size: None)
                if after_list:
                    after_list(par)
            with eng.Fori(0, LIST_STEPS // 2) as pair:
                for par in range(2):
                    one_step(pair * 2 + par + 2, par, lambda half, u, size: chunk and chunk(
                        *which_chunk(pair, par, half, u), size))
            if chunk and left:
                chunk(*left_over, left)

        def edge_chunks(eng, chunk):
            with eng.Fori(0, LIST_STEPS // 2) as pair:
                for par in range(2):
                    if CHUNKS > 1:
                        with eng.Fori(0, CHUNKS // 2) as half:
                            for u in range(2):
                                chunk(*which_chunk(pair, par, half, u), stride)
                    chunk(*which_chunk(pair, par, CHUNKS // 2, 0), last)
            if left:
                chunk(*left_over, left)

        def slots_of_window(eng, n, h):
            ch = Chain(eng, slot_dve)
            ch.n = 1 + (n * (W + 1) + h) * 4
            eng.tensor_scalar(same[:, :], k["window"][n][:, :], k["wcol"][0:EP, bass.ds(h, 1)], None,
                              ALU.is_equal).then_inc(slot_dve, 1)
            ch.n = ch.n + 1
            ch.wait()
            ch.link(eng.tensor_tensor_scan(count[:, :], ones_e[:, :], same[:, :], k["first"][n][0:EP, bass.ds(h, 1)],
                                           ALU.mult, ALU.add))
            ch.link(eng.tensor_tensor(count[:, :], count[:, :], same[:, :], ALU.mult))
            ch.add(eng.tensor_tensor(slot[n], slot[n], count[:, :], ALU.add))

        def finish_slots(eng, n):
            ch = Chain(eng, slot_dve)
            ch.n = 1 + (n * (W + 1) + W) * 4
            ch.wait()
            eng.wait_ge(ordered, 1)
            ch.link(eng.tensor_tensor(slot[n], slot[n], own[:, :], ALU.subtract))
            ch.link(eng.scalar_tensor_tensor(slot[n], slot[n], k["flags"][0:EP, 0:1], own[:, :], ALU.mult, ALU.add))
            ch.link(eng.tensor_copy(count[:, :], slot[n]))
            ch.link(eng.tensor_copy(k["slot"][n][:, :], count[:, :]))

        def fetch(eng, n, first, b, visit, size):
            eng.wait_ge(freed, n + 1)
            eng.dma_start(stage[b][:, 0:size, 0:P], edges[:, bass.ds(first, size), :]).then_inc(fetched[b], 16)

        def fill(eng, n, first, b, visit, size):
            cols = slice(None), bass.ds(first, size)
            now = stage[b][:, 0:size, :]
            ch = Chain(eng, stage_dve)
            ch.n = n * 3 + 1
            ch.wait()
            eng.wait_ge(freed, n + 1)
            eng.sem_inc(begun, 1)
            for side in range(2):
                eng.tensor_copy(place[b][:, side, 0:size], k["slot"][side][cols])
                eng.tensor_copy(now[:, :, DST1 + side], k["end1"][side][cols])
            eng.tensor_copy(now[:, :, SRC].bitcast(I32), k["src_i"][cols])
            eng.wait_ge(fetched[b], 16 * (visit + 1))
            ch.link(eng.tensor_tensor(product[:, 0:size, :], now[:, :, 0:P],
                                      c["we"][0:EP, :].unsqueeze(1).broadcast_to([EP, size, P]), ALU.mult))
            eng.tensor_reduce(now[:, :, SCORE], product[:, 0:size, :], X, ALU.add).then_inc(filled, 1)
            eng.wait_ge(filled, n + 1)
            ch.link(eng.tensor_reduce(chunk_most[:, :], now[:, :, SCORE], X, ALU.max, apply_absolute_value=True))
            ch.add(eng.tensor_tensor(most[0:EP, :], most[0:EP, :], chunk_most[:, :], ALU.max))

        def scatter(eng, n, first, b, visit, size):
            eng.wait_ge(filled, n + 1)
            eng.sem_inc(begun_p, 1)
            for e in range(size):
                for side in range(2):
                    eng.indirect_dma_start(
                        k["list"][side], bass.IndirectOffsetOnAxis(ap=place[b][:, side, e:e + 1], axis=0),
                        stage[b][:, e, :], None).then_inc(scattered, 16)
            eng.wait_ge(scattered, 2 * 16 * (first + size))
            eng.sem_inc(freed, 1)

        def chunks(eng, body, step_start=lambda step: None):
            with eng.Fori(0, STEPS) as step:
                step_start(step)
                with eng.Fori(0, W) as w:
                    with eng.Fori(0, W) as ck:
                        body(step, ck, (step * W + w) * W + ck)

        @block.sync
        def _(eng):
            with eng.If(is_dense(eng)):
                def body(step, par, j, b, visit):
                    eng.wait_ge(summed[b], visit + 1)
                    eng.dma_start(matrix[b][:, :, :].rearrange("p w n -> p (w n)").bitcast(U32),
                                  k["adj"][bass.ds(j, 1), :, :].squeeze(0)).then_inc(loaded[b], 16)
                steps(eng, body, lambda *chunk: fetch(eng, *chunk))
            with eng.Else():
                edge_chunks(eng, lambda *chunk: fetch(eng, *chunk))
                eng.wait_ge(freed, 2 + LIST_STEPS * CHUNKS + (left > 0))
                listed = k["list"][0].rearrange("(w p q) f -> w p q f", p=P, q=CAP)

                def step_start(step):
                    eng.wait_ge(g_done, step * W + 1)
                    eng.dma_start(k["z_rows"].rearrange("(w p) f -> p w f", p=P), z[:, :, :]).then_inc(g_saved, 16)

                def body(step, ck, q):
                    eng.wait_ge(g_saved, 16 * (step + 1))
                    eng.wait_ge(g_used, q + 1)
                    eng.dma_start(meta[:, :, :], listed[bass.ds(ck, 1), :, :, DST1:SRC + 1].squeeze(0))\
                       .then_inc(g_meta, 16)
                chunks(eng, body, step_start)

        @block.gpsimd
        def _(eng):
            eng.iota(own[:, :], [[1, s.ET]], base=0, channel_multiplier=s.ET,
                     allow_small_or_imprecise_dtypes=True).then_inc(ordered, 1)
            eng.sem_inc(freed, 2)
            edge_chunks(eng, lambda *chunk: scatter(eng, *chunk))
            with eng.If(is_dense(eng)):
                eng.drain()
            with eng.Else():
                def body(step, ck, q):
                    eng.wait_ge(g_meta, 16 * (q + 1))
                    eng.sem_inc(g_begun, 1)
                    for t in range(CAP):
                        eng.indirect_dma_start(gathered[:, t, :], None, k["z_rows"], bass.IndirectOffsetOnAxis(
                            ap=meta[:, t, 2:3].bitcast(I32), axis=0)).then_inc(g_rows, 16)
                    eng.wait_ge(g_rows, 16 * CAP)
                    eng.inc_swdge_sem([g_rows], [16 * CAP], mode="sub")
                    eng.sem_inc(g_ready, 1)
                chunks(eng, body)
            eng.wait_ge(most_ready, 1)
            eng.partition_all_reduce(all_most[:, :], most[:, :], P, bass.bass_isa.ReduceOp.max).then_inc(most_all, 1)

        @block.tensor
        def _(eng):
            eng.sem_inc(updated, 1)
            for b in range(NB):
                eng.sem_inc(summed[b], 1)
                eng.sem_inc(added[b], 1)
            with eng.If(is_dense(eng)):
                def body(step, par, j, b, visit):
                    eng.wait_ge(updated, step * W + 1)
                    eng.wait_ge(loaded[b], 16 * (visit + 1))
                    eng.wait_ge(added[b], visit + 1)
                    out = psum[b][:, 0:2 * P]
                    eng.matmul(out, c["ident16"][:, :], pieces[par][:, bass.ds(j, 1), :].squeeze(1),
                               start=True, stop=False)
                    for w in range(W):
                        m = eng.matmul(out, matrix[b][:, w, :], pieces[par][:, w, :], start=False, stop=w == W - 1)
                    m.then_inc(summed[b], 1)
                steps(eng, body)
            with eng.Else():
                def body(step, ck, q):
                    eng.wait_ge(g_hot, q + 1)
                    eng.wait_ge(g_ready, q + 1)
                    for t in range(CAP):
                        m = eng.matmul(psg[:, 0:P], hot[:, t, :], gathered[:, t, :], start=t == 0, stop=t == CAP - 1)
                    m.then_inc(g_sum, 1)
                chunks(eng, body)

        @block.scalar
        def _(eng):
            with eng.If(is_dense(eng)):
                def body(step, par, j, b, visit):
                    eng.wait_ge(summed[b], visit + 2)
                    eng.wait_ge(added[b], visit + 1)
                    eng.activation(part[b][:, :], psum[b][:, P:2 * P], ACT.Copy,
                                   scale=k["keep"][:, bass.ds(j, 1)]).then_inc(scaled, 1)
                steps(eng, body)
            with eng.Else():
                eng.drain()

        @block.vector
        def _(eng):
            eng.memset(most[:, :], 0.0).then_inc(stage_dve, 1)
            for b in range(2):
                eng.memset(stage[b][:, :, ONE:ONE + 1], 1.0)
            for n in range(2):
                eng.memset(slot[n], 0.0)
            eng.memset(ones_e[:, :], 1.0).then_inc(slot_dve, 1)
            eng.wait_ge(slot_dve, 1)
            eng.sem_inc(own_dve, 1)
            with eng.If(is_dense(eng)):
                def body(step, par, j, b, visit):
                    n = step * W + j
                    now = z[:, bass.ds(j, 1), :].squeeze(1)
                    new = pieces[1 - par][:, bass.ds(j, 1), :].squeeze(1)
                    eng.wait_ge(scaled, n + 1)
                    eng.scalar_tensor_tensor(now, psum[b][:, 0:P], k["keep"][:, bass.ds(j, 1)], part[b][:, :],
                                             ALU.mult, ALU.add).then_inc(added[b], 1)
                    eng.wait_ge(added[b], visit + 2)
                    eng.tensor_tensor(now, now, z01[:, bass.ds(j, 1), :].squeeze(1), ALU.add).then_inc(own_dve, 1)
                    eng.wait_ge(own_dve, 2 * n + 2)
                    eng.tensor_copy(new[:, 0:P], now).then_inc(own_dve, 1)
                    eng.wait_ge(own_dve, 2 * n + 3)
                    eng.tensor_tensor(new[:, P:2 * P], now, new[:, 0:P], ALU.subtract).then_inc(updated, 1)
                    if isinstance(step, int):
                        slots_of_window(eng, step, j)
                steps(eng, body, lambda *chunk: fill(eng, *chunk), lambda n: finish_slots(eng, n))
            with eng.Else():
                for n in range(2):
                    with eng.Fori(0, W) as h:
                        slots_of_window(eng, n, h)
                    finish_slots(eng, n)
                edge_chunks(eng, lambda *chunk: fill(eng, *chunk))
                for ours in (g_own, g_done, g_used):
                    eng.sem_inc(ours, 1)
                per = 1 + 4 * W
                with eng.Fori(0, STEPS) as step:
                    eng.wait_ge(g_saved, 16 * (step + 1))
                    eng.wait_ge(g_own, step * per + 1)
                    eng.tensor_copy(names[:, :], c["row1"][:, :]).then_inc(g_own, 1)
                    with eng.Fori(0, W) as w:
                        own = step * per + 2 + 4 * w
                        eng.wait_ge(g_own, own)
                        eng.wait_ge(g_done, step * W + w + 1)
                        eng.memset(acc[:, :], 0.0).then_inc(g_own, 1)
                        with eng.Fori(0, W) as ck:
                            q = (step * W + w) * W + ck
                            eng.wait_ge(g_own, own + 1)
                            eng.wait_ge(g_meta, 16 * (q + 1))
                            eng.tensor_tensor(hot[:, :, :], names[:, :].unsqueeze(1).broadcast_to([P, CAP, P]),
                                              meta[:, :, 0:1].broadcast_to([P, CAP, P]),
                                              ALU.is_equal).then_inc(g_hot, 1)
                            eng.wait_ge(g_sum, q + 1)
                            eng.wait_ge(g_used, q + 1)
                            eng.tensor_tensor(acc[:, :], acc[:, :], psg[:, 0:P], ALU.add).then_inc(g_used, 1)
                        now = z[:, bass.ds(w, 1), :].squeeze(1)
                        eng.wait_ge(g_used, (step * W + w + 1) * W + 1)
                        eng.tensor_tensor(acc[:, :], acc[:, :], now, ALU.add).then_inc(g_own, 1)
                        eng.wait_ge(g_own, own + 2)
                        eng.tensor_scalar(acc[:, :], acc[:, :], k["keep"][:, bass.ds(w, 1)], None,
                                          ALU.mult).then_inc(g_own, 1)
                        eng.tensor_scalar(names[:, :], names[:, :], float(P), None, ALU.add).then_inc(g_own, 1)
                        eng.wait_ge(g_own, own + 4)
                        eng.tensor_tensor(now, acc[:, :], z01[:, bass.ds(w, 1), :].squeeze(1),
                                          ALU.add).then_inc(g_done, 1)
                    eng.wait_ge(g_done, (step + 1) * W + 1)
            eng.drain().then_inc(most_ready, 1)
            eng.wait_ge(most_all, 1)
            eng.tensor_scalar(k["lift"][:, :], all_most[:, :], 2.0, 1.0, ALU.mult, ALU.add)


def ring(eng, trips, body):
    if trips > 1:
        with eng.Fori(0, trips // 2) as i:
            for b in range(2):
                body(2 * i + b, b, i)
    if trips % 2:
        body(trips - 1, 0, trips // 2)


def window_chunks(eng, s, k, body):
    with eng.If(eng.value_load(k["by_window"][0:1, 0:1], min_val=0, max_val=1) == 0):
        with eng.Fori(0, s.W) as w:
            ring(eng, s.W, lambda ck, b, i: body(w, ck, w * s.W + ck, b, w * ((s.W + 1 - b) // 2) + i))
    with eng.Else():
        eng.drain()


def maxima_phase(nc, s, c, k):
    ctx = ExitStack()
    with ctx:
        def sb(name, shape, dt):
            return ctx.enter_context(nc.sbuf_tensor(name, shape, dt))

        def sem(name):
            return ctx.enter_context(nc.semaphore(name))

        W, CAP = s.W, s.CAP
        banks = -(-CAP // 4)
        meta = [sb(f"m_meta{b}", [P, 2, CAP, 3], FP32) for b in range(2)]
        masked = [sb(f"m_masked{b}", [P, 2, CAP, P], FP32) for b in range(2)]
        names = sb("m_names", [P, P], FP32)
        best = sb("m_best", [P, W], FP32)
        new_best = sb("m_new_best", [P, 1], FP32)
        cand = sb("m_cand", [P, 2 * banks], FP32)
        turned = sb("m_turned", [P, P], FP32)
        psum = [ctx.enter_context(nc.psum_tensor(f"m_ps{i}", [P, 512], FP32)) for i in range(banks)]
        pst = ctx.enter_context(nc.psum_tensor("m_pst", [P, 512], FP32))
        loaded = [sem(f"mx_loaded{b}") for b in range(2)]
        turns = [sem(f"mx_turns{b}") for b in range(2)]
        masks, reads, own_dve, final, turn, flat, stored = (
            sem("mx_masks"), sem("mx_reads"), sem("mx_dve"), sem("mx_final"), sem("mx_turn"), sem("mx_flat"),
            sem("mx_stored"))
        listed = [k["list"][n].rearrange("(w p q) f -> w p q f", p=P, q=CAP) for n in range(2)]
        PER = 5
        block = ctx.enter_context(nc.Block())

        @block.sync
        def _(eng):
            def body(w, ck, q, b, visit):
                eng.wait_ge(turns[b], 2 * visit + 1)
                for n in range(2):
                    eng.dma_start(meta[b][:, n, :, :], listed[n][bass.ds(ck, 1), :, :, SCORE:SRC].squeeze(0))\
                       .then_inc(loaded[b], 16)
            window_chunks(eng, s, k, body)
            eng.wait_ge(flat, 1)
            eng.dma_start(k["node_rows"][:, 1, :], turned[0:W, :]).then_inc(stored, 16)
            eng.wait_ge(stored, 16)

        @block.vector
        def _(eng):
            ch = Chain(eng, own_dve)
            ch.link(eng.memset(best[:, :], -BIG))

            def body(w, ck, q, b, visit):
                ch.n = 1 + q * PER
                ch.link(eng.tensor_scalar(names[:, :], c["row1"][:, :], k["first_node"][:, bass.ds(w, 1)], None,
                                          ALU.add))
                eng.wait_ge(loaded[b], 32 * (visit + 1))
                eng.wait_ge(turns[b], 2 * visit + 1)
                for n in range(2):
                    tiles = masked[b][:, n, :, :]
                    ch.link(eng.tensor_tensor(tiles, names[:, :].unsqueeze(1).broadcast_to([P, CAP, P]),
                                              meta[b][:, n, :, 1 + n:2 + n].broadcast_to([P, CAP, P]),
                                              ALU.not_equal))
                    eng.scalar_tensor_tensor(tiles, tiles, -BIG, meta[b][:, n, :, 0:1].broadcast_to([P, CAP, P]),
                                             ALU.mult, ALU.add).then_inc(masks, 1)
                for n in range(2):
                    eng.wait_ge(turns[b], 2 * visit + n + 2)
                    for g in range(banks):
                        t = min(4, CAP - 4 * g)
                        eng.tensor_reduce(cand[:, n * banks + g:n * banks + g + 1], psum[g][:, 0:t * P], X,
                                          ALU.max).then_inc(reads, 1)
                eng.wait_ge(reads, banks + 2 * banks * (q + 1))
                ch.link(eng.tensor_reduce(new_best[:, :], cand[:, :], X, ALU.max))
                now = best[:, bass.ds(w, 1)]
                ch.link(eng.tensor_tensor(now, now, new_best[:, :], ALU.max))
            window_chunks(eng, s, k, body)
            eng.drain().then_inc(final, 1)
            eng.wait_ge(turn, 1)
            eng.tensor_copy(turned[0:W, :], pst[0:W, 0:P]).then_inc(flat, 1)

        @block.tensor
        def _(eng):
            eng.sem_inc(reads, banks)
            for b in range(2):
                eng.sem_inc(turns[b], 1)

            def body(w, ck, q, b, visit):
                for n in range(2):
                    eng.wait_ge(masks, 2 * q + n + 1)
                    for t in range(CAP):
                        if t % 4 == 0:
                            eng.wait_ge(reads, (2 * q + n) * banks + t // 4 + 1)
                        m = eng.transpose(psum[t // 4][:, (t % 4) * P:(t % 4 + 1) * P], masked[b][:, n, t, :],
                                          c["ident"][:, :])
                    m.then_inc(turns[b], 1)
            window_chunks(eng, s, k, body)
            eng.wait_ge(final, 1)
            eng.transpose(pst[0:W, 0:P], best[:, :], c["ident"][:, :]).then_inc(turn, 1)


def layer_norm(eng, ch, s, t, sq, mean, var, root_sem, ready_sem):
    wide = lambda a: a[:, :].unsqueeze(2).broadcast_to([P, s.W, P])
    ch.link(eng.tensor_reduce(mean[:, :], t[:, :, :], X, ALU.add))
    ch.link(eng.tensor_scalar(mean[:, :], mean[:, :], 1.0 / P, None, ALU.mult))
    ch.link(eng.tensor_tensor(t[:, :, :], t[:, :, :], wide(mean), ALU.subtract))
    ch.link(eng.tensor_tensor(sq[:, :, :], t[:, :, :], t[:, :, :], ALU.mult))
    ch.link(eng.tensor_reduce(var[:, :], sq[:, :, :], X, ALU.add))
    eng.tensor_scalar(var[:, :], var[:, :], 1.0 / P, EPS, ALU.mult, ALU.add).then_inc(ready_sem, 1)
    eng.wait_ge(root_sem, 1)
    ch.link(eng.reciprocal(var[:, :], var[:, :]))
    ch.link(eng.tensor_tensor(t[:, :, :], t[:, :, :], wide(var), ALU.mult))


def nodes_phase(nc, s, c, k, v, x):
    ctx = ExitStack()
    with ctx:
        def sb(name, shape, dt):
            return ctx.enter_context(nc.sbuf_tensor(name, shape, dt))

        def sem(name):
            return ctx.enter_context(nc.semaphore(name))

        W = s.W
        z, other = v["z"], v["z01"]
        mean, var, score = sb("n_mean", [P, W], FP32), sb("n_var", [P, W], FP32), v["score"]
        turned = sb("n_turned", [P, P], FP32)
        pst = ctx.enter_context(nc.psum_tensor("n_pst", [P, 512], FP32))
        loaded, own_dve, varied, rooted, scored, turn, flat, stored = (
            sem("no_loaded"), sem("no_dve"), sem("no_varied"), sem("no_rooted"), sem("no_scored"), sem("no_turn"),
            sem("no_flat"), sem("no_stored"))
        wide = lambda a: a[:, :].unsqueeze(2).broadcast_to([P, W, P])
        counts = [0]
        block = ctx.enter_context(nc.Block())

        @block.sync
        def _(eng):
            counts[0] = load_nodes(eng, s, other, x, loaded)
            eng.wait_ge(flat, 1)
            eng.dma_start(k["node_rows"][:, 0, :], turned[0:W, :]).then_inc(stored, 16)
            eng.wait_ge(stored, 16)

        @block.scalar
        def _(eng):
            eng.wait_ge(varied, 1)
            eng.activation(var[:, :], var[:, :], ACT.Sqrt).then_inc(rooted, 1)

        @block.tensor
        def _(eng):
            eng.wait_ge(scored, 1)
            eng.transpose(pst[0:W, 0:P], score[:, :], c["ident"][:, :]).then_inc(turn, 1)

        @block.vector
        def _(eng):
            ch = Chain(eng, own_dve)
            ch.link(eng.tensor_tensor(z[:, :, :], z[:, :, :], wide(k["root"]), ALU.mult))
            ch.link(eng.tensor_scalar(z[:, :, :], z[:, :, :], k["unscale"][:, 0:1], 0.0, ALU.mult, ALU.max))
            eng.wait_ge(loaded, counts[0])
            ch.link(eng.tensor_tensor(z[:, :, :], z[:, :, :], other[:, :, :], ALU.add))
            layer_norm(eng, ch, s, z, other, mean, var, rooted, varied)
            ch.link(eng.tensor_tensor(other[:, :, :], z[:, :, :],
                                      c["wn"][:, :].unsqueeze(1).broadcast_to([P, W, P]), ALU.mult))
            ch.link(eng.tensor_reduce(score[:, :], other[:, :, :], X, ALU.add))
            eng.tensor_scalar(score[:, :], score[:, :], c["b"][:, 0:1], None, ALU.add).then_inc(scored, 1)
            eng.wait_ge(turn, 1)
            eng.tensor_copy(turned[0:W, :], pst[0:W, 0:P]).then_inc(flat, 1)


def attention_phase(nc, s, c, k, v):
    ctx = ExitStack()
    with ctx:
        def sb(name, shape, dt):
            return ctx.enter_context(nc.sbuf_tensor(name, shape, dt))

        def sem(name):
            return ctx.enter_context(nc.semaphore(name))

        W, CAP = s.W, s.CAP
        T = 2 * CAP
        acc, total = v["z01"], v["total"]
        rows = [sb(f"t_rows{b}", [P, 2, CAP, ROW], FP32) for b in range(2)]
        tables = [sb(f"t_tables{b}", [P, 2, P], FP32) for b in range(2)]
        weights = sb("t_weights", [P, 2, CAP, P], FP32)
        waste = sb("t_waste", [P, 2, P], FP32)
        names = sb("t_names", [P, P], FP32)
        names_p = sb("t_names_p", [P, P], FP32)
        own = [sb(f"t_own{b}", [P, 2, CAP], FP32) for b in range(2)]
        top = [sb(f"t_top{b}", [P, 2, CAP], FP32) for b in range(2)]
        score = [sb(f"t_score{b}", [P, 2, CAP], FP32) for b in range(2)]
        weight = [sb(f"t_weight{b}", [P, 2, CAP], FP32) for b in range(2)]
        sums = [sb(f"t_sums{b}", [P, P + 1], FP32) for b in range(2)]
        psum = [ctx.enter_context(nc.psum_tensor(f"t_ps{b}", [P, 512], FP32)) for b in range(2)]
        loaded = [sem(f"at_loaded{b}") for b in range(2)]
        summed = [sem(f"at_summed{b}") for b in range(2)]
        own_dve, gathered, scored, weighed, hot, read, added, begun, named, blank = (
            sem("at_dve"), sem("at_gathered"), sem("at_scored"), sem("at_weighed"), sem("at_hot"), sem("at_read"),
            sem("at_added"), sem("at_begun"), sem("at_named"), sem("at_blank"))
        listed = [k["list"][n].rearrange("(w p q) f -> w p (q f)", p=P, q=CAP) for n in range(2)]
        PER = 6
        block = ctx.enter_context(nc.Block())

        @block.sync
        def _(eng):
            def body(w, ck, q, b, visit):
                eng.wait_ge(summed[b], visit + 1)
                for n in range(2):
                    eng.dma_start(rows[b][:, n, :, :].rearrange("p q f -> p (q f)"),
                                  listed[n][bass.ds(ck, 1), :, :].squeeze(0)).then_inc(loaded[b], 16)
                eng.dma_start(tables[b][:, :, :],
                              k["node_rows"][bass.ds(w, 1), :, :].broadcast_to([P, 2, P])).then_inc(loaded[b], 16)
            window_chunks(eng, s, k, body)

        @block.vector
        def _(eng):
            ch = Chain(eng, own_dve)

            ch.add(eng.memset(names[:, :], 0.0))

            def body(w, ck, q, b, visit):
                ch.n = 1 + q * PER
                ch.wait()
                ch.link(eng.tensor_scalar(names[:, :], c["row1"][:, :], k["first_node"][:, bass.ds(w, 1)], None,
                                          ALU.add))
                eng.wait_ge(loaded[b], 48 * (visit + 1))
                for t in range(T):
                    n, i = t // CAP, t % CAP
                    for m, into in enumerate((own, top)):
                        if t:
                            eng.wait_ge(gathered, 2 * (T * q + t - 1) + m + 1)
                        eng.scalar_tensor_tensor(waste[:, m, :], names[:, :], rows[b][:, n, i, DST1 + n:DST1 + n + 1],
                                                 tables[b][:, m, :], ALU.is_equal, ALU.mult,
                                                 accum_out=into[b][:, n, i:i + 1]).then_inc(gathered, 1)
                eng.wait_ge(gathered, 2 * T * (q + 1))
                edge = rows[b][:, :, :, SCORE]
                ch.add(eng.tensor_tensor(score[b][:, :, :], own[b][:, :, :], edge, ALU.add))
                ch.link(eng.tensor_tensor(top[b][:, :, :], own[b][:, :, :], top[b][:, :, :], ALU.add))
                ch.add(eng.scalar_tensor_tensor(score[b][:, :, :], score[b][:, :, :], SLOPE, score[b][:, :, :],
                                                ALU.mult, ALU.max))
                ch.link(eng.scalar_tensor_tensor(top[b][:, :, :], top[b][:, :, :], SLOPE, top[b][:, :, :],
                                                 ALU.mult, ALU.max))
                ch.link(eng.tensor_tensor(score[b][:, :, :], score[b][:, :, :], top[b][:, :, :], ALU.subtract))
                eng.tensor_scalar(score[b][:, :, :], score[b][:, :, :], 0.0, None, ALU.min).then_inc(scored, 1)
                eng.wait_ge(scored, q + 1)
            window_chunks(eng, s, k, body)

        @block.scalar
        def _(eng):
            def body(w, ck, q, b, visit):
                eng.wait_ge(scored, q + 1)
                eng.activation(weight[b][:, :, :], score[b][:, :, :], ACT.Exp).then_inc(weighed, 1)
                eng.wait_ge(summed[b], visit + 2)
                eng.copy(sums[b][:, :], psum[b][:, 0:P + 1]).then_inc(read, 1)
            window_chunks(eng, s, k, body)

        @block.gpsimd
        def _(eng):
            eng.memset(acc[:, :, :], 0.0)
            eng.memset(total[:, :], 0.0).then_inc(blank, 1)
            eng.wait_ge(blank, 1)
            eng.sem_inc(hot, 1)
            eng.sem_inc(added, 1)

            def body(w, ck, q, b, visit):
                eng.wait_ge(hot, T * q + 1)
                eng.sem_inc(begun, 1)
                eng.tensor_tensor(names_p[:, :], c["row1"][:, :],
                                  k["first_node"][:, bass.ds(w, 1)].broadcast_to([P, P]), ALU.add).then_inc(named, 1)
                eng.wait_ge(named, q + 1)
                eng.wait_ge(weighed, q + 1)
                eng.sem_inc(begun, 1)
                for t in range(T):
                    n, i = t // CAP, t % CAP
                    eng.tensor_scalar(weights[:, n, i, :], names_p[:, :], rows[b][:, n, i, DST1 + n:DST1 + n + 1],
                                      weight[b][:, n, i:i + 1], ALU.is_equal, ALU.mult).then_inc(hot, 1)
                eng.wait_ge(read, q + 1)
                eng.wait_ge(added, q + 1)
                eng.sem_inc(begun, 1)
                now, now_total = acc[:, bass.ds(w, 1), :].squeeze(1), total[:, bass.ds(w, 1)]
                eng.tensor_tensor(now, now, sums[b][:, 0:P], ALU.add)
                eng.tensor_tensor(now_total, now_total, sums[b][:, P:P + 1], ALU.add).then_inc(added, 1)
            window_chunks(eng, s, k, body)

        @block.tensor
        def _(eng):
            for b in range(2):
                eng.sem_inc(summed[b], 1)

            def body(w, ck, q, b, visit):
                for t in range(T):
                    n, i = t // CAP, t % CAP
                    eng.wait_ge(hot, T * q + t + 2)
                    m = eng.matmul(psum[b][:, 0:P + 1], weights[:, n, i, :], rows[b][:, n, i, 0:P + 1],
                                   start=t == 0, stop=t == T - 1)
                m.then_inc(summed[b], 1)
            window_chunks(eng, s, k, body)


def by_three(eng, start, stop, body):
    rounds = (stop - start) // 3
    if rounds > 1:
        with eng.Fori(0, rounds) as i:
            for r in range(start, start + 3):
                body(i * 3 + r, r % 3, i + r // 3)
        start = start + 3 * rounds
    for w in range(start, stop):
        body(w, w % 3, w // 3)


def after(w, b, visit):
    return w + 1, (b + 1) % 3, visit + (b + 1) // 3


def windows_phase(nc, s, c, k, v):
    ctx = ExitStack()
    with ctx:
        def sb(name, shape, dt):
            return ctx.enter_context(nc.sbuf_tensor(name, shape, dt))

        def sem(name):
            return ctx.enter_context(nc.semaphore(name))

        W, CAP = s.W, s.CAP
        sums, totals = v["z01"], v["total"]
        GROUPS = [(n, t, min(t + 4, CAP)) for n in range(2) for t in range(0, CAP, 4)]
        NG = len(GROUPS)
        PARTS = (0, CAP), (CAP, 2 * CAP)
        RING = 4
        EARLY = max(1, NG // 2 - 2)
        rows = [sb(f"w_rows{b}", [P, 2, CAP, ROW], FP32) for b in range(3)]
        hot = [sb(f"w_hot{b}", [P, 2, CAP, P], BF16) for b in range(3)]
        lifted = [sb(f"w_lifted{b}", [P, 2, CAP], FP32) for b in range(3)]
        place = sb("w_place", [P, 2, CAP], BF16)
        hot_turned = sb("w_hot_turned", [P, 2, CAP, P], BF16)
        scores = sb("w_scores", [P, 2, CAP, P], FP32)
        weights = sb("w_weights", [P, 2 * CAP, P], FP32)
        cand = sb("w_cand", [P, NG], FP32)
        best = sb("w_best", [P, 1], FP32)
        pair = sb("w_pair", [P, 2], FP32)
        rest = sb("w_rest", [P, 2], FP32)
        pieces = sb("w_pieces", [P, 3, 2], BF16)
        edge_pair = sb("w_edge_pair", [P, 2 * CAP, 2], FP32)
        score = sb("w_score", [P, 2, CAP], FP32)
        weight = [sb(f"w_weight{b}", [P, 2 * CAP], FP32) for b in range(3)]
        rowb = sb("w_row", [P, P], BF16)
        identb = sb("w_ident", [P, P], BF16)
        ps_hot = [ctx.enter_context(nc.psum_tensor(f"w_ps_hot{i}", [P, 512], FP32)) for i in range(2)]
        ps_max = [ctx.enter_context(nc.psum_tensor(f"w_ps_max{i}", [P, 512], FP32)) for i in range(RING)]
        ps_pair = ctx.enter_context(nc.psum_tensor("w_ps_pair", [P, 512], FP32))
        ps_sum = ctx.enter_context(nc.psum_tensor("w_ps_sum", [P, 512], FP32))
        loaded = [sem(f"wi_loaded{b}") for b in range(3)]
        own_dve, hots, scored_a, scored_p, hot_turns, hot_copied, max_turns, max_read = (
            sem("wi_dve"), sem("wi_hots"), sem("wi_scored_a"), sem("wi_scored_p"), sem("wi_hot_turns"),
            sem("wi_hot_copied"), sem("wi_max_turns"), sem("wi_max_read"))
        tabled, paired, pair_read, ready, weighed, multiplied, copied, consts, begun = (
            sem("wi_tabled"), sem("wi_paired"), sem("wi_pair_read"), sem("wi_ready"), sem("wi_weighed"),
            sem("wi_multiplied"), sem("wi_copied"), sem("wi_consts"), sem("wi_begun"))
        weighted = [sem(f"wi_weighted{n}") for n in range(2)]
        FREE = 6
        listed = [k["list"][n].rearrange("(w p q) f -> w p (q f)", p=P, q=CAP) for n in range(2)]
        block = ctx.enter_context(nc.Block())

        def by_window(eng):
            return eng.value_load(k["by_window"][0:1, 0:1], min_val=0, max_val=1) == 1

        def weighted_rows(eng, b, part):
            first, end = PARTS[part]
            eng.tensor_tensor(weights[:, first:end, :],
                              hot[b][:, :, :, :].rearrange("p n t m -> p (n t) m")[:, first:end, :],
                              weight[b][:, first:end].unsqueeze(2).broadcast_to([P, end - first, P]),
                              ALU.mult).then_inc(weighted[part], 1)

        @block.sync
        def _(eng):
            with eng.If(by_window(eng)):
                def body(w, b, visit):
                    eng.wait_ge(multiplied, 2 * w + 2)
                    for n in range(2):
                        eng.dma_start(rows[b][:, n, :, :].rearrange("p q f -> p (q f)"),
                                      listed[n][bass.ds(w, 1), :, :].squeeze(0)).then_inc(loaded[b], 16)
                by_three(eng, 0, W, body)
            with eng.Else():
                eng.drain()

        @block.vector
        def _(eng):
            with eng.If(by_window(eng)):
                ch = Chain(eng, own_dve)
                ch.add(eng.tensor_copy(rowb[:, :], c["row"][:, :]))
                eng.tensor_copy(identb[:, :], c["ident"][:, :]).then_inc(consts, 1)
                HOT, PAIR, MAX = 2, 2, 8
                PER = HOT + PAIR + MAX

                def one_hot(w, b, visit):
                    eng.wait_ge(loaded[b], 32 * (visit + 1))
                    ch.wait()
                    for n in range(2):
                        ch.add(eng.tensor_scalar(place[:, n, :], rows[b][:, n, :, DST1 + n],
                                                 k["first_node"][:, bass.ds(w, 1)], 1.0, ALU.subtract, ALU.subtract))
                    for n in range(2):
                        eng.tensor_scalar(lifted[b][:, n, :], rows[b][:, n, :, SCORE], k["lift"][:, 0:1], None,
                                          ALU.add)
                    ch.wait()
                    for n in range(2):
                        eng.tensor_tensor(hot[b][:, n, :, :], rowb[:, :].unsqueeze(1).broadcast_to([P, CAP, P]),
                                          place[:, n, :].unsqueeze(2).broadcast_to([P, CAP, P]),
                                          ALU.is_equal).then_inc(hots, 1)

                def maxima(w, b, visit):
                    for g, (n, t, end) in enumerate(GROUPS):
                        eng.wait_ge(max_turns, NG * w + g + 2)
                        eng.tensor_reduce(cand[:, g:g + 1], ps_max[g % RING][:, 0:(end - t) * P], X,
                                          ALU.max).then_inc(max_read, 1)
                    eng.wait_ge(max_read, RING + NG * (w + 1))
                    ch.add(eng.tensor_copy(pair[:, 0:1], v["score"][:, bass.ds(w, 1)]))
                    ch.link(eng.tensor_reduce(best[:, :], cand[:, :], X, ALU.max))
                    ch.link(eng.tensor_scalar(best[:, :], best[:, :], k["lift"][:, 0:1], pair[:, 0:1],
                                              ALU.subtract, ALU.add))
                    ch.link(eng.scalar_tensor_tensor(pair[:, 1:2], best[:, :], SLOPE, best[:, :], ALU.mult, ALU.max))
                    ch.link(eng.tensor_copy(pieces[:, 0, :], pair[:, :]))
                    ch.link(eng.tensor_tensor(rest[:, :], pair[:, :], pieces[:, 0, :], ALU.subtract))
                    ch.link(eng.tensor_copy(pieces[:, 1, :], rest[:, :]))
                    ch.link(eng.tensor_tensor(rest[:, :], rest[:, :], pieces[:, 1, :], ALU.subtract))
                    eng.tensor_copy(pieces[:, 2, :], rest[:, :]).then_inc(tabled, 1)

                def weigh(w, b, visit):
                    eng.wait_ge(paired, w + 1)
                    eng.tensor_reduce(edge_pair[:, :, :],
                                      ps_pair[:, 0:12 * CAP].rearrange("p (t k a) -> p t a k", k=3, a=2), X,
                                      ALU.add).then_inc(pair_read, 1)
                    eng.wait_ge(pair_read, w + 2)
                    both = edge_pair[:, :, :].rearrange("p (n t) a -> p n t a", n=2)
                    ch.link(eng.tensor_tensor(score[:, :, :], both[:, :, :, 0], rows[b][:, :, :, SCORE], ALU.add))
                    ch.link(eng.scalar_tensor_tensor(score[:, :, :], score[:, :, :], SLOPE, score[:, :, :],
                                                     ALU.mult, ALU.max))
                    eng.tensor_tensor(score[:, :, :], score[:, :, :], both[:, :, :, 1],
                                      ALU.subtract).then_inc(ready, 1)
                    eng.wait_ge(weighed, w + 1)
                    eng.wait_ge(multiplied, 2 * (w - 1) + 1 + FREE)
                    weighted_rows(eng, b, 0)

                eng.wait_ge(consts, 1)
                one_hot(0, 0, 0)
                maxima(0, 0, 0)
                counted = ch.n

                def body(w, b, visit):
                    ch.n = counted + w * PER
                    one_hot(*after(w, b, visit))
                    weigh(w, b, visit)
                    maxima(*after(w, b, visit))
                by_three(eng, 0, W - 1, body)
                ch.n = counted + (W - 1) * PER
                weigh(W - 1, (W - 1) % 3, (W - 1) // 3)
            with eng.Else():
                eng.drain()

        @block.scalar
        def _(eng):
            with eng.If(by_window(eng)):
                eng.sem_inc(hot_copied, 2)
                eng.sem_inc(copied, 1)

                def score_tiles(w, b, g):
                    n, t, end = GROUPS[g]
                    for i in range(t, end):
                        m = eng.activation(scores[:, n, i, :], hot[b][:, n, i, :], ACT.Copy,
                                           scale=lifted[b][:, n, i:i + 1])
                    m.then_inc(scored_a, 1)

                def spread_first(w, b, visit):
                    eng.wait_ge(hots, 2 * w + 1)
                    eng.wait_ge(max_turns, NG * w + 1)
                    for g in range(EARLY):
                        score_tiles(w, b, g)

                def spread_rest(w, b, visit):
                    for g, (n, t, end) in enumerate(GROUPS):
                        eng.wait_ge(hot_turns, NG * w + g + 1)
                        eng.copy(hot_turned[:, n, t:end, :].rearrange("p t n -> p (t n)"),
                                 ps_hot[g % 2][:, 0:(end - t) * P]).then_inc(hot_copied, 1)
                        if EARLY + g < NG // 2:
                            score_tiles(w, b, EARLY + g)

                def exponent(w, b):
                    eng.wait_ge(ready, w + 1)
                    eng.activation(weight[b][:, :], score[:, :, :].rearrange("p n t -> p (n t)"),
                                   ACT.Exp).then_inc(weighed, 1)

                def take_sums(w):
                    eng.wait_ge(multiplied, 2 * w + 2 + FREE)
                    eng.sem_inc(begun, 1)
                    eng.copy(sums[:, bass.ds(w, 1), :].squeeze(1), ps_sum[:, 0:P])
                    eng.copy(totals[:, bass.ds(w, 1)], ps_sum[:, P:P + 1]).then_inc(copied, 1)

                spread_first(0, 0, 0)
                spread_rest(0, 0, 0)
                spread_first(1, 1, 0)
                exponent(0, 0)
                spread_rest(1, 1, 0)

                def body(w, b, visit):
                    spread_first(*after(w, b, visit))
                    exponent(w, b)
                    spread_rest(*after(w, b, visit))
                    take_sums(w - 1)
                by_three(eng, 1, W - 1, body)
                exponent(W - 1, (W - 1) % 3)
                take_sums(W - 2)
                take_sums(W - 1)
            with eng.Else():
                eng.drain()

        @block.gpsimd
        def _(eng):
            with eng.If(by_window(eng)):
                def spread(w, b, visit):
                    eng.wait_ge(hots, 2 * w + 2)
                    eng.wait_ge(max_turns, NG * w + 1)
                    eng.sem_inc(begun, 1)
                    eng.tensor_tensor(scores[:, 1, :, :], hot[b][:, 1, :, :],
                                      lifted[b][:, 1, :].unsqueeze(2).broadcast_to([P, CAP, P]),
                                      ALU.mult).then_inc(scored_p, 1)

                def weigh(w, b, visit):
                    eng.wait_ge(weighed, w + 1)
                    eng.wait_ge(multiplied, 2 * w + FREE)
                    eng.sem_inc(begun, 1)
                    weighted_rows(eng, b, 1)

                spread(0, 0, 0)

                def body(w, b, visit):
                    spread(*after(w, b, visit))
                    weigh(w, b, visit)
                by_three(eng, 0, W - 1, body)
                weigh(W - 1, (W - 1) % 3, (W - 1) // 3)
            with eng.Else():
                eng.drain()

        @block.tensor
        def _(eng):
            with eng.If(by_window(eng)):
                eng.wait_ge(consts, 1)
                eng.sem_inc(max_read, RING)
                eng.sem_inc(pair_read, 1)
                eng.sem_inc(multiplied, FREE)
                eng.sem_inc(max_turns, 1)

                def turn(w, b, visit):
                    for g, (n, t, end) in enumerate(GROUPS):
                        if t == 0:
                            eng.wait_ge(hots, 2 * w + n + 1)
                        eng.wait_ge(hot_copied, NG * w + g + 1)
                        for i in range(t, end):
                            m = eng.matmul(ps_hot[g % 2][:, (i - t) * P:(i - t + 1) * P], hot[b][:, n, i, :],
                                           identb[:, :], start=True, stop=True)
                        m.then_inc(hot_turns, 1)
                        if n == 0:
                            eng.wait_ge(scored_a, NG // 2 * w + g + 1)
                        elif t == 0:
                            eng.wait_ge(scored_p, w + 1)
                        eng.wait_ge(max_read, NG * w + g + 1)
                        for i in range(t, end):
                            m = eng.transpose(ps_max[g % RING][:, (i - t) * P:(i - t + 1) * P], scores[:, n, i, :],
                                              c["ident"][:, :])
                        m.then_inc(max_turns, 1)

                def look_up(w, b, visit):
                    eng.wait_ge(tabled, w + 1)
                    eng.wait_ge(hot_copied, NG * (w + 1) + 2)
                    eng.wait_ge(pair_read, w + 1)
                    for n in range(2):
                        for i in range(CAP):
                            at = 6 * (n * CAP + i)
                            m = eng.matmul(ps_pair[:, at:at + 6], hot_turned[:, n, i, :],
                                           pieces[:, :, :].rearrange("p k a -> p (k a)"), start=True, stop=True)
                    m.then_inc(paired, 1)

                def sum_up(w, b, part):
                    if part == 0:
                        eng.wait_ge(copied, w + 1)
                    eng.wait_ge(weighted[part], w + 1)
                    for i in range(*PARTS[part]):
                        m = eng.matmul(ps_sum[:, 0:P + 1], weights[:, i, :], rows[b][:, i // CAP, i % CAP, 0:P + 1],
                                       start=i == 0, stop=i == 2 * CAP - 1)
                    m.then_inc(multiplied, 1)

                turn(0, 0, 0)
                look_up(0, 0, 0)

                def body(w, b, visit):
                    turn(*after(w, b, visit))
                    sum_up(w, b, 0)
                    look_up(*after(w, b, visit))
                    sum_up(w, b, 1)
                by_three(eng, 0, W - 1, body)
                for n in range(2):
                    sum_up(W - 1, (W - 1) % 3, n)
            with eng.Else():
                eng.drain()


def output_phase(nc, s, c, k, v, out):
    ctx = ExitStack()
    with ctx:
        def sb(name, shape, dt):
            return ctx.enter_context(nc.sbuf_tensor(name, shape, dt))

        def sem(name):
            return ctx.enter_context(nc.semaphore(name))

        W = s.W
        x1, t = v["z"], v["z01"]
        mean, var = sb("o_mean", [P, W], FP32), sb("o_var", [P, W], FP32)
        none, some, inv = sb("o_none", [P, W], FP32), sb("o_some", [P, W], FP32), sb("o_inv", [P, W], FP32)
        own_dve, ready, gelu, varied, rooted, normed, stored = (
            sem("ou_dve"), sem("ou_ready"), sem("ou_gelu"), sem("ou_varied"), sem("ou_rooted"), sem("ou_normed"),
            sem("ou_stored"))
        wide = lambda a: a[:, :].unsqueeze(2).broadcast_to([P, W, P])
        block = ctx.enter_context(nc.Block())

        @block.vector
        def _(eng):
            ch = Chain(eng, own_dve)
            total = v["total"][:, :]
            ch.link(eng.tensor_scalar(some[:, :], total, 0.0, None, ALU.is_gt))
            ch.link(eng.tensor_scalar(none[:, :], some[:, :], -1.0, 1.0, ALU.mult, ALU.add))
            ch.link(eng.tensor_tensor(inv[:, :], total, none[:, :], ALU.add))
            ch.link(eng.reciprocal(inv[:, :], inv[:, :]))
            eng.tensor_tensor(t[:, :, :], t[:, :, :], wide(inv), ALU.mult).then_inc(ready, 1)
            eng.wait_ge(gelu, 1)
            ch.link(eng.tensor_scalar(none[:, :], none[:, :], 1.0, None, ALU.add))
            ch.link(eng.tensor_tensor(x1[:, :, :], x1[:, :, :], wide(none), ALU.mult))
            ch.link(eng.tensor_tensor(t[:, :, :], t[:, :, :], x1[:, :, :], ALU.add))
            layer_norm(eng, ch, s, t, x1, mean, var, rooted, varied)
            eng.drain().then_inc(normed, 1)

        @block.scalar
        def _(eng):
            eng.wait_ge(ready, 1)
            eng.activation(t[:, :, :], t[:, :, :], ACT.Gelu).then_inc(gelu, 1)
            eng.wait_ge(varied, 1)
            eng.activation(var[:, :], var[:, :], ACT.Sqrt).then_inc(rooted, 1)

        @block.sync
        def _(eng):
            eng.wait_ge(normed, 1)
            full, rest = s.nodes // P, s.nodes % P
            eng.dma_start(out[0:full * P, :].rearrange("(w p) f -> p w f", p=P), t[:, 0:full, :]).then_inc(stored, 16)
            if rest:
                eng.dma_start(out[full * P:s.nodes, :], t[0:rest, full, :]).then_inc(stored, 16)
            eng.wait_ge(stored, 32 if rest else 16)


def gnn_kernel(nc, x, src, dst, edge_rows, att_w, att_b, out):
    s = Shapes(x.shape[0], src.shape[0])
    ctx = ExitStack()
    with ctx:
        def sb(name, shape, dt):
            return ctx.enter_context(nc.sbuf_tensor(name, shape, dt))

        c, k = constants(nc, sb, s), kept(nc, sb, s)
        v = {"z": sb("v_z", [P, s.W, P], FP32), "z01": sb("v_z01", [P, s.W, P], FP32),
             "score": sb("v_score", [P, s.W], FP32), "total": sb("v_total", [P, s.W], FP32)}
        with ExitStack() as steps:
            def sb_steps(name, shape, dt):
                return steps.enter_context(nc.sbuf_tensor(name, shape, dt))

            of_edges(nc, sb_steps, s, k)
            with nc.sbuf_tensor("zeros", [P, s.CAP * ROW], FP32) as k["zeros"]:
                slots_phase(nc, s, c, k, src, dst, att_w, att_b)
                adjacency_phase(nc, s, c, k)
            v["pieces"] = [sb_steps(f"v_pieces{n}", [P, s.W, 2 * P], FP16) for n in range(2)]
            prepare_phase(nc, s, c, k, v, x)
            appnp_phase(nc, s, c, k, v, edge_rows)
        nodes_phase(nc, s, c, k, v, x)
        maxima_phase(nc, s, c, k)
        attention_phase(nc, s, c, k, v)
        windows_phase(nc, s, c, k, v)
        output_phase(nc, s, c, k, v, out)


_INS = ["x", "src", "dst", "edge_attr_128", "L1_gnn_W_att_w", "L1_gnn_W_att_b"]


def kernel(**inputs):
    import numpy as _np
    import concourse.bacc as _bacc
    from concourse import mybir as _mybir
    from concourse.bass_utils import run_bass_kernel_spmd as _run

    nc = _bacc.Bacc("TRN2", target_bir_lowering=False, num_devices=1)
    arrays, args = {}, []
    for name in _INS:
        a = _np.ascontiguousarray(inputs[name])
        arrays[f"in_{name}_dram"] = a
        args.append(nc.dram_tensor(f"in_{name}_dram", a.shape, _mybir.dt.from_np(a.dtype), kind="ExternalInput").ap())
    shape = inputs["x"].shape
    args.append(nc.dram_tensor("out_dram", shape, _mybir.dt.float32, kind="ExternalOutput").ap())
    gnn_kernel(nc, *args)
    r = _run(nc, [arrays], core_ids=[0])
    return r.results[0]["out_dram"]
```
